# Optimizing a Trainium2 kernel written in Bass

```python
import numpy as np
import jax
import jax.numpy as jnp

def _softmax(x, axis=-1):
    return jax.nn.softmax(x, axis=axis)

def _gelu(x):
    return jax.nn.gelu(x, approximate=True)

def _silu(x):
    return jax.nn.silu(x)

def _sigmoid(x):
    return jax.nn.sigmoid(x)

def _layernorm(x, axis=-1, eps=1e-05):
    m = jnp.mean(x, axis=axis, keepdims=True)
    v = jnp.var(x, axis=axis, keepdims=True)
    return (x - m) / jnp.sqrt(v + eps)

def _scatter_add(tgt, idx, src, axis=0):
    return tgt.at[idx].add(src)

def _segment_sum(src, seg, n):
    return jax.ops.segment_sum(src, seg, n)
kernel_name = 'mk_decoder_postln_d4_seqx_r8_4b12df'

def setup_inputs(seed: int=0):
    np.random.seed(seed)
    _w = jnp.asarray

    def _rec_inputs():
        import jax
        import jax.numpy as jnp
        _rk = jax.random.key(seed)
        x = 7.22e-05 + 1 * jax.random.normal(jax.random.fold_in(_rk, 1), (32, 128, 128), jnp.float32)
        _lenS = 128 - jax.random.randint(jax.random.fold_in(_rk, 7), (32,), 0, max(1, 128 // 4) + 1, jnp.int32)
        _lenS2 = 128 - jax.random.randint(jax.random.fold_in(_rk, 8), (32,), 0, max(1, 128 // 4) + 1, jnp.int32)
        _ctx_768P = jax.random.normal(jax.random.fold_in(_rk, 11), (32, 16, 96), jnp.float32)
        _ctx_768c = jax.random.dirichlet(jax.random.fold_in(_rk, 511), 0.3 * jnp.ones((16,), jnp.float32), (32, 128))
        _ctx_768t = jnp.einsum('bsk,bkd->bsd', _ctx_768c, _ctx_768P)
        _ctx_768t = _ctx_768t * jax.lax.rsqrt(jnp.mean(jnp.square(_ctx_768t)) + 1e-12) * 0.953939
        ctx_768 = 3.88148e-05 + 0.999967 * (_ctx_768t + 0.3 * jax.random.normal(jax.random.fold_in(_rk, 611), (32, 128, 96), jnp.float32))
        _validS = jnp.arange(128)[None, :] < _lenS[:, None]
        _validS2 = jnp.arange(128)[None, :] < _lenS2[:, None]
        _causal = jnp.tril(jnp.ones((128, 128), dtype=bool))
        mask_BxS_bf1 = jnp.ones((32, 128), dtype=bool)
        mask_BxS2_bf1 = jnp.ones((32, 128), dtype=bool)
        return (x, ctx_768, mask_BxS_bf1, mask_BxS2_bf1)
    x, ctx_768, mask_BxS_bf1, mask_BxS2_bf1 = _rec_inputs()

    def _L0_attn_setup():
        import jax, jax.numpy as jnp
        import numpy as np
        EMB = 128
        HEADS = 16
        HEAD_DIM = EMB // HEADS
        MAX_LEN = 125
        key = jax.random.key(seed)
        ks = jax.random.split(key, 11)
        s = 0.02
        x = jax.random.normal(ks[0], (4, 128, EMB), dtype=jnp.float32)
        Wq = jax.random.normal(ks[1], (EMB, EMB), dtype=jnp.float32) * s
        bq = jnp.zeros((EMB,), dtype=jnp.float32)
        Wk = jax.random.normal(ks[2], (EMB, EMB), dtype=jnp.float32) * s
        bk = jnp.zeros((EMB,), dtype=jnp.float32)
        Wv = jax.random.normal(ks[3], (EMB, EMB), dtype=jnp.float32) * s
        bv = jnp.zeros((EMB,), dtype=jnp.float32)
        Wp = jax.random.normal(ks[4], (EMB, EMB), dtype=jnp.float32) * s
        bp = jnp.zeros((EMB,), dtype=jnp.float32)
        bias_table = jax.random.normal(ks[5], (2 * MAX_LEN - 1, HEADS), dtype=jnp.float32) * 0.02
        temperature = jnp.ones((1,), dtype=jnp.float32)
        return {'x': x, 'Wq': Wq, 'bq': bq, 'Wk': Wk, 'bk': bk, 'Wv': Wv, 'bv': bv, 'Wp': Wp, 'bp': bp, 'bias_table': bias_table, 'temperature': temperature}
    _L0_attn_all = _L0_attn_setup()
    _L0_attn_in = {k: v for k, v in _L0_attn_all.items() if k in ('Wq', 'bq', 'Wk', 'bk', 'Wv', 'bv', 'Wp', 'bp', 'bias_table', 'temperature')}
    del _L0_attn_all

    def _L0_xattn_setup():
        import jax, jax.numpy as jnp
        import numpy as np
        B, T, DT, G, DV = (16, 64, 128, 72, 96)
        H, DH = (4, 32)
        INNER = H * DH
        HID = 4 * DT
        N_STATE = 64
        K_TOP = 32

        def layernorm(x, g, b, eps=1e-05):
            m = x.mean(-1, keepdims=True)
            v = x.var(-1, keepdims=True)
            return (x - m) * jax.lax.rsqrt(v + eps) * g + b

        def s4d(x, log_dt, A_re, A_im, C_re, C_im, D_skip):
            Bb, L, D = x.shape
            dt = jnp.exp(log_dt)
            A = A_re + 1j * A_im
            C = C_re + 1j * C_im
            dtA = dt[:, None] * A
            dC = C * (jnp.exp(dtA) - 1.0) / A
            powers = jnp.exp(dtA[:, :, None] * jnp.arange(L))
            K = 2.0 * jnp.einsum('dn,dnl->dl', dC, powers).real
            n = 2 * L
            Kf = jnp.fft.rfft(K, n=n, axis=-1)
            xf = jnp.fft.rfft(x, n=n, axis=1)
            y = jnp.fft.irfft(xf * Kf.T[None], n=n, axis=1)[:, :L]
            return y + x * D_skip
        key = jax.random.key(seed)
        ks = jax.random.split(key, 16)
        s = 0.02
        inp = {'x_text': jax.random.normal(ks[0], (B, T, DT), jnp.float32), 'x_vision': jax.random.normal(ks[1], (B, G, DV), jnp.float32), 'text_mask': jnp.ones((B, T), bool), 'vision_mask': jnp.ones((B, G), bool), 'Wq': jax.random.normal(ks[2], (DT, INNER), jnp.float32) * s, 'Wk': jax.random.normal(ks[3], (DV, INNER), jnp.float32) * s, 'Wv': jax.random.normal(ks[4], (DV, DT), jnp.float32) * s, 'W_film_in': jax.random.normal(ks[5], (DT, 2 * DT), jnp.float32) * s, 'b_film_in': jnp.zeros((2 * DT,), jnp.float32), 'W_film_out': jax.random.normal(ks[6], (DT, 2 * DT), jnp.float32) * s, 'b_film_out': jnp.zeros((2 * DT,), jnp.float32), 'g_norm_in': jnp.ones((DT,), jnp.float32), 'b_norm_in': jnp.zeros((DT,), jnp.float32), 'g_norm_out': jnp.ones((DT,), jnp.float32), 'b_norm_out': jnp.zeros((DT,), jnp.float32), 'g_ffn': jnp.ones((DT,), jnp.float32), 'b_ffn': jnp.zeros((DT,), jnp.float32), 'W1': jax.random.normal(ks[7], (DT, HID), jnp.float32) * s, 'b1': jnp.zeros((HID,), jnp.float32), 'W2': jax.random.normal(ks[8], (HID, DT), jnp.float32) * s, 'b2': jnp.zeros((DT,), jnp.float32), 'log_dt': jnp.log(0.001) + jax.random.uniform(ks[9], (DT,), jnp.float32) * (jnp.log(0.1) - jnp.log(0.001)), 'A_re': -0.5 * jnp.ones((DT, N_STATE), jnp.float32), 'A_im': jnp.tile(jnp.pi * jnp.arange(N_STATE, dtype=jnp.float32), (DT, 1)), 'C_re': jax.random.normal(ks[10], (DT, N_STATE), jnp.float32) * 0.5 ** 0.5, 'C_im': jax.random.normal(ks[11], (DT, N_STATE), jnp.float32) * 0.5 ** 0.5, 'D_skip': jax.random.normal(ks[12], (DT,), jnp.float32), 'mod_gate': jnp.array(0.5, jnp.float32)}
        return inp
    _L0_xattn_all = _L0_xattn_setup()
    _L0_xattn_in = {k: v for k, v in _L0_xattn_all.items() if k in ('Wq', 'Wk', 'Wv', 'W_film_in', 'b_film_in', 'W_film_out', 'b_film_out', 'g_norm_in', 'b_norm_in', 'g_norm_out', 'b_norm_out', 'g_ffn', 'b_ffn', 'W1', 'b1', 'W2', 'b2', 'log_dt', 'A_re', 'A_im', 'C_re', 'C_im', 'D_skip', 'mod_gate')}
    del _L0_xattn_all

    def _L0_ffn_setup():
        import jax, jax.numpy as jnp
        import numpy as np
        D_MODEL = 128
        NUM_SLOTS = 64
        TOP_K = 8
        B, T = (4, 512)

        def _forward(x, slot_init, slot_scale, w1, b1, w2, b2, gru_wih, gru_whh, gru_bih, gru_bhh, wv, bv, wo, bo, tau):
            Bn, Tn, D = x.shape
            Sn = slot_init.shape[0]
            S = jnp.broadcast_to((slot_init * slot_scale)[None], (Bn, Sn, D)).astype(x.dtype)
            slot_mean = S.mean(axis=1, keepdims=True)
            ctx = jnp.concatenate([x, jnp.broadcast_to(slot_mean, x.shape)], axis=-1)
            h = jax.nn.gelu(ctx @ w1.T + b1, approximate=False)
            route_logits = (h @ w2.T + b2) / (jnp.abs(tau) + 0.1)
            topk_vals, topk_idx = jax.lax.top_k(route_logits, TOP_K)
            topk_w = jax.nn.softmax(topk_vals, axis=-1)
            alpha = jnp.sum(topk_w[..., None] * jax.nn.one_hot(topk_idx, Sn, dtype=x.dtype), axis=-2)
            slot_input = jnp.einsum('bts,btd->bsd', alpha, x)
            slot_wsum = alpha.sum(axis=1) + 1e-08
            gi = (slot_input / slot_wsum[..., None]).reshape(Bn * Sn, D)
            hs = S.reshape(Bn * Sn, D)
            gx = gi @ gru_wih.T + gru_bih
            gh = hs @ gru_whh.T + gru_bhh
            xr, xz, xn = jnp.split(gx, 3, axis=-1)
            hr, hz, hn = jnp.split(gh, 3, axis=-1)
            r = jax.nn.sigmoid(xr + hr)
            z = jax.nn.sigmoid(xz + hz)
            n = jnp.tanh(xn + r * hn)
            h_new = (1.0 - z) * n + z * hs
            S_new = h_new.reshape(Bn, Sn, D)
            slot_values = S_new @ wv.T + bv
            out = jnp.einsum('bts,bsd->btd', alpha, slot_values)
            return out @ wo.T + bo
        key = jax.random.key(seed)
        ks = jax.random.split(key, 16)
        D, S = (D_MODEL, NUM_SLOTS)
        H = D // 2
        sc = lambda fan_in: 1.0 / np.sqrt(fan_in)
        inp = {'x': jax.random.normal(ks[0], (B, T, D), dtype=jnp.float32), 'slot_init': jax.random.normal(ks[1], (S, D), dtype=jnp.float32) * 0.1, 'slot_scale': jnp.ones((S, 1), dtype=jnp.float32), 'w1': jax.random.normal(ks[2], (H, 2 * D), dtype=jnp.float32) * sc(2 * D), 'b1': jnp.zeros((H,), dtype=jnp.float32), 'w2': jax.random.normal(ks[3], (S, H), dtype=jnp.float32) * sc(H), 'b2': jnp.zeros((S,), dtype=jnp.float32), 'gru_wih': jax.random.normal(ks[4], (3 * D, D), dtype=jnp.float32) * sc(D), 'gru_whh': jax.random.normal(ks[5], (3 * D, D), dtype=jnp.float32) * sc(D), 'gru_bih': jnp.zeros((3 * D,), dtype=jnp.float32), 'gru_bhh': jnp.zeros((3 * D,), dtype=jnp.float32), 'wv': jax.random.normal(ks[6], (D, D), dtype=jnp.float32) * sc(D), 'bv': jnp.zeros((D,), dtype=jnp.float32), 'wo': jax.random.normal(ks[7], (D, D), dtype=jnp.float32) * sc(D), 'bo': jnp.zeros((D,), dtype=jnp.float32), 'tau': jnp.ones((1,), dtype=jnp.float32)}
        return inp
    _L0_ffn_all = _L0_ffn_setup()
    _L0_ffn_in = {k: v for k, v in _L0_ffn_all.items() if k in ('slot_init', 'slot_scale', 'w1', 'b1', 'w2', 'b2', 'gru_wih', 'gru_whh', 'gru_bih', 'gru_bhh', 'wv', 'bv', 'wo', 'bo', 'tau')}
    del _L0_ffn_all

    def _L1_attn_setup():
        import jax, jax.numpy as jnp
        import numpy as np
        H = 8
        EPS = 1e-06

        def _pos_encoding(S, D):
            pos = jnp.arange(S, dtype=jnp.float32)[:, None]
            div = jnp.exp(jnp.arange(0, D, 2, dtype=jnp.float32) * (-np.log(10000.0) / D))
            pe = jnp.zeros((S, D), dtype=jnp.float32)
            pe = pe.at[:, 0::2].set(jnp.sin(pos * div))
            pe = pe.at[:, 1::2].set(jnp.cos(pos * div))
            return pe
        key = jax.random.key(seed)
        ks = jax.random.split(key, 5)
        S, B, D = (256, 16, 128)
        s = 1.0 / np.sqrt(D)
        return {'x': jax.random.normal(ks[0], (S, B, D), dtype=jnp.float32), 'Wq': jax.random.normal(ks[1], (D, D), dtype=jnp.float32) * s, 'bq': jnp.zeros((D,), dtype=jnp.float32), 'Wk': jax.random.normal(ks[2], (D, D), dtype=jnp.float32) * s, 'bk': jnp.zeros((D,), dtype=jnp.float32), 'Wv': jax.random.normal(ks[3], (D, D), dtype=jnp.float32) * s, 'bv': jnp.zeros((D,), dtype=jnp.float32), 'Wo': jax.random.normal(ks[4], (D, D), dtype=jnp.float32) * s, 'bo': jnp.zeros((D,), dtype=jnp.float32)}
    _L1_attn_all = _L1_attn_setup()
    _L1_attn_in = {k: v for k, v in _L1_attn_all.items() if k in ('Wq', 'bq', 'Wk', 'bk', 'Wv', 'bv', 'Wo', 'bo')}
    del _L1_attn_all

    def _L1_xattn_setup():
        import jax, jax.numpy as jnp
        import numpy as np
        HEADS = 8
        DIM_HEAD = 64
        SCALE = DIM_HEAD ** (-0.5)
        key = jax.random.key(seed)
        ks = jax.random.split(key, 7)
        b, n, m = (4, 256, 128)
        qd, cd, inner = (128, 96, HEADS * DIM_HEAD)
        s = lambda fan_in: 1.0 / np.sqrt(fan_in)
        return {'x': jax.random.normal(ks[0], (b, n, qd), jnp.float32), 'context': jax.random.normal(ks[1], (b, m, cd), jnp.float32), 'Wq': jax.random.normal(ks[2], (qd, inner), jnp.float32) * s(qd), 'Wk': jax.random.normal(ks[3], (cd, inner), jnp.float32) * s(cd), 'Wv': jax.random.normal(ks[4], (cd, inner), jnp.float32) * s(cd), 'Wout': jax.random.normal(ks[5], (inner, qd), jnp.float32) * s(inner), 'bout': jax.random.normal(ks[6], (qd,), jnp.float32) * 0.01}
    _L1_xattn_all = _L1_xattn_setup()
    _L1_xattn_in = {k: v for k, v in _L1_xattn_all.items() if k in ('Wq', 'Wk', 'Wv', 'Wout', 'bout')}
    del _L1_xattn_all

    def _L1_ffn_setup():
        import jax, jax.numpy as jnp
        import numpy as np
        B, S, D = (2, 256, 128)
        H, HKV = (16, 4)
        HD = D // H
        F, E, K = (256, 8, 2)
        THETA = 10000.0
        EPS = 1e-05

        def _rmsnorm(x, w):
            return x * jax.lax.rsqrt(jnp.mean(x * x, axis=-1, keepdims=True) + EPS) * w

        def _rope_cos_sin(seq_len, head_dim, theta):
            inv_freq = 1.0 / theta ** (jnp.arange(0, head_dim, 2, dtype=jnp.float32) / head_dim)
            freqs = jnp.arange(seq_len, dtype=jnp.float32)[:, None] * inv_freq
            return (jnp.cos(freqs), jnp.sin(freqs))

        def _apply_rope(x, cos, sin):
            x1, x2 = jnp.split(x, 2, axis=-1)
            c = cos[None, :, None, :]
            s = sin[None, :, None, :]
            return jnp.concatenate([x1 * c - x2 * s, x2 * c + x1 * s], axis=-1)
        key = jax.random.key(seed)
        ks = jax.random.split(key, 12)
        s = 0.02
        return {'hidden_states': jax.random.normal(ks[0], (B, S, D), jnp.float32), 'ln1_w': 1.0 + 0.1 * jax.random.normal(ks[1], (D,), jnp.float32), 'ln2_w': 1.0 + 0.1 * jax.random.normal(ks[2], (D,), jnp.float32), 'Wq': s * jax.random.normal(ks[3], (D, H * HD), jnp.float32), 'Wk': s * jax.random.normal(ks[4], (D, HKV * HD), jnp.float32), 'Wv': s * jax.random.normal(ks[5], (D, HKV * HD), jnp.float32), 'Wo': s * jax.random.normal(ks[6], (H * HD, D), jnp.float32), 'Wr': s * jax.random.normal(ks[7], (D, E), jnp.float32), 'Wg': s * jax.random.normal(ks[8], (E, D, F), jnp.float32), 'Wu': s * jax.random.normal(ks[9], (E, D, F), jnp.float32), 'Wd': s * jax.random.normal(ks[10], (E, F, D), jnp.float32)}
    _L1_ffn_all = _L1_ffn_setup()
    _L1_ffn_in = {k: v for k, v in _L1_ffn_all.items() if k in ('ln1_w', 'ln2_w', 'Wq', 'Wk', 'Wv', 'Wo', 'Wr', 'Wg', 'Wu', 'Wd')}
    del _L1_ffn_all

    def _L2_attn_setup():
        import jax, jax.numpy as jnp
        import numpy as np
        B, L, D = (2, 256, 128)
        H = 16
        DH = D // H
        key = jax.random.key(seed)
        ks = jax.random.split(key, 9)
        s = 1.0 / np.sqrt(D)
        return {'x': jax.random.normal(ks[0], (B, L, D), dtype=jnp.float32), 'Wq': jax.random.normal(ks[1], (D, D), dtype=jnp.float32) * s, 'bq': jnp.zeros((D,), dtype=jnp.float32), 'Wk': jax.random.normal(ks[2], (D, D), dtype=jnp.float32) * s, 'bk': jnp.zeros((D,), dtype=jnp.float32), 'Wv': jax.random.normal(ks[3], (D, D), dtype=jnp.float32) * s, 'bv': jnp.zeros((D,), dtype=jnp.float32), 'Wo': jax.random.normal(ks[4], (D, D), dtype=jnp.float32) * s, 'bo': jnp.zeros((D,), dtype=jnp.float32)}
    _L2_attn_all = _L2_attn_setup()
    _L2_attn_in = {k: v for k, v in _L2_attn_all.items() if k in ('Wq', 'bq', 'Wk', 'bk', 'Wv', 'bv', 'Wo', 'bo')}
    del _L2_attn_all

    def _L2_xattn_setup():
        import jax, jax.numpy as jnp
        import numpy as np
        IMAGE_DIM = 128
        TEXT_DIM = 96
        NUM_HEADS = 16
        HEAD_DIM = IMAGE_DIM // NUM_HEADS
        key = jax.random.key(seed)
        ks = jax.random.split(key, 14)
        B, N, M = (4, 512, 64)
        s_img = 1.0 / np.sqrt(IMAGE_DIM)
        s_txt = 1.0 / np.sqrt(TEXT_DIM)
        s_ff = 1.0 / np.sqrt(2 * IMAGE_DIM)
        return {'x': jax.random.normal(ks[0], (B, N, IMAGE_DIM), jnp.float32), 'y': jax.random.normal(ks[1], (B, M, TEXT_DIM), jnp.float32), 'Wq': jax.random.normal(ks[2], (IMAGE_DIM, IMAGE_DIM), jnp.float32) * s_img, 'bq': jax.random.normal(ks[3], (IMAGE_DIM,), jnp.float32) * s_img, 'Wk': jax.random.normal(ks[4], (TEXT_DIM, IMAGE_DIM), jnp.float32) * s_txt, 'bk': jax.random.normal(ks[5], (IMAGE_DIM,), jnp.float32) * s_txt, 'Wv': jax.random.normal(ks[6], (TEXT_DIM, IMAGE_DIM), jnp.float32) * s_txt, 'bv': jax.random.normal(ks[7], (IMAGE_DIM,), jnp.float32) * s_txt, 'W1': jax.random.normal(ks[8], (IMAGE_DIM, 2 * IMAGE_DIM), jnp.float32) * s_img, 'b1': jax.random.normal(ks[9], (2 * IMAGE_DIM,), jnp.float32) * s_img, 'W2': jax.random.normal(ks[10], (2 * IMAGE_DIM, IMAGE_DIM), jnp.float32) * s_ff, 'b2': jax.random.normal(ks[11], (IMAGE_DIM,), jnp.float32) * s_ff}
    _L2_xattn_all = _L2_xattn_setup()
    _L2_xattn_in = {k: v for k, v in _L2_xattn_all.items() if k in ('Wq', 'bq', 'Wk', 'bk', 'Wv', 'bv', 'W1', 'b1', 'W2', 'b2')}
    del _L2_xattn_all

    def _L2_ffn_setup():
        import jax, jax.numpy as jnp
        import numpy as np
        D_MODEL = 128
        NUM_EXPERTS = 8
        TOP_K = 2
        key = jax.random.key(seed)
        ks = jax.random.split(key, 5)
        scale = 1.0 / np.sqrt(D_MODEL)
        x = jax.random.normal(ks[0], (4, 256, D_MODEL), dtype=jnp.float32)
        We = jax.random.uniform(ks[1], (NUM_EXPERTS, D_MODEL, D_MODEL), jnp.float32, -scale, scale)
        be = jax.random.uniform(ks[2], (NUM_EXPERTS, D_MODEL), jnp.float32, -scale, scale)
        Wg = jax.random.uniform(ks[3], (NUM_EXPERTS, D_MODEL), jnp.float32, -scale, scale)
        bg = jax.random.uniform(ks[4], (NUM_EXPERTS,), jnp.float32, -scale, scale)
        return {'x': x, 'We': We, 'be': be, 'Wg': Wg, 'bg': bg}
    _L2_ffn_all = _L2_ffn_setup()
    _L2_ffn_in = {k: v for k, v in _L2_ffn_all.items() if k in ('We', 'be', 'Wg', 'bg')}
    del _L2_ffn_all

    def _L3_attn_setup():
        import jax, jax.numpy as jnp
        import numpy as np
        NUM_HEADS = 16
        HEAD_DIM = 64
        NEG_INF = -1000000000.0

        def rotary_embedding(x, seq_len, head_dim):
            positions = jnp.arange(seq_len)
            dim_pairs = jnp.arange(0, head_dim, 2)
            freqs = 1.0 / 10000.0 ** (dim_pairs / head_dim)
            angles = positions[:, None] * freqs[None, :]
            cos = jnp.cos(angles)[:, None, :]
            sin = jnp.sin(angles)[:, None, :]
            x1 = x[..., ::2]
            x2 = x[..., 1::2]
            out1 = x1 * cos - x2 * sin
            out2 = x1 * sin + x2 * cos
            return jnp.stack([out1, out2], axis=-1).reshape(x.shape)
        key = jax.random.key(seed)
        k1, k2, k3 = jax.random.split(key, 3)
        batch, seq_len, embed_dim = (2, 256, 128)
        x = jax.random.normal(k1, (batch, seq_len, embed_dim), dtype=jnp.float32)
        W_qkv = jax.random.normal(k2, (embed_dim, 3 * NUM_HEADS * HEAD_DIM), dtype=jnp.float32) * 0.02
        W_out = jax.random.normal(k3, (NUM_HEADS * HEAD_DIM, embed_dim), dtype=jnp.float32) * 0.02
        return {'x': x, 'W_qkv': W_qkv, 'W_out': W_out}
    _L3_attn_all = _L3_attn_setup()
    _L3_attn_in = {k: v for k, v in _L3_attn_all.items() if k in ('W_qkv', 'W_out')}
    del _L3_attn_all

    def _L3_xattn_setup():
        import math
        import jax, jax.numpy as jnp
        import numpy as np
        B, SQ, SKV = (4, 256, 256)
        D_EMBED, D_CROSS, D_ATT, N_HEADS = (128, 96, 128, 16)
        D_HEAD = D_ATT // N_HEADS

        def _split_heads(t):
            b, s, _ = t.shape
            return t.reshape(b, s, N_HEADS, D_HEAD).transpose(0, 2, 1, 3)
        key = jax.random.key(seed)
        ks = jax.random.split(key, 10)
        s_e = 1.0 / math.sqrt(D_EMBED)
        s_c = 1.0 / math.sqrt(D_CROSS)
        s_a = 1.0 / math.sqrt(D_ATT)
        return {'x': jax.random.normal(ks[0], (B, SQ, D_EMBED), jnp.float32), 'y': jax.random.normal(ks[1], (B, SKV, D_CROSS), jnp.float32), 'Wq': jax.random.normal(ks[2], (D_EMBED, D_ATT), jnp.float32) * s_e, 'bq': jax.random.normal(ks[3], (D_ATT,), jnp.float32) * 0.01, 'Wk': jax.random.normal(ks[4], (D_CROSS, D_ATT), jnp.float32) * s_c, 'bk': jax.random.normal(ks[5], (D_ATT,), jnp.float32) * 0.01, 'Wv': jax.random.normal(ks[6], (D_CROSS, D_ATT), jnp.float32) * s_c, 'bv': jax.random.normal(ks[7], (D_ATT,), jnp.float32) * 0.01, 'Wo': jax.random.normal(ks[8], (D_ATT, D_EMBED), jnp.float32) * s_a, 'bo': jax.random.normal(ks[9], (D_EMBED,), jnp.float32) * 0.01}
    _L3_xattn_all = _L3_xattn_setup()
    _L3_xattn_in = {k: v for k, v in _L3_xattn_all.items() if k in ('Wq', 'bq', 'Wk', 'bk', 'Wv', 'bv', 'Wo', 'bo')}
    del _L3_xattn_all

    def _L3_ffn_setup():
        import jax, jax.numpy as jnp
        import numpy as np
        NEG_INF = -1e+30
        K = 2
        key = jax.random.key(seed)
        ks = jax.random.split(key, 5)
        B, S, D, O, E = (8, 256, 128, 128, 8)
        scale = 1.0 / np.sqrt(D)
        return {'x': jax.random.normal(ks[0], (B, S, D), dtype=jnp.float32), 'gate_w': jax.random.normal(ks[1], (E, D), dtype=jnp.float32) * scale, 'gate_b': jnp.zeros((E,), dtype=jnp.float32), 'expert_w': jax.random.normal(ks[2], (E, O, D), dtype=jnp.float32) * scale, 'expert_b': jnp.zeros((E, O), dtype=jnp.float32)}
    _L3_ffn_all = _L3_ffn_setup()
    _L3_ffn_in = {k: v for k, v in _L3_ffn_all.items() if k in ('gate_w', 'gate_b', 'expert_w', 'expert_b')}
    del _L3_ffn_all
    return {'x': x, 'ctx_768': ctx_768, 'mask_BxS_bf1': mask_BxS_bf1, 'mask_BxS2_bf1': mask_BxS2_bf1, 'L0_attn_Wq': _L0_attn_in['Wq'], 'L0_attn_bq': _L0_attn_in['bq'], 'L0_attn_Wk': _L0_attn_in['Wk'], 'L0_attn_bk': _L0_attn_in['bk'], 'L0_attn_Wv': _L0_attn_in['Wv'], 'L0_attn_bv': _L0_attn_in['bv'], 'L0_attn_Wp': _L0_attn_in['Wp'], 'L0_attn_bp': _L0_attn_in['bp'], 'L0_attn_bias_table': _L0_attn_in['bias_table'], 'L0_attn_temperature': _L0_attn_in['temperature'], 'L0_xattn_Wq': _L0_xattn_in['Wq'], 'L0_xattn_Wk': _L0_xattn_in['Wk'], 'L0_xattn_Wv': _L0_xattn_in['Wv'], 'L0_xattn_W_film_in': _L0_xattn_in['W_film_in'], 'L0_xattn_b_film_in': _L0_xattn_in['b_film_in'], 'L0_xattn_W_film_out': _L0_xattn_in['W_film_out'], 'L0_xattn_b_film_out': _L0_xattn_in['b_film_out'], 'L0_xattn_g_norm_in': _L0_xattn_in['g_norm_in'], 'L0_xattn_b_norm_in': _L0_xattn_in['b_norm_in'], 'L0_xattn_g_norm_out': _L0_xattn_in['g_norm_out'], 'L0_xattn_b_norm_out': _L0_xattn_in['b_norm_out'], 'L0_xattn_g_ffn': _L0_xattn_in['g_ffn'], 'L0_xattn_b_ffn': _L0_xattn_in['b_ffn'], 'L0_xattn_W1': _L0_xattn_in['W1'], 'L0_xattn_b1': _L0_xattn_in['b1'], 'L0_xattn_W2': _L0_xattn_in['W2'], 'L0_xattn_b2': _L0_xattn_in['b2'], 'L0_xattn_log_dt': _L0_xattn_in['log_dt'], 'L0_xattn_A_re': _L0_xattn_in['A_re'], 'L0_xattn_A_im': _L0_xattn_in['A_im'], 'L0_xattn_C_re': _L0_xattn_in['C_re'], 'L0_xattn_C_im': _L0_xattn_in['C_im'], 'L0_xattn_D_skip': _L0_xattn_in['D_skip'], 'L0_xattn_mod_gate': _L0_xattn_in['mod_gate'], 'L0_ffn_slot_init': _L0_ffn_in['slot_init'], 'L0_ffn_slot_scale': _L0_ffn_in['slot_scale'], 'L0_ffn_w1': _L0_ffn_in['w1'], 'L0_ffn_b1': _L0_ffn_in['b1'], 'L0_ffn_w2': _L0_ffn_in['w2'], 'L0_ffn_b2': _L0_ffn_in['b2'], 'L0_ffn_gru_wih': _L0_ffn_in['gru_wih'], 'L0_ffn_gru_whh': _L0_ffn_in['gru_whh'], 'L0_ffn_gru_bih': _L0_ffn_in['gru_bih'], 'L0_ffn_gru_bhh': _L0_ffn_in['gru_bhh'], 'L0_ffn_wv': _L0_ffn_in['wv'], 'L0_ffn_bv': _L0_ffn_in['bv'], 'L0_ffn_wo': _L0_ffn_in['wo'], 'L0_ffn_bo': _L0_ffn_in['bo'], 'L0_ffn_tau': _L0_ffn_in['tau'], 'L1_attn_Wq': _L1_attn_in['Wq'], 'L1_attn_bq': _L1_attn_in['bq'], 'L1_attn_Wk': _L1_attn_in['Wk'], 'L1_attn_bk': _L1_attn_in['bk'], 'L1_attn_Wv': _L1_attn_in['Wv'], 'L1_attn_bv': _L1_attn_in['bv'], 'L1_attn_Wo': _L1_attn_in['Wo'], 'L1_attn_bo': _L1_attn_in['bo'], 'L1_xattn_Wq': _L1_xattn_in['Wq'], 'L1_xattn_Wk': _L1_xattn_in['Wk'], 'L1_xattn_Wv': _L1_xattn_in['Wv'], 'L1_xattn_Wout': _L1_xattn_in['Wout'], 'L1_xattn_bout': _L1_xattn_in['bout'], 'L1_ffn_ln1_w': _L1_ffn_in['ln1_w'], 'L1_ffn_ln2_w': _L1_ffn_in['ln2_w'], 'L1_ffn_Wq': _L1_ffn_in['Wq'], 'L1_ffn_Wk': _L1_ffn_in['Wk'], 'L1_ffn_Wv': _L1_ffn_in['Wv'], 'L1_ffn_Wo': _L1_ffn_in['Wo'], 'L1_ffn_Wr': _L1_ffn_in['Wr'], 'L1_ffn_Wg': _L1_ffn_in['Wg'], 'L1_ffn_Wu': _L1_ffn_in['Wu'], 'L1_ffn_Wd': _L1_ffn_in['Wd'], 'L2_attn_Wq': _L2_attn_in['Wq'], 'L2_attn_bq': _L2_attn_in['bq'], 'L2_attn_Wk': _L2_attn_in['Wk'], 'L2_attn_bk': _L2_attn_in['bk'], 'L2_attn_Wv': _L2_attn_in['Wv'], 'L2_attn_bv': _L2_attn_in['bv'], 'L2_attn_Wo': _L2_attn_in['Wo'], 'L2_attn_bo': _L2_attn_in['bo'], 'L2_xattn_Wq': _L2_xattn_in['Wq'], 'L2_xattn_bq': _L2_xattn_in['bq'], 'L2_xattn_Wk': _L2_xattn_in['Wk'], 'L2_xattn_bk': _L2_xattn_in['bk'], 'L2_xattn_Wv': _L2_xattn_in['Wv'], 'L2_xattn_bv': _L2_xattn_in['bv'], 'L2_xattn_W1': _L2_xattn_in['W1'], 'L2_xattn_b1': _L2_xattn_in['b1'], 'L2_xattn_W2': _L2_xattn_in['W2'], 'L2_xattn_b2': _L2_xattn_in['b2'], 'L2_ffn_We': _L2_ffn_in['We'], 'L2_ffn_be': _L2_ffn_in['be'], 'L2_ffn_Wg': _L2_ffn_in['Wg'], 'L2_ffn_bg': _L2_ffn_in['bg'], 'L3_attn_W_qkv': _L3_attn_in['W_qkv'], 'L3_attn_W_out': _L3_attn_in['W_out'], 'L3_xattn_Wq': _L3_xattn_in['Wq'], 'L3_xattn_bq': _L3_xattn_in['bq'], 'L3_xattn_Wk': _L3_xattn_in['Wk'], 'L3_xattn_bk': _L3_xattn_in['bk'], 'L3_xattn_Wv': _L3_xattn_in['Wv'], 'L3_xattn_bv': _L3_xattn_in['bv'], 'L3_xattn_Wo': _L3_xattn_in['Wo'], 'L3_xattn_bo': _L3_xattn_in['bo'], 'L3_ffn_gate_w': _L3_ffn_in['gate_w'], 'L3_ffn_gate_b': _L3_ffn_in['gate_b'], 'L3_ffn_expert_w': _L3_ffn_in['expert_w'], 'L3_ffn_expert_b': _L3_ffn_in['expert_b']}

def reference(x, ctx_768, mask_BxS_bf1, mask_BxS2_bf1, L0_attn_Wq, L0_attn_bq, L0_attn_Wk, L0_attn_bk, L0_attn_Wv, L0_attn_bv, L0_attn_Wp, L0_attn_bp, L0_attn_bias_table, L0_attn_temperature, L0_xattn_Wq, L0_xattn_Wk, L0_xattn_Wv, L0_xattn_W_film_in, L0_xattn_b_film_in, L0_xattn_W_film_out, L0_xattn_b_film_out, L0_xattn_g_norm_in, L0_xattn_b_norm_in, L0_xattn_g_norm_out, L0_xattn_b_norm_out, L0_xattn_g_ffn, L0_xattn_b_ffn, L0_xattn_W1, L0_xattn_b1, L0_xattn_W2, L0_xattn_b2, L0_xattn_log_dt, L0_xattn_A_re, L0_xattn_A_im, L0_xattn_C_re, L0_xattn_C_im, L0_xattn_D_skip, L0_xattn_mod_gate, L0_ffn_slot_init, L0_ffn_slot_scale, L0_ffn_w1, L0_ffn_b1, L0_ffn_w2, L0_ffn_b2, L0_ffn_gru_wih, L0_ffn_gru_whh, L0_ffn_gru_bih, L0_ffn_gru_bhh, L0_ffn_wv, L0_ffn_bv, L0_ffn_wo, L0_ffn_bo, L0_ffn_tau, L1_attn_Wq, L1_attn_bq, L1_attn_Wk, L1_attn_bk, L1_attn_Wv, L1_attn_bv, L1_attn_Wo, L1_attn_bo, L1_xattn_Wq, L1_xattn_Wk, L1_xattn_Wv, L1_xattn_Wout, L1_xattn_bout, L1_ffn_ln1_w, L1_ffn_ln2_w, L1_ffn_Wq, L1_ffn_Wk, L1_ffn_Wv, L1_ffn_Wo, L1_ffn_Wr, L1_ffn_Wg, L1_ffn_Wu, L1_ffn_Wd, L2_attn_Wq, L2_attn_bq, L2_attn_Wk, L2_attn_bk, L2_attn_Wv, L2_attn_bv, L2_attn_Wo, L2_attn_bo, L2_xattn_Wq, L2_xattn_bq, L2_xattn_Wk, L2_xattn_bk, L2_xattn_Wv, L2_xattn_bv, L2_xattn_W1, L2_xattn_b1, L2_xattn_W2, L2_xattn_b2, L2_ffn_We, L2_ffn_be, L2_ffn_Wg, L2_ffn_bg, L3_attn_W_qkv, L3_attn_W_out, L3_xattn_Wq, L3_xattn_bq, L3_xattn_Wk, L3_xattn_bk, L3_xattn_Wv, L3_xattn_bv, L3_xattn_Wo, L3_xattn_bo, L3_ffn_gate_w, L3_ffn_gate_b, L3_ffn_expert_w, L3_ffn_expert_b):
    import jax
    import jax.numpy as jnp

    def _L0_attn_ref(x, Wq, bq, Wk, bk, Wv, bv, Wp, bp, bias_table, temperature):
        import jax, jax.numpy as jnp
        import numpy as np
        EMB = 128
        HEADS = 16
        HEAD_DIM = EMB // HEADS
        MAX_LEN = 125
        B, N, C = x.shape
        H, D = (HEADS, C // HEADS)

        def split_heads(t):
            return t.reshape(B, N, H, D).transpose(0, 2, 1, 3)
        q = split_heads(x @ Wq + bq)
        k = split_heads(x @ Wk + bk)
        v = split_heads(x @ Wv + bv)
        energy = jnp.einsum('bhqd,bhkd->bhqk', q, k)
        pos = jnp.arange(N)
        rel = pos[:, None] - pos[None, :] + (N - 1)
        rel = jnp.clip(rel, 0, bias_table.shape[0] - 1)
        bias = bias_table[rel].transpose(2, 0, 1)
        energy = energy + bias[None]
        scaling = jnp.sqrt(jnp.float32(C))
        temp = jnp.clip(temperature[0], 0.1, 10.0)
        att = jax.nn.softmax(energy / (scaling * temp), axis=-1)
        out = jnp.einsum('bhqk,bhkd->bhqd', att, v)
        out = out.transpose(0, 2, 1, 3).reshape(B, N, C)
        return out @ Wp + bp

    def _L0_xattn_ref(x_text, x_vision, text_mask, vision_mask, Wq, Wk, Wv, W_film_in, b_film_in, W_film_out, b_film_out, g_norm_in, b_norm_in, g_norm_out, b_norm_out, g_ffn, b_ffn, W1, b1, W2, b2, log_dt, A_re, A_im, C_re, C_im, D_skip, mod_gate):
        import jax, jax.numpy as jnp
        import numpy as np
        B, T, DT, G, DV = (16, 64, 128, 72, 96)
        H, DH = (4, 32)
        INNER = H * DH
        HID = 4 * DT
        N_STATE = 64
        K_TOP = 32

        def layernorm(x, g, b, eps=1e-05):
            m = x.mean(-1, keepdims=True)
            v = x.var(-1, keepdims=True)
            return (x - m) * jax.lax.rsqrt(v + eps) * g + b

        def s4d(x, log_dt, A_re, A_im, C_re, C_im, D_skip):
            Bb, L, D = x.shape
            dt = jnp.exp(log_dt)
            A = A_re + 1j * A_im
            C = C_re + 1j * C_im
            dtA = dt[:, None] * A
            dC = C * (jnp.exp(dtA) - 1.0) / A
            powers = jnp.exp(dtA[:, :, None] * jnp.arange(L))
            K = 2.0 * jnp.einsum('dn,dnl->dl', dC, powers).real
            n = 2 * L
            Kf = jnp.fft.rfft(K, n=n, axis=-1)
            xf = jnp.fft.rfft(x, n=n, axis=1)
            y = jnp.fft.irfft(xf * Kf.T[None], n=n, axis=1)[:, :L]
            return y + x * D_skip
        Bb, Tt, D = x_text.shape
        Gg = x_vision.shape[1]
        Q = (x_text @ Wq).reshape(Bb, Tt, H, DH)
        K = (x_vision @ Wk).reshape(Bb, Gg, H, DH)
        scores = jnp.einsum('bthd,bghd->bhtg', Q, K) / np.sqrt(DH).astype(np.float32)
        scores = jnp.where(vision_mask[:, None, None, :], scores, -jnp.inf)
        topv, topi = jax.lax.top_k(scores, K_TOP)
        probs = jax.nn.softmax(topv, axis=-1)
        bi = jnp.arange(Bb)[:, None, None, None]
        hi = jnp.arange(H)[None, :, None, None]
        ti = jnp.arange(Tt)[None, None, :, None]
        attn = jnp.zeros_like(scores).at[bi, hi, ti, topi].set(probs)
        attn_mean = attn.mean(axis=1)
        V = x_vision @ Wv
        c_t = jnp.einsum('btg,bgd->btd', attn_mean, V)
        c_t = c_t * text_mask[..., None]
        x = layernorm(x_text, g_norm_in, b_norm_in)
        scale_in, shift_in = jnp.split(c_t @ W_film_in + b_film_in, 2, axis=-1)
        x = x * (1.0 + mod_gate * scale_in) + mod_gate * shift_in
        y = s4d(x, log_dt, A_re, A_im, C_re, C_im, D_skip)
        scale_out, shift_out = jnp.split(c_t @ W_film_out + b_film_out, 2, axis=-1)
        y = y * (1.0 + mod_gate * scale_out) + mod_gate * shift_out
        xt = x_text + y
        h = layernorm(xt, g_ffn, b_ffn)
        h = jax.nn.gelu(h @ W1 + b1, approximate=False) @ W2 + b2
        xt = xt + h
        return layernorm(xt, g_norm_out, b_norm_out)

    def _L0_ffn_ref(x, slot_init, slot_scale, w1, b1, w2, b2, gru_wih, gru_whh, gru_bih, gru_bhh, wv, bv, wo, bo, tau):
        import jax, jax.numpy as jnp
        import numpy as np
        D_MODEL = 128
        NUM_SLOTS = 64
        TOP_K = 8
        B, T = (4, 512)

        def _forward(x, slot_init, slot_scale, w1, b1, w2, b2, gru_wih, gru_whh, gru_bih, gru_bhh, wv, bv, wo, bo, tau):
            Bn, Tn, D = x.shape
            Sn = slot_init.shape[0]
            S = jnp.broadcast_to((slot_init * slot_scale)[None], (Bn, Sn, D)).astype(x.dtype)
            slot_mean = S.mean(axis=1, keepdims=True)
            ctx = jnp.concatenate([x, jnp.broadcast_to(slot_mean, x.shape)], axis=-1)
            h = jax.nn.gelu(ctx @ w1.T + b1, approximate=False)
            route_logits = (h @ w2.T + b2) / (jnp.abs(tau) + 0.1)
            topk_vals, topk_idx = jax.lax.top_k(route_logits, TOP_K)
            topk_w = jax.nn.softmax(topk_vals, axis=-1)
            alpha = jnp.sum(topk_w[..., None] * jax.nn.one_hot(topk_idx, Sn, dtype=x.dtype), axis=-2)
            slot_input = jnp.einsum('bts,btd->bsd', alpha, x)
            slot_wsum = alpha.sum(axis=1) + 1e-08
            gi = (slot_input / slot_wsum[..., None]).reshape(Bn * Sn, D)
            hs = S.reshape(Bn * Sn, D)
            gx = gi @ gru_wih.T + gru_bih
            gh = hs @ gru_whh.T + gru_bhh
            xr, xz, xn = jnp.split(gx, 3, axis=-1)
            hr, hz, hn = jnp.split(gh, 3, axis=-1)
            r = jax.nn.sigmoid(xr + hr)
            z = jax.nn.sigmoid(xz + hz)
            n = jnp.tanh(xn + r * hn)
            h_new = (1.0 - z) * n + z * hs
            S_new = h_new.reshape(Bn, Sn, D)
            slot_values = S_new @ wv.T + bv
            out = jnp.einsum('bts,bsd->btd', alpha, slot_values)
            return out @ wo.T + bo
        return _forward(x, slot_init, slot_scale, w1, b1, w2, b2, gru_wih, gru_whh, gru_bih, gru_bhh, wv, bv, wo, bo, tau)

    def _L1_attn_ref(x, Wq, bq, Wk, bk, Wv, bv, Wo, bo):
        import jax, jax.numpy as jnp
        import numpy as np
        H = 8
        EPS = 1e-06

        def _pos_encoding(S, D):
            pos = jnp.arange(S, dtype=jnp.float32)[:, None]
            div = jnp.exp(jnp.arange(0, D, 2, dtype=jnp.float32) * (-np.log(10000.0) / D))
            pe = jnp.zeros((S, D), dtype=jnp.float32)
            pe = pe.at[:, 0::2].set(jnp.sin(pos * div))
            pe = pe.at[:, 1::2].set(jnp.cos(pos * div))
            return pe
        S, B, D = x.shape
        dh = D // H
        h = x + _pos_encoding(S, D)[:, None, :]
        q = (h @ Wq.T + bq).reshape(S, B, H, dh)
        k = (h @ Wk.T + bk).reshape(S, B, H, dh)
        v = (h @ Wv.T + bv).reshape(S, B, H, dh)
        pq = jax.nn.elu(q) + 1.0
        pk = jax.nn.elu(k) + 1.0
        kv = jnp.einsum('sbhd,sbhe->bhde', pk, v)
        z = pk.sum(axis=0)
        num = jnp.einsum('sbhd,bhde->sbhe', pq, kv)
        den = jnp.einsum('sbhd,bhd->sbh', pq, z)
        att = num / (den[..., None] + EPS)
        out = att.reshape(S, B, D) @ Wo.T + bo
        return out

    def _L1_xattn_ref(x, context, Wq, Wk, Wv, Wout, bout):
        import jax, jax.numpy as jnp
        import numpy as np
        HEADS = 8
        DIM_HEAD = 64
        SCALE = DIM_HEAD ** (-0.5)
        b, n, _ = x.shape
        m = context.shape[1]
        q = (x @ Wq).reshape(b, n, HEADS, DIM_HEAD)
        k = (context @ Wk).reshape(b, m, HEADS, DIM_HEAD)
        v = (context @ Wv).reshape(b, m, HEADS, DIM_HEAD)
        sim = jnp.einsum('bihd,bjhd->bhij', q, k) * SCALE
        attn = jax.nn.softmax(sim, axis=-1)
        out = jnp.einsum('bhij,bjhd->bihd', attn, v).reshape(b, n, HEADS * DIM_HEAD)
        return out @ Wout + bout

    def _L1_ffn_ref(hidden_states, ln1_w, ln2_w, Wq, Wk, Wv, Wo, Wr, Wg, Wu, Wd):
        import jax, jax.numpy as jnp
        import numpy as np
        B, S, D = (2, 256, 128)
        H, HKV = (16, 4)
        HD = D // H
        F, E, K = (256, 8, 2)
        THETA = 10000.0
        EPS = 1e-05

        def _rmsnorm(x, w):
            return x * jax.lax.rsqrt(jnp.mean(x * x, axis=-1, keepdims=True) + EPS) * w

        def _rope_cos_sin(seq_len, head_dim, theta):
            inv_freq = 1.0 / theta ** (jnp.arange(0, head_dim, 2, dtype=jnp.float32) / head_dim)
            freqs = jnp.arange(seq_len, dtype=jnp.float32)[:, None] * inv_freq
            return (jnp.cos(freqs), jnp.sin(freqs))

        def _apply_rope(x, cos, sin):
            x1, x2 = jnp.split(x, 2, axis=-1)
            c = cos[None, :, None, :]
            s = sin[None, :, None, :]
            return jnp.concatenate([x1 * c - x2 * s, x2 * c + x1 * s], axis=-1)
        b, s, d = hidden_states.shape
        residual = hidden_states
        h = _rmsnorm(hidden_states, ln1_w)
        q = (h @ Wq).reshape(b, s, H, HD)
        k = (h @ Wk).reshape(b, s, HKV, HD)
        v = (h @ Wv).reshape(b, s, HKV, HD)
        cos, sin = _rope_cos_sin(s, HD, THETA)
        q = _apply_rope(q, cos, sin)
        k = _apply_rope(k, cos, sin)
        rep = H // HKV
        k = jnp.repeat(k, rep, axis=2)
        v = jnp.repeat(v, rep, axis=2)
        scores = jnp.einsum('bqhd,bkhd->bhqk', q, k) / np.sqrt(HD).astype(np.float32)
        causal = jnp.tril(jnp.ones((s, s), dtype=bool))
        scores = jnp.where(causal[None, None], scores, jnp.finfo(scores.dtype).min)
        attn = jax.nn.softmax(scores, axis=-1)
        ctx = jnp.einsum('bhqk,bkhd->bqhd', attn, v).reshape(b, s, H * HD)
        attn_out = ctx @ Wo
        h = jnp.clip(residual + attn_out, -100.0, 100.0)
        residual = h
        hn = _rmsnorm(h, ln2_w)
        flat = hn.reshape(b * s, d)
        logits = flat @ Wr
        probs = jax.nn.softmax(logits, axis=-1)
        topv, topi = jax.lax.top_k(probs, K)
        topv = topv / jnp.sum(topv, axis=-1, keepdims=True)
        w = jnp.sum(jax.nn.one_hot(topi, E, dtype=flat.dtype) * topv[..., None], axis=1)
        g = jnp.einsum('td,edf->etf', flat, Wg)
        u = jnp.einsum('td,edf->etf', flat, Wu)
        a = jax.nn.silu(g) * u
        o = jnp.einsum('etf,efd->etd', a, Wd)
        moe_out = jnp.einsum('te,etd->td', w, o).reshape(b, s, d)
        out = jnp.clip(residual + moe_out, -100.0, 100.0)
        return out

    def _L2_attn_ref(x, Wq, bq, Wk, bk, Wv, bv, Wo, bo):
        import jax, jax.numpy as jnp
        import numpy as np
        B, L, D = (2, 256, 128)
        H = 16
        DH = D // H
        b, l, _ = x.shape

        def split_heads(t):
            return t.reshape(b, l, H, DH).transpose((0, 2, 1, 3))
        q = jax.nn.relu(split_heads(x @ Wq + bq))
        k = jax.nn.relu(split_heads(x @ Wk + bk))
        v = split_heads(x @ Wv + bv)
        context = jnp.einsum('bhld,bhkd->bhlk', q, k) / (l * DH)
        attn = jnp.einsum('bhlk,bhkd->bhld', context, v)
        attn = attn.transpose((0, 2, 1, 3)).reshape(b, l, D)
        return attn @ Wo + bo

    def _L2_xattn_ref(x, y, Wq, bq, Wk, bk, Wv, bv, W1, b1, W2, b2):
        import jax, jax.numpy as jnp
        import numpy as np
        IMAGE_DIM = 128
        TEXT_DIM = 96
        NUM_HEADS = 16
        HEAD_DIM = IMAGE_DIM // NUM_HEADS
        B, N, _ = x.shape
        M = y.shape[1]
        q = (x @ Wq + bq).reshape(B, N, NUM_HEADS, HEAD_DIM)
        k = (y @ Wk + bk).reshape(B, M, NUM_HEADS, HEAD_DIM)
        v = (y @ Wv + bv).reshape(B, M, NUM_HEADS, HEAD_DIM)
        scale = 1.0 / np.sqrt(HEAD_DIM)
        scores = jnp.einsum('bnhd,bmhd->bhnm', q, k) * scale
        attn = jax.nn.softmax(scores, axis=-1)
        out = jnp.einsum('bhnm,bmhd->bnhd', attn, v).reshape(B, N, IMAGE_DIM)
        h = jax.nn.relu(out @ W1 + b1)
        return h @ W2 + b2

    def _L2_ffn_ref(x, We, be, Wg, bg):
        import jax, jax.numpy as jnp
        import numpy as np
        D_MODEL = 128
        NUM_EXPERTS = 8
        TOP_K = 2
        B, S, D = x.shape
        xf = x.reshape(-1, D)
        gate_logits = xf @ Wg.T + bg
        topk_vals, topk_idx = jax.lax.top_k(gate_logits, TOP_K)
        gate_w = jax.nn.softmax(topk_vals, axis=-1)
        all_out = jnp.einsum('nd,ehd->neh', xf, We) + be
        sel = jnp.take_along_axis(all_out, topk_idx[:, :, None], axis=1)
        out = jnp.sum(sel * gate_w[:, :, None], axis=1)
        return out.reshape(B, S, D)

    def _L3_attn_ref(x, W_qkv, W_out):
        import jax, jax.numpy as jnp
        import numpy as np
        NUM_HEADS = 16
        HEAD_DIM = 64
        NEG_INF = -1000000000.0

        def rotary_embedding(x, seq_len, head_dim):
            positions = jnp.arange(seq_len)
            dim_pairs = jnp.arange(0, head_dim, 2)
            freqs = 1.0 / 10000.0 ** (dim_pairs / head_dim)
            angles = positions[:, None] * freqs[None, :]
            cos = jnp.cos(angles)[:, None, :]
            sin = jnp.sin(angles)[:, None, :]
            x1 = x[..., ::2]
            x2 = x[..., 1::2]
            out1 = x1 * cos - x2 * sin
            out2 = x1 * sin + x2 * cos
            return jnp.stack([out1, out2], axis=-1).reshape(x.shape)
        batch, seq_len, embed_dim = x.shape
        qkv = jnp.einsum('bse,ef->bsf', x, W_qkv)
        qkv = qkv.reshape(batch, seq_len, 3, NUM_HEADS, HEAD_DIM)
        q, k, v = (qkv[:, :, 0], qkv[:, :, 1], qkv[:, :, 2])
        q = rotary_embedding(q, seq_len, HEAD_DIM)
        k = rotary_embedding(k, seq_len, HEAD_DIM)
        scale = 1.0 / jnp.sqrt(jnp.asarray(HEAD_DIM, dtype=x.dtype))
        scores = jnp.einsum('bqhd,bkhd->bhqk', q, k) * scale
        mask = jnp.tril(jnp.ones((seq_len, seq_len), dtype=bool))[None, None, :, :]
        scores = jnp.where(mask, scores, NEG_INF)
        weights = jax.nn.softmax(scores, axis=-1)
        out = jnp.einsum('bhqk,bkhd->bqhd', weights, v)
        out = out.reshape(batch, seq_len, NUM_HEADS * HEAD_DIM)
        return jnp.einsum('bsf,fe->bse', out, W_out)

    def _L3_xattn_ref(x, y, Wq, bq, Wk, bk, Wv, bv, Wo, bo):
        import math
        import jax, jax.numpy as jnp
        import numpy as np
        B, SQ, SKV = (4, 256, 256)
        D_EMBED, D_CROSS, D_ATT, N_HEADS = (128, 96, 128, 16)
        D_HEAD = D_ATT // N_HEADS

        def _split_heads(t):
            b, s, _ = t.shape
            return t.reshape(b, s, N_HEADS, D_HEAD).transpose(0, 2, 1, 3)
        q = _split_heads(x @ Wq + bq)
        k = _split_heads(y @ Wk + bk)
        v = _split_heads(y @ Wv + bv)
        scale = 1.0 / math.sqrt(D_HEAD)
        scores = jnp.einsum('bhqd,bhkd->bhqk', q, k) * scale
        weights = jax.nn.softmax(scores, axis=-1)
        out = jnp.einsum('bhqk,bhkd->bhqd', weights, v)
        out = out.transpose(0, 2, 1, 3).reshape(x.shape[0], x.shape[1], D_ATT)
        return out @ Wo + bo

    def _L3_ffn_ref(x, gate_w, gate_b, expert_w, expert_b):
        import jax, jax.numpy as jnp
        import numpy as np
        NEG_INF = -1e+30
        K = 2
        pooled = x.mean(axis=1)
        logits = pooled @ gate_w.T + gate_b
        topk_vals, _ = jax.lax.top_k(logits, K)
        min_topk = topk_vals[:, -1:]
        masked = jnp.where(logits < min_topk, -jnp.inf, logits)
        gates = jax.nn.softmax(masked, axis=-1)
        expert_out = jax.nn.gelu(jnp.einsum('bsd,eod->beso', x, expert_w) + expert_b[None, :, None, :], approximate=False)
        return jnp.einsum('be,beso->bso', gates, expert_out)
    x = _layernorm(x + _L0_attn_ref(x, L0_attn_Wq, L0_attn_bq, L0_attn_Wk, L0_attn_bk, L0_attn_Wv, L0_attn_bv, L0_attn_Wp, L0_attn_bp, L0_attn_bias_table, L0_attn_temperature), axis=-1)
    x = _layernorm(x + _L0_xattn_ref(x, ctx_768, mask_BxS_bf1, mask_BxS2_bf1, L0_xattn_Wq, L0_xattn_Wk, L0_xattn_Wv, L0_xattn_W_film_in, L0_xattn_b_film_in, L0_xattn_W_film_out, L0_xattn_b_film_out, L0_xattn_g_norm_in, L0_xattn_b_norm_in, L0_xattn_g_norm_out, L0_xattn_b_norm_out, L0_xattn_g_ffn, L0_xattn_b_ffn, L0_xattn_W1, L0_xattn_b1, L0_xattn_W2, L0_xattn_b2, L0_xattn_log_dt, L0_xattn_A_re, L0_xattn_A_im, L0_xattn_C_re, L0_xattn_C_im, L0_xattn_D_skip, L0_xattn_mod_gate), axis=-1)
    x = _layernorm(x + _L0_ffn_ref(x, L0_ffn_slot_init, L0_ffn_slot_scale, L0_ffn_w1, L0_ffn_b1, L0_ffn_w2, L0_ffn_b2, L0_ffn_gru_wih, L0_ffn_gru_whh, L0_ffn_gru_bih, L0_ffn_gru_bhh, L0_ffn_wv, L0_ffn_bv, L0_ffn_wo, L0_ffn_bo, L0_ffn_tau), axis=-1)
    x = _layernorm(x + _L1_attn_ref(x, L1_attn_Wq, L1_attn_bq, L1_attn_Wk, L1_attn_bk, L1_attn_Wv, L1_attn_bv, L1_attn_Wo, L1_attn_bo), axis=-1)
    x = _layernorm(x + _L1_xattn_ref(x, ctx_768, L1_xattn_Wq, L1_xattn_Wk, L1_xattn_Wv, L1_xattn_Wout, L1_xattn_bout), axis=-1)
    x = _layernorm(x + _L1_ffn_ref(x, L1_ffn_ln1_w, L1_ffn_ln2_w, L1_ffn_Wq, L1_ffn_Wk, L1_ffn_Wv, L1_ffn_Wo, L1_ffn_Wr, L1_ffn_Wg, L1_ffn_Wu, L1_ffn_Wd), axis=-1)
    x = _layernorm(x + _L2_attn_ref(x, L2_attn_Wq, L2_attn_bq, L2_attn_Wk, L2_attn_bk, L2_attn_Wv, L2_attn_bv, L2_attn_Wo, L2_attn_bo), axis=-1)
    x = _layernorm(x + _L2_xattn_ref(x, ctx_768, L2_xattn_Wq, L2_xattn_bq, L2_xattn_Wk, L2_xattn_bk, L2_xattn_Wv, L2_xattn_bv, L2_xattn_W1, L2_xattn_b1, L2_xattn_W2, L2_xattn_b2), axis=-1)
    x = _layernorm(x + _L2_ffn_ref(x, L2_ffn_We, L2_ffn_be, L2_ffn_Wg, L2_ffn_bg), axis=-1)
    x = _layernorm(x + _L3_attn_ref(x, L3_attn_W_qkv, L3_attn_W_out), axis=-1)
    x = _layernorm(x + _L3_xattn_ref(x, ctx_768, L3_xattn_Wq, L3_xattn_bq, L3_xattn_Wk, L3_xattn_bk, L3_xattn_Wv, L3_xattn_bv, L3_xattn_Wo, L3_xattn_bo), axis=-1)
    x = _layernorm(x + _L3_ffn_ref(x, L3_ffn_gate_w, L3_ffn_gate_b, L3_ffn_expert_w, L3_ffn_expert_b), axis=-1)
    return x

_drawn_inputs = setup_inputs


def setup_inputs(seed=0):
    import zlib

    import numpy as np

    out = dict(_drawn_inputs(seed))
    spreads = {'L0_attn_bq': (0.0, 0.8),
     'L0_attn_bk': (0.0, 2.0),
     'L0_attn_bv': (0.0, 0.1),
     'L0_attn_bp': (0.0, 0.1),
     'L0_xattn_b_film_in': (0.0, 0.1),
     'L0_xattn_b_film_out': (0.0, 0.1),
     'L0_xattn_g_norm_in': (1.0, 0.2),
     'L0_xattn_b_norm_in': (0.0, 0.1),
     'L0_xattn_g_norm_out': (1.0, 0.2),
     'L0_xattn_b_norm_out': (0.0, 0.1),
     'L0_xattn_g_ffn': (1.0, 0.6),
     'L0_xattn_b_ffn': (0.0, 0.396),
     'L0_xattn_b1': (0.0, 0.1),
     'L0_xattn_b2': (0.0, 0.1),
     'L0_xattn_A_re': (-0.5, 0.2),
     'L0_ffn_slot_scale': (1.0, 0.6),
     'L0_ffn_b1': (0.0, 0.1),
     'L0_ffn_b2': (0.0, 0.1),
     'L0_ffn_gru_bih': (0.0, 0.1),
     'L0_ffn_gru_bhh': (0.0, 0.1),
     'L0_ffn_bv': (0.0, 0.1),
     'L0_ffn_bo': (0.0, 0.1),
     'L1_attn_bq': (0.0, 0.526),
     'L1_attn_bk': (0.0, 0.455),
     'L1_attn_bv': (0.0, 0.1),
     'L1_attn_bo': (0.0, 0.1),
     'L2_attn_bq': (0.0, 0.294),
     'L2_attn_bk': (0.0, 0.362),
     'L2_attn_bv': (0.0, 0.1),
     'L2_attn_bo': (0.0, 0.1),
     'L3_ffn_gate_b': (0.0, 0.1),
     'L3_ffn_expert_b': (0.0, 0.1)}
    factors = {'L0_attn_Wq': 8.0,
     'L0_attn_Wk': 8.0,
     'L0_attn_bias_table': 92.037,
     'L0_xattn_Wq': 3.498,
     'L0_xattn_Wk': 3.665,
     'L1_ffn_ln1_w': 5.553,
     'L1_ffn_ln2_w': 6.18,
     'L1_ffn_Wq': 8.0,
     'L1_ffn_Wk': 8.0,
     'L1_ffn_Wr': 3.276,
     'L1_ffn_Wg': 3.247,
     'L1_ffn_Wu': 3.23,
     'L1_ffn_Wd': 3.189,
     'L2_xattn_bk': 200.0,
     'L3_xattn_bq': 24.744,
     'L3_xattn_bk': 200.0,
     'L3_xattn_bv': 5.615,
     'L3_xattn_bo': 5.629}
    for name, (base, spread) in spreads.items():
        noise = np.random.default_rng([zlib.crc32(name.encode()), seed]).standard_normal(out[name].shape)
        drawn = base * np.exp(spread * noise) if base else spread * noise
        out[name] = jnp.asarray(drawn.astype(out[name].dtype))
    for name, factor in factors.items():
        out[name] = (out[name] * factor).astype(out[name].dtype)
    return out
```

```python
from contextlib import ExitStack

import numpy as np

import concourse.bass as bass
from concourse import mybir

ALU = mybir.AluOpType
ACT = mybir.ActivationFunctionType
AX = mybir.AxisListType
F32 = mybir.dt.float32
BF16 = mybir.dt.bfloat16
U8 = mybir.dt.uint8
U32 = mybir.dt.uint32

P = 128
NB = 32
DM = 128
DC = 96
STEPS = NB // 2
D64 = 64
NE = 8
NS = 64
D16 = 16
H16, D8 = 16, 8
EPS = 1e-5
NEG = -1.0e30

STAGES = list(range(12))
ORDER = [0, 1, 2, 3, 4, 5, 5.5, 6, 7, 8, 9, 10, 11]
BUFFER = {stage: i % 2 for i, stage in enumerate(ORDER)}


class Count:

    def __init__(self, sem, base, per):
        self.sem, self.base, self.per = sem, base, per

    def at(self, step, n):
        return step * self.per + (self.base + n)


class Signals:

    def __init__(self, nc):
        self.nc, self.last, self.of = nc, {}, (0, "")

    def new_stage(self, name):
        if self.last:
            self.nc.clear_and_free_semaphores([c.sem for c, _ in self.last.values()])
            self.nc.all_engine_barrier()
        self.last, self.of = {}, (self.of[0] + 1, name)

    def one(self, name, per, steps):
        if name not in self.last:
            c = Count(self.nc.alloc_semaphore(name=f"{self.of[1]}{self.of[0]}_{name}"), 0, per)
        else:
            old, old_steps = self.last[name]
            c = Count(old.sem, old.base + old.per * old_steps, per)
        self.last[name] = (c, steps)
        return c

    def pair(self, name, per=1, steps=STEPS):
        return [self.one(f"{name}{s}", per, steps) for s in range(2)]

    def ring(self, name, n, per, steps=STEPS):
        return [self.one(f"{name}{r}", per, steps) for r in range(n)]



def rows(v):
    return np.broadcast_to(np.asarray(v).reshape(1, -1), (P, np.asarray(v).size))


def col(v):
    return np.asarray(v).reshape(-1, 1)


def head_mask():
    return (np.arange(P)[:, None] // D8 == np.arange(H16)[None, :]).astype(np.float32)


def chunks(w):
    c = w.shape[0] // P
    return w.reshape(c, P, w.shape[1]).transpose(1, 0, 2).reshape(P, -1)


def host_pack(I):
    A = []

    def put(stage, name, a):
        A.append((stage, name, np.asarray(a)))

    g = lambda n: np.asarray(I[n])
    put("const", "ident", np.eye(P, dtype=np.float32))
    put("const", "head_mask", head_mask())
    upper = np.where(np.arange(P)[None, :] > np.arange(P)[:, None], NEG, 0.0).astype(np.float32)
    put("const", "iota8", rows(np.tile(np.arange(NE, dtype=np.float32), NB)))
    put("const", "ones", np.ones((P, P), np.float32))
    put("const", "causal", np.concatenate([upper, upper.T], 1))
    n = "L0_attn_"
    for w in ("Wq", "Wk", "Wv"):
        put(0, n + w, g(n + w))
    put(0, n + "Wo", g(n + "Wp"))
    put(0, n + "bq", col(g(n + "bq")))
    put(0, n + "bk", col(g(n + "bk")))
    put(0, n + "bv", rows(g(n + "bv")))
    put(0, n + "bo", rows(g(n + "bp")))
    put(0, n + "temp", rows(g(n + "temperature")))
    rel = np.clip(np.arange(P)[:, None] - np.arange(P)[None, :] + P - 1, 0, g(n + "bias_table").shape[0] - 1)
    bias = g(n + "bias_table")[rel]
    put(0, n + "bias_qk", bias.transpose(0, 2, 1).reshape(P, -1))
    put(0, n + "bias_kq", bias.transpose(1, 2, 0).reshape(P, -1))
    n = "L1_ffn_"
    kv = (np.arange(P) // (4 * D8)) * D8 + np.arange(P) % D8
    swap = np.arange(P) ^ (D8 // 2)
    put(5, n + "Wq", g(n + "Wq"))
    put(5, n + "Wk", g(n + "Wk")[:, kv])
    put(5, n + "Wv", g(n + "Wv")[:, kv])
    put(5, n + "Wq_swapped", g(n + "Wq")[:, swap])
    put(5, n + "Wk_swapped", g(n + "Wk")[:, kv[swap]])
    put(5, n + "Wo", g(n + "Wo"))
    put(5, n + "ln1_w", rows(g(n + "ln1_w")))
    inv = (1.0 / 10000.0 ** (np.arange(0, D8, 2, dtype=np.float32) / np.float32(D8))).astype(np.float32)
    ang = (np.arange(P, dtype=np.float32)[None, :] * inv[np.arange(P) % (D8 // 2)][:, None]).astype(np.float32)
    sign = np.where(np.arange(P) % D8 < D8 // 2, -1.0, 1.0)[:, None]
    cos, sin = np.cos(ang).astype(np.float32), (sign * np.sin(ang)).astype(np.float32)
    put(5, "rope8", np.concatenate([cos, cos, sin, sin], 1))
    n = "L0_ffn_"
    put(2, n + "w1", np.concatenate([g(n + "w1")[:, :DM].T, g(n + "w1")[:, DM:].T], 1))
    put(2, n + "b1", col(g(n + "b1")))
    put(2, n + "w2", g(n + "w2").T)
    put(2, n + "b2", rows(g(n + "b2")))
    put(2, n + "slot_init", g(n + "slot_init"))
    put(2, n + "slot_scale", g(n + "slot_scale"))
    put(2, n + "wih", g(n + "gru_wih").T)
    put(2, n + "whh", g(n + "gru_whh").T)
    put(2, n + "bih", g(n + "gru_bih").reshape(3, P).T)
    put(2, n + "bhh", g(n + "gru_bhh").reshape(3, P).T)
    put(2, n + "wv", g(n + "wv").T)
    put(2, n + "bv", rows(g(n + "bv"))[0:NS])
    put(2, n + "wo", g(n + "wo").T)
    put(2, n + "bo", rows(g(n + "bo")))
    put(2, n + "tau", rows(g(n + "tau")))
    n = "L0_xattn_"
    put(1, n + "Wq", g(n + "Wq"))
    put(1, n + "Wk", g(n + "Wk"))
    put(1, n + "Wv", g(n + "Wv"))
    put(1, n + "W_film", np.concatenate([g(n + "W_film_in"), g(n + "W_film_out")], 1))
    put(1, n + "b_film", rows(np.concatenate([g(n + "b_film_in"), g(n + "b_film_out")])))
    put(1, n + "g_in", rows(g(n + "g_norm_in")))
    put(1, n + "b_in", rows(g(n + "b_norm_in")))
    put(1, n + "g_out", rows(g(n + "g_norm_out")))
    put(1, n + "b_out", rows(g(n + "b_norm_out")))
    put(1, n + "g_ffn", col(g(n + "g_ffn")))
    put(1, n + "b_ffn", col(g(n + "b_ffn")))
    put(1, n + "W1", g(n + "W1"))
    put(1, n + "b1", g(n + "b1").reshape(4, P).T)
    put(1, n + "W2", chunks(g(n + "W2")))
    put(1, n + "b2", rows(g(n + "b2")))
    for w in ("log_dt", "D_skip"):
        put(1, n + w, col(g(n + w)))
    for w in ("A_re", "A_im", "C_re", "C_im"):
        put(1, n + w, g(n + w))
    put(1, n + "gate", rows(g(n + "mod_gate")))
    put(1, n + "flip", np.eye(P, dtype=np.float32)[::-1])
    n = "L1_attn_"
    put(3, n + "Wq", g(n + "Wq").T)
    put(3, n + "Wkv", np.concatenate([g(n + "Wk").T, g(n + "Wv").T], 1))
    put(3, n + "Wo", g(n + "Wo").T)
    put(3, n + "bq", col(g(n + "bq")))
    put(3, n + "bkv", rows(np.concatenate([g(n + "bk"), g(n + "bv")])))
    put(3, n + "bo", col(g(n + "bo")))
    pos = np.arange(NB, dtype=np.float32)[:, None]
    div = np.exp(np.arange(0, DM, 2, dtype=np.float32) * np.float32(-np.log(10000.0) / DM))
    pe = np.zeros((NB, DM), np.float32)
    pe[:, 0::2], pe[:, 1::2] = np.sin(pos * div), np.cos(pos * div)
    put(3, "positions", pe.T)
    blocks = np.kron(np.eye(DM // D16), np.ones((D16, D16))).astype(np.float32)
    put(3, n + "blocks", np.concatenate([blocks, blocks], 1))
    n = "L1_xattn_"
    for w in ("Wq", "Wk", "Wv"):
        put(4, n + w, g(n + w))
    put(4, n + "Wo", chunks(g(n + "Wout")))
    put(4, n + "bo", rows(g(n + "bout")))
    n = "L1_ffn_"
    put(5.5, n + "ln2_w", rows(g(n + "ln2_w")))
    put(5.5, n + "Wr", g(n + "Wr"))
    put(5.5, n + "Wg", g(n + "Wg").transpose(1, 0, 2).reshape(DM, -1))
    put(5.5, n + "Wu", g(n + "Wu").transpose(1, 0, 2).reshape(DM, -1))
    put(5.5, n + "Wd", g(n + "Wd").reshape(NE, 2, P, DM).transpose(2, 0, 1, 3).reshape(P, -1))
    n = "L2_attn_"
    put(6, n + "Wq", g(n + "Wq"))
    put(6, n + "Wkv", np.concatenate([g(n + "Wk"), g(n + "Wv")], 1))
    put(6, n + "Wo", g(n + "Wo"))
    put(6, n + "bq", col(g(n + "bq")))
    put(6, n + "bkv", rows(np.concatenate([g(n + "bk"), g(n + "bv")])))
    put(6, n + "bo", rows(g(n + "bo")))
    put(6, n + "blocks", np.kron(np.eye(H16), np.full((D8, D8), 1.0 / (P * D8))).astype(np.float32))
    n = "L2_ffn_"
    put(8, n + "We", g(n + "We").transpose(2, 0, 1).reshape(DM, -1))
    put(8, n + "be", g(n + "be"))
    put(8, n + "Wg", g(n + "Wg").T)
    put(8, n + "bg", rows(g(n + "bg")))
    n = "L3_ffn_"
    put(11, n + "gate_w", g(n + "gate_w").T)
    put(11, n + "gate_b", rows(g(n + "gate_b")))
    put(11, n + "expert_w", g(n + "expert_w").transpose(2, 0, 1).reshape(DM, -1))
    put(11, n + "expert_b", g(n + "expert_b").T)
    n = "L3_attn_"
    qkv = g(n + "W_qkv").reshape(DM, 3, -1)
    swap = np.arange(qkv.shape[2]) ^ 1
    for i, w in enumerate(("Wq", "Wk", "Wv")):
        put(9, n + w, qkv[:, i])
    put(9, n + "Wq_swapped", qkv[:, 0][:, swap])
    put(9, n + "Wk_swapped", qkv[:, 1][:, swap])
    put(9, n + "Wo", chunks(g(n + "W_out")))
    freq = (1.0 / 10000.0 ** (np.arange(0, D64, 2) / D64)).astype(np.float32)
    ang = (np.arange(P, dtype=np.float32)[None, :] * freq[np.arange(P) % D64 // 2][:, None]).astype(np.float32)
    sign = np.where(np.arange(P) % 2 == 0, -1.0, 1.0)[:, None]
    cos, sin = np.cos(ang).astype(np.float32), (sign * np.sin(ang)).astype(np.float32)
    put(9, "rope64", np.concatenate([cos, cos, sin, sin], 1))
    n = "L2_xattn_"
    for w in ("Wq", "Wk", "Wv", "W1"):
        put(7, n + w, g(n + w))
    put(7, n + "W2", chunks(g(n + "W2")))
    put(7, n + "bq", col(g(n + "bq")))
    put(7, n + "bk", col(g(n + "bk")))
    put(7, n + "b1_0", col(g(n + "b1")[:P]))
    put(7, n + "b1_1", col(g(n + "b1")[P:]))
    put(7, n + "bv", rows(g(n + "bv")))
    put(7, n + "bo", rows(g(n + "b2")))
    n = "L3_xattn_"
    for w in ("Wq", "Wk", "Wv", "Wo"):
        put(10, n + w, g(n + w))
    put(10, n + "bq", col(g(n + "bq")))
    put(10, n + "bk", col(g(n + "bk")))
    put(10, n + "bv", rows(g(n + "bv")))
    put(10, n + "bo", rows(g(n + "bo")))
    return A


class Kernel:

    def __init__(self, nc, ctx, table, pack, x, ctxT, masks, out):
        self.nc, self.ctx = nc, ctx
        self.sig = Signals(nc)
        self.x, self.ctxT_dram, self.masks, self.out = x, ctxT, masks, out
        self.pack_dram = pack
        self.X = self.sb("X", [P, NB, DM], F32)
        self.ctxT = self.sb("ctxT", [DC, NB, P], F32)
        self.place, self.span, o = {}, {}, 0
        for stage, name, r, c in table:
            a, b = self.span.get(stage, (o, o))
            self.span[stage] = (a, o + c)
            self.place[name] = (stage, r, o - a, c)
            o += c
        self.weights = [self.sb(f"weights{i}", [P, max([b - a for s, (a, b) in self.span.items()
                                                        if s != "const" and BUFFER[s] == i] + [1])], F32)
                        for i in range(2)]
        a, b = self.span["const"]
        self.consts = self.sb("consts", [P, b - a], F32)
        self.bank = [ctx.enter_context(nc.psum_tensor(f"bank{i}", [P, 512], F32)) for i in range(8)]
        self.ident_bf = self.sb("ident_bf", [P, P], BF16)
        self.causal = self.sb("causal", [P, 2, 4, P], BF16)
        self.head_row = self.sb("head_row", [P, H16, P], BF16)
        self.neg_half = self.sb("neg_half", [P, 2], F32)
        self.eps = self.sb("eps", [P, 2], F32)
        self.carry = self.sb("carry", [P, 4], F32)
        self.loaded = {s: ctx.enter_context(nc.semaphore(f"weights_loaded{s}")) for s in self.span}
        self.x_loaded = ctx.enter_context(nc.semaphore("x_loaded"))
        self.ctx_loaded = ctx.enter_context(nc.semaphore("ctx_loaded"))
        self.const_ready = ctx.enter_context(nc.semaphore("const_ready"))
        self.cleared = ctx.enter_context(nc.semaphore("head_row_cleared"))
        self.stored = ctx.enter_context(nc.semaphore("stored"))

    def sb(self, name, shape, dt):
        return self.ctx.enter_context(self.nc.sbuf_tensor(name, shape, dt))

    def w(self, name):
        stage, r, o, c = self.place[name]
        tile = self.consts if stage == "const" else self.weights[BUFFER[stage]]
        return tile[0:r, o:o + c]

    def load_weights(self, eng, stage):
        if stage in self.span:
            a, b = self.span[stage]
            tile = self.consts if stage == "const" else self.weights[BUFFER[stage]]
            eng.dma_start(tile[:, 0:b - a], self.pack_dram[:, a:b]).then_inc(self.loaded[stage], 16)

    def next_stage(self, stage):
        later = [s for s in ORDER if s > stage and (s in STAGES or s == 5.5 and 5 in STAGES)]
        return later[0] if later else None


def load_stage(k):
    nc = k.nc
    with nc.Block() as block:

        @block.sync
        def _(sp):
            k.load_weights(sp, "const")
            k.load_weights(sp, STAGES[0])
            sp.dma_start(k.X[:], k.x.rearrange("b t d -> t b d")).then_inc(k.x_loaded, 16)
            sp.dma_start(k.ctxT[:], k.ctxT_dram).then_inc(k.ctx_loaded, 16)

        @block.gpsimd
        def _(pool):
            nc.gpsimd.memset(k.neg_half[:], -0.5)
            nc.gpsimd.memset(k.eps[:], EPS)
            nc.gpsimd.memset(k.carry[:], 0.0)
            nc.gpsimd.memset(k.head_row[:], 0.0).then_inc(k.cleared, 1)
        @block.vector
        def _(dve):
            dve.wait_ge(k.cleared, 1)
            dve.wait_ge(k.loaded["const"], 16)
            nc.vector.tensor_copy(k.ident_bf[:], k.w("ident")).then_inc(k.const_ready, 1)
            dve.wait_ge(k.const_ready, 1)
            for b0 in (0, D64):
                last = nc.vector.tensor_copy(
                    k.head_row[b0:b0 + H16, :, :],
                    k.ident_bf[b0:b0 + H16, b0:b0 + H16].unsqueeze(2).to_broadcast([H16, H16, P]))
            last.then_inc(k.const_ready, 1)
            for i in range(2):
                last = nc.vector.tensor_copy(
                    k.causal[:, i], k.w("causal")[:, P * i:P * i + P].unsqueeze(1).to_broadcast([P, 4, P]))
            last.then_inc(k.const_ready, 1)
            dve.wait_ge(k.const_ready, 3)
            dve.wait_ge(k.x_loaded, 16)


def store_stage(k):
    with k.nc.Block() as block:

        @block.sync
        def _(sp):
            sp.dma_start(k.out.rearrange("b t d -> t b d"), k.X[:]).then_inc(k.stored, 16)
            sp.wait_ge(k.stored, 16)


def rms_root(k, pool, ms, s, t, mean_square, plus_eps, root):
    pool.wait_ge(mean_square[s].sem, mean_square[s].at(t, 1))
    k.nc.gpsimd.tensor_tensor(ms[:, s, 1:2], ms[:, s, 0:1], k.eps[:, 0:1], ALU.add).then_inc(plus_eps[s].sem, 1)
    pool.wait_ge(plus_eps[s].sem, plus_eps[s].at(t, 1))
    k.nc.gpsimd.tensor_tensor(ms[:, s, 2:3], ms[:, s, 1:2], k.neg_half[:, 0:1],
                              ALU.pow).then_inc(root[s].sem, 1)


class Tail:

    def __init__(self, k, ctx, name, steps=STEPS):
        sig = k.sig
        self.k, self.nc = k, k.nc
        self.r = ctx.enter_context(k.nc.sbuf_tensor(name + "r", [P, 2, DM], F32))
        self.st = ctx.enter_context(k.nc.sbuf_tensor(name + "st", [P, 2, 6], F32))
        self.mv = ctx.enter_context(k.nc.sbuf_tensor(name + "mv", [P, 2, 2], F32))
        self.rs = ctx.enter_context(k.nc.sbuf_tensor(name + "rstd", [P, 2, 2], F32))
        self.summed = sig.pair("summed", 1, steps)
        self.halves = sig.pair("ln_halves", 1, steps)
        self.moments = sig.pair("ln_moments", 1, steps)
        self.var_eps = sig.pair("ln_var_eps", 1, steps)
        self.rstd_sb = sig.pair("ln_rstd", 1, steps)
        self.written = sig.pair("x_written", 1, steps)

    def stats(self, dve, t, s):
        nc = self.nc
        dve.wait_ge(self.summed[s].sem, self.summed[s].at(t, 1))
        nc.vector.bn_stats(self.st[:, s, :], self.r[:, s, :]).then_inc(self.halves[s].sem, 1)
        dve.wait_ge(self.halves[s].sem, self.halves[s].at(t, 1))
        nc.vector.tensor_copy(self.k.carry[:, 1:2], self.k.carry[:, 0:1])
        nc.vector.bn_aggr(self.mv[:, s, :], self.st[:, s, :]).then_inc(self.moments[s].sem, 1)

    def rstd(self, pool, t, s):
        nc = self.nc
        pool.wait_ge(self.moments[s].sem, self.moments[s].at(t, 1))
        nc.gpsimd.tensor_tensor(self.rs[:, s, 0:1], self.mv[:, s, 1:2], self.k.eps[:, 0:1],
                                ALU.add).then_inc(self.var_eps[s].sem, 1)
        pool.wait_ge(self.var_eps[s].sem, self.var_eps[s].at(t, 1))
        nc.gpsimd.tensor_tensor(self.rs[:, s, 1:2], self.rs[:, s, 0:1], self.k.neg_half[:, 0:1],
                                ALU.pow).then_inc(self.rstd_sb[s].sem, 1)

    def apply(self, dve, t, s):
        nc = self.nc
        dve.wait_ge(self.rstd_sb[s].sem, self.rstd_sb[s].at(t, 1))
        nc.vector.tensor_scalar(self.k.X[:, 2 * t + s, :], self.r[:, s, :], self.mv[:, s, 0:1],
                                self.rs[:, s, 1:2], ALU.subtract, ALU.mult).then_inc(self.written[s].sem, 1)


def attention8(k, stage, name, cross=False, bias=False, mlp=False, grouped=None, scale=D8 ** -0.5):
    k.sig.new_stage(name)
    nc, sig = k.nc, k.sig
    with ExitStack() as ctx:
        def sb(what, shape, dt=F32):
            return ctx.enter_context(nc.sbuf_tensor(f"{name}_{what}", shape, dt))

        xs = sb("xs", [P, 2, DM])
        cs = sb("cs", [DC, 2, P])
        xT = sb("xT", [P, 2, P])
        qk = sb("qk", [P, 2, 2, P])
        qT, kT = qk[:, :, 0, :], qk[:, :, 1, :]
        if grouped is not None:
            turned = sb("turned", [P, 2, 4, P])
            xn = sb("xn", [P, 2, DM])
            ms = sb("ms", [P, 2, 4])
            rms_in = sig.pair("rms_in")
            rms_eps = sig.pair("rms_eps")
            rms_rs = sig.pair("rms_rs")
            xn_sb = sig.pair("xn_sb")
            turned_sb = sig.pair("turned_sb")
        if mlp:
            hid = sb("hid", [P, 2, 2, P])
            hid_ps = sig.pair("hid_ps")
            hid_sb = sig.pair("hid_sb")
        qTm = sb("qTm", [P, 2, H16, P])
        q16 = sb("q16", [P, 2, P], BF16)
        k16m = sb("k16m", [P, 2, H16, P], BF16)
        if bias:
            bias16 = sb("bias16", [P, H16 * P], BF16)
        v1 = sb("v1", [P, 2, H16, D8 + 1])
        nm = sb("nm", [P, 2, H16], BF16)
        nmT = sb("nmT", [P, 2, P], BF16)
        pT = sb("pT", [P, 2, H16, P])
        rs = sb("rs", [P, 2, H16])
        o = sb("o", [P, 2, DM])
        oT = sb("oT", [P, 2, P])
        xb = sb("xb", [P, 2, DM])
        tail = Tail(k, ctx, name)
        r, r_sb, x_out = tail.r, tail.summed, tail.written
        sc = sb("sc", [P, 4])
        sq = sb("sq", [P, 2, DM]) if grouped is not None else None

        A, B, C, O = k.bank[0], k.bank[1], k.bank[2], k.bank[3]
        ring = k.bank[4:8]
        turned_o = [A[:, 0:P], O[:, 3 * P:4 * P]]
        y_bank = [C, O]
        ident = k.w("ident")
        added = bias or grouped is not None

        src_x = xs if grouped is None else xn
        src_ready = staged = sig.pair("staged")
        if grouped is not None:
            src_ready = xn_sb
        xT_ps = sig.pair("xT_ps")
        xT_sb = sig.pair("xT_sb")
        qk_ps = sig.pair("qk_ps")
        v_ps = sig.pair("v_ps")
        q_sb = sig.pair("q_sb")
        k_sb = sig.pair("k_sb")
        v_sb = sig.pair("v_sb")
        qm_sb = sig.pair("qm_sb")
        km16_sb = sig.pair("km16_sb")
        bias16_sb = sig.one("bias16_sb", 1, 1)
        filled = sig.ring("scores_in_bank", 4, 4)
        max_read = sig.ring("max_read", 4, 2)
        nmT_ps = sig.pair("nmT_ps")
        nmT_sb = sig.pair("nmT_sb")
        p_sb = sig.pair("p_sb", 4)
        biased_sb = sig.pair("biased_sb", 4)
        drained = biased_sb if bias else p_sb
        o_ps = sig.pair("o_ps")
        o_sb = sig.pair("o_sb")
        oT_ps = sig.pair("oT_ps")
        oT_sb = sig.pair("oT_sb")
        y_ps = sig.pair("y_ps")
        xb_sb = sig.pair("xb_sb")
        rs_sb = sig.pair("rs_sb")
        const = sig.one("stage_const", 4, 1)

        with nc.Block() as block:

            @block.sync
            def _(sp):
                k.load_weights(sp, k.next_stage(stage))

            @block.gpsimd
            def _(pool):
                def stage_in(t):
                    for s in range(2):
                        pool.wait_ge(xT_ps[s].sem, xT_ps[s].at(t, 0))
                        if grouped is not None:
                            pool.wait_ge(xn_sb[s].sem, xn_sb[s].at(t, 0))
                        else:
                            pool.wait_ge(xb_sb[s].sem, xb_sb[s].at(t, 0))
                        if cross:
                            pool.wait_ge(v_ps[s].sem, v_ps[s].at(t, 0))
                            nc.gpsimd.tensor_copy(cs[:, s, :], k.ctxT[:, 2 * t + s, :])
                        nc.gpsimd.tensor_copy(xs[:, s, :], k.X[:, 2 * t + s, :]).then_inc(staged[s].sem, 1)

                def spread_queries(t):
                    for s in range(2):
                        if grouped is not None:
                            rms_root(k, pool, ms, s, t, rms_in, rms_eps, rms_rs)
                    for s in range(2):
                        if grouped is not None:
                            pool.wait_ge(turned_sb[s].sem, turned_sb[s].at(t, 1))
                            pool.wait_ge(p_sb[s].sem, p_sb[s].at(t, 0))
                            nc.gpsimd.tensor_tensor(qk[:, s], turned[:, s, 0:2, :], turned[:, s, 2:4, :],
                                                    ALU.add).then_inc(k_sb[s].sem, 1)
                        q_ready = q_sb if grouped is None else k_sb
                        pool.wait_ge(q_ready[s].sem, q_ready[s].at(t, 1))
                        pool.wait_ge(p_sb[s].sem, p_sb[s].at(t, 0))
                        nc.gpsimd.tensor_tensor(
                            qTm[:, s], qT[:, s, :].unsqueeze(1).to_broadcast([P, H16, P]),
                            k.w("head_mask").unsqueeze(2).to_broadcast([P, H16, P]),
                            ALU.mult).then_inc(qm_sb[s].sem, 1)

                def residual(t):
                    for s in range(2):
                        if grouped is None:
                            pool.wait_ge(r_sb[s].sem, r_sb[s].at(t, 0))
                            pool.wait_ge(staged[s].sem, staged[s].at(t, 1))
                            nc.gpsimd.tensor_tensor(xb[:, s, :], xs[:, s, :], k.w(name + "bo"),
                                                    ALU.add).then_inc(xb_sb[s].sem, 1)

                def roots(t):
                    for s in range(2):
                        if grouped is None:
                            tail.rstd(pool, t, s)

                nc.gpsimd.memset(nmT[:], 0.0)
                nc.gpsimd.memset(v1[:], 1.0).then_inc(const.sem, 1)
                pool.wait_ge(k.loaded[stage], 16)
                if cross:
                    pool.wait_ge(k.ctx_loaded, 16)
                stage_in(0)
                spread_queries(0)
                residual(0)
                with pool.Fori(0, STEPS - 1) as t:
                    stage_in(t + 1)
                    spread_queries(t + 1)
                    roots(t)
                    residual(t + 1)
                roots(STEPS - 1)

            @block.scalar
            def _(act):
                def mean_squares(t):
                    for s in range(2):
                        if grouped is not None:
                            act.wait_ge(staged[s].sem, staged[s].at(t, 1))
                            nc.scalar.activation(sq[:, s, :], xs[:, s, :], ACT.Square, scale=DM ** -0.5,
                                                 accum_out=ms[:, s, 0:1]).then_inc(rms_in[s].sem, 1)

                def projected(t):
                    for s in range(2):
                        act.wait_ge(xT_ps[s].sem, xT_ps[s].at(t, 1))
                        nc.scalar.activation(xT[:, s, :], A[:, 0:P], ACT.Copy).then_inc(xT_sb[s].sem, 1)
                        if grouped is not None:
                            continue
                        act.wait_ge(qk_ps[s].sem, qk_ps[s].at(t, 1))
                        act.wait_ge(qm_sb[s].sem, qm_sb[s].at(t, 0))
                        act.wait_ge(km16_sb[s].sem, km16_sb[s].at(t, 0))
                        nc.scalar.activation(qT[:, s, :], B[:, 0:P], ACT.Identity,
                                             bias=k.w(name + "bq")).then_inc(q_sb[s].sem, 1)
                        nc.scalar.activation(kT[:, s, :], B[:, P:2 * P], ACT.Identity,
                                             bias=k.w(name + "bk")).then_inc(k_sb[s].sem, 1)

                def exponentials(t):
                    for s in range(2):
                        act.wait_ge(nmT_ps[s].sem, nmT_ps[s].at(t, 1))
                        nc.scalar.activation(nmT[0:H16, s, :], A[0:H16, 0:P // 2].bitcast(BF16),
                                             ACT.Copy).then_inc(nmT_sb[s].sem, 1)
                        for j in range(4):
                            unit = pT[:, s, 4 * j:4 * j + 4, :].rearrange("p h q -> p (h q)")
                            if bias:
                                act.wait_ge(biased_sb[s].sem, biased_sb[s].at(t, j + 1))
                                nc.scalar.activation(unit, unit, ACT.Exp, scale=sc[:, 1:2]).then_inc(p_sb[s].sem, 1)
                                continue
                            if j == 0:
                                act.wait_ge(o_ps[s].sem, o_ps[s].at(t, 0))
                            act.wait_ge(filled[j].sem, filled[j].at(t, 3 + s))
                            nc.scalar.activation(unit, ring[j][:], ACT.Exp, scale=scale).then_inc(p_sb[s].sem, 1)

                def outputs(t):
                    for s in range(2):
                        act.wait_ge(oT_ps[s].sem, oT_ps[s].at(t, 1))
                        nc.scalar.activation(oT[:, s, :], turned_o[s], ACT.Copy).then_inc(oT_sb[s].sem, 1)
                        if mlp:
                            act.wait_ge(hid_ps[s].sem, hid_ps[s].at(t, 1))
                            for c in range(2):
                                last = nc.scalar.activation(hid[:, s, c, :], B[:, P * c:P * c + P], ACT.Relu,
                                                            bias=k.w(f"{name}b1_{c}"))
                            last.then_inc(hid_sb[s].sem, 1)

                act.wait_ge(k.loaded[stage], 16)
                if bias:
                    act.wait_ge(const.sem, const.base + 4)
                    nc.scalar.activation(bias16[:], k.w(name + "bias_qk"), ACT.Copy).then_inc(bias16_sb.sem, 1)
                mean_squares(0)
                projected(0)
                with act.Fori(0, STEPS - 1) as t:
                    mean_squares(t + 1)
                    exponentials(t)
                    projected(t + 1)
                    outputs(t)
                exponentials(STEPS - 1)
                outputs(STEPS - 1)

            @block.vector
            def _(dve):
                def spread_keys(t):
                    for s in range(2):
                        if grouped is not None:
                            dve.wait_ge(rms_rs[s].sem, rms_rs[s].at(t, 1))
                            dve.wait_ge(xT_ps[s].sem, xT_ps[s].at(t, 0))
                            nc.vector.scalar_tensor_tensor(
                                out=xn[:, s, :], in0=xs[:, s, :], scalar=ms[:, s, 2:3], in1=k.w(name + "ln1_w"),
                                op0=ALU.mult, op1=ALU.mult).then_inc(xn_sb[s].sem, 1)
                    for s in range(2):
                        if grouped is not None:
                            dve.wait_ge(qk_ps[s].sem, qk_ps[s].at(t, 1))
                            dve.wait_ge(k_sb[s].sem, k_sb[s].at(t, 0))
                            nc.vector.tensor_tensor(turned[:, s].rearrange("p a q -> p (a q)"), B[:],
                                                    k.w("rope8"), ALU.mult).then_inc(turned_sb[s].sem, 1)
                    for s in range(2):
                        dve.wait_ge(max_read[3].sem, max_read[3].at(t, 0))
                        if grouped is None:
                            dve.wait_ge(q_sb[s].sem, q_sb[s].at(t, 1))
                        dve.wait_ge(k_sb[s].sem, k_sb[s].at(t, 1))
                        nc.vector.tensor_copy(q16[:, s, :], qT[:, s, :])
                        nc.vector.tensor_tensor(
                            k16m[:, s], kT[:, s, :].unsqueeze(1).to_broadcast([P, H16, P]),
                            k.w("head_mask").unsqueeze(2).to_broadcast([P, H16, P]),
                            ALU.mult).then_inc(km16_sb[s].sem, 1)

                def values(t):
                    dve.wait_ge(v_ps[1].sem, v_ps[1].at(t, 1))
                    for s in range(2):
                        dve.wait_ge(v_ps[s].sem, v_ps[s].at(t, 1))
                        dve.wait_ge(o_ps[s].sem, o_ps[s].at(t, 0))
                        v = C[:, P * s:P * s + P].rearrange("p (h d) -> p h d", d=D8)
                        if grouped is not None:
                            nc.vector.tensor_copy(v1[:, s, :, 0:D8], v).then_inc(v_sb[s].sem, 1)
                        else:
                            nc.vector.tensor_tensor(v1[:, s, :, 0:D8], v,
                                                    k.w(name + "bv").rearrange("p (h d) -> p h d", d=D8),
                                                    ALU.add).then_inc(v_sb[s].sem, 1)

                def maxima(t):
                    for s in range(2):
                        for j in range(4):
                            dve.wait_ge(filled[j].sem, filled[j].at(t, 1 + s))
                            if j == 0:
                                dve.wait_ge(nmT_ps[s].sem, nmT_ps[s].at(t, 0))
                            nc.vector.tensor_reduce(
                                nm[:, s, 4 * j:4 * j + 4], ring[j][:].rearrange("p (h q) -> p h q", q=P),
                                AX.X, ALU.max, negate=True).then_inc(max_read[j].sem, 1)

                def biased(t):
                    for s in range(2 if bias else 0):
                        dve.wait_ge(o_ps[s].sem, o_ps[s].at(t, 0))
                        for j in range(4):
                            dve.wait_ge(filled[j].sem, filled[j].at(t, 3 + s))
                            nc.vector.tensor_tensor(
                                pT[:, s, 4 * j:4 * j + 4, :].rearrange("p h q -> p (h q)"), ring[j][:],
                                k.w(name + "bias_kq")[:, 512 * j:512 * j + 512], ALU.add).then_inc(biased_sb[s].sem, 1)

                def normalised(t):
                    for s in range(2):
                        dve.wait_ge(o_ps[s].sem, o_ps[s].at(t, 1))
                        ov = O[:, 0:H16 * (D8 + 1)].rearrange("p (h d) -> p h d", d=D8 + 1)
                        nc.vector.reciprocal(rs[:, s, :], ov[:, :, D8]).then_inc(rs_sb[s].sem, 1)
                        dve.wait_ge(rs_sb[s].sem, rs_sb[s].at(t, 1))
                        dve.wait_ge(oT_ps[s].sem, oT_ps[s].at(t, 0))
                        nc.vector.tensor_tensor(
                            o[:, s, :].rearrange("p (h d) -> p h d", d=D8), ov[:, :, 0:D8],
                            rs[:, s, :].unsqueeze(2).to_broadcast([P, H16, D8]), ALU.mult).then_inc(o_sb[s].sem, 1)

                def summed(t):
                    for s in range(2):
                        dve.wait_ge(y_ps[s].sem, y_ps[s].at(t, 1))
                        dve.wait_ge(x_out[s].sem, x_out[s].at(t, 0))
                        if grouped is None:
                            dve.wait_ge(xb_sb[s].sem, xb_sb[s].at(t, 1))
                        x_now = xb[:, s, :] if grouped is None else k.X[:, 2 * t + s, :]
                        nc.vector.tensor_tensor(r[:, s, :], y_bank[s][:, 2 * P:3 * P], x_now, ALU.add).then_inc(r_sb[s].sem, 1)
                        if grouped is not None:
                            dve.wait_ge(r_sb[s].sem, r_sb[s].at(t, 1))
                            nc.vector.tensor_scalar(grouped[:, 2 * t + s, :], r[:, s, :], -100.0, 100.0, ALU.max,
                                                    ALU.min).then_inc(x_out[s].sem, 1)
                            continue
                        tail.stats(dve, t, s)
                    for s in range(2):
                        if grouped is None:
                            tail.apply(dve, t, s)

                dve.wait_ge(k.loaded[stage], 16)
                dve.wait_ge(const.sem, const.base + 1)
                if bias:
                    nc.vector.tensor_scalar(sc[:, 0:1], k.w(name + "temp"), 0.1, 10.0, ALU.max,
                                            ALU.min).then_inc(const.sem, 1)
                    dve.wait_ge(const.sem, const.base + 2)
                    nc.vector.tensor_scalar(sc[:, 2:3], sc[:, 0:1], float(np.float32(np.sqrt(DM))), None,
                                            ALU.mult).then_inc(const.sem, 1)
                    dve.wait_ge(const.sem, const.base + 3)
                    nc.vector.reciprocal(sc[:, 1:2], sc[:, 2:3]).then_inc(const.sem, 1)
                spread_keys(0)
                values(0)
                maxima(0)
                with dve.Fori(0, STEPS - 1) as t:
                    biased(t)
                    spread_keys(t + 1)
                    normalised(t)
                    values(t + 1)
                    maxima(t + 1)
                    summed(t)
                biased(STEPS - 1)
                normalised(STEPS - 1)
                summed(STEPS - 1)

            @block.tensor
            def _(pe):
                def project(t, before):
                    for s in range(2):
                        pe.wait_ge(src_ready[s].sem, src_ready[s].at(t, 1))
                        if s == 1:
                            pe.wait_ge(xT_sb[0].sem, xT_sb[0].at(t, 1))
                        elif before is not None:
                            pe.wait_ge(nmT_sb[1].sem, nmT_sb[1].at(before, 1))
                        nc.tensor.transpose(A[:, 0:P], src_x[:, s, :], ident).then_inc(xT_ps[s].sem, 1)
                        pe.wait_ge(xT_sb[s].sem, xT_sb[s].at(t, 1))
                        if mlp and s == 0 and before is not None:
                            pe.wait_ge(hid_sb[1].sem, hid_sb[1].at(before, 0))
                        b_read = k_sb if grouped is None else turned_sb
                        if s == 0:
                            pe.wait_ge(b_read[1].sem, b_read[1].at(t, 0))
                        else:
                            pe.wait_ge(b_read[0].sem, b_read[0].at(t, 1))
                        src = cs[:, s, :] if cross else xT[:, s, :]
                        nc.tensor.matmul(B[:, 0:P], k.w(name + "Wq"), xT[:, s, :], start=True, stop=True)
                        if grouped is not None:
                            nc.tensor.matmul(B[:, 2 * P:3 * P], k.w(name + "Wq_swapped"), src, start=True, stop=True)
                            nc.tensor.matmul(B[:, 3 * P:4 * P], k.w(name + "Wk_swapped"), src, start=True, stop=True)
                        nc.tensor.matmul(B[:, P:2 * P], k.w(name + "Wk"), src, start=True,
                                         stop=True).then_inc(qk_ps[s].sem, 1)
                        if s == 0 and before is not None:
                            pe.wait_ge(r_sb[0].sem, r_sb[0].at(before, 0))
                        nc.tensor.matmul(C[:, P * s:P * s + P], src, k.w(name + "Wv"), start=True,
                                         stop=True).then_inc(v_ps[s].sem, 1)

                def score_roughly(t, slots):
                    for s in slots:
                        pe.wait_ge(km16_sb[s].sem, km16_sb[s].at(t, 1))
                        for j in range(4):
                            if s == 0:
                                pe.wait_ge(drained[1].sem, drained[1].at(t, 0))
                            else:
                                pe.wait_ge(max_read[j].sem, max_read[j].at(t, 1))
                            if bias:
                                nc.tensor.matmul(ring[j][:], k.ident_bf[:], bias16[:, 512 * j:512 * j + 512],
                                                 start=True, stop=False)
                            if grouped is not None:
                                nc.tensor.matmul(ring[j][:], k.ident_bf[:], k.causal[:, 0].rearrange("p h q -> p (h q)"),
                                                 start=True, stop=False)
                            nc.tensor.matmul(ring[j][:], q16[:, s, :],
                                             k16m[:, s, 4 * j:4 * j + 4, :].rearrange("p h q -> p (h q)"),
                                             start=not added, stop=True).then_inc(filled[j].sem, 1)
                def score(t):
                    for s in range(2):
                        pe.wait_ge(max_read[3].sem, max_read[3].at(t, 1 + s))
                        if s == 1:
                            pe.wait_ge(nmT_sb[0].sem, nmT_sb[0].at(t, 1))
                        else:
                            pe.wait_ge(oT_sb[0].sem, oT_sb[0].at(t, 0))
                            pe.wait_ge(xT_sb[1].sem, xT_sb[1].at(t, 1))
                        nc.tensor.transpose(A[0:H16, 0:P // 2].bitcast(BF16), nm[:, s, :],
                                            k.ident_bf[:]).then_inc(nmT_ps[s].sem, 1)
                        pe.wait_ge(nmT_sb[s].sem, nmT_sb[s].at(t, 1))
                        pe.wait_ge(qm_sb[s].sem, qm_sb[s].at(t, 1))
                        for j in range(4):
                            if s == 0:
                                pe.wait_ge(max_read[j].sem, max_read[j].at(t, 2))
                            else:
                                pe.wait_ge(drained[0].sem, drained[0].at(t, j + 1))
                            if grouped is not None:
                                nc.tensor.matmul(ring[j][:], k.ident_bf[:], k.causal[:, 1].rearrange("p h q -> p (h q)"),
                                                 start=True, stop=False, skip_group_check=True)
                            nc.tensor.matmul(ring[j][:], kT[:, s, :],
                                             qTm[:, s, 4 * j:4 * j + 4, :].rearrange("p h q -> p (h q)"),
                                             start=grouped is None, stop=False, skip_group_check=True)
                            for i in range(4):
                                last = nc.tensor.matmul(ring[j][:, P * i:P * i + P], k.head_row[:, 4 * j + i, :],
                                                        nmT[:, s, :], start=False, stop=True, skip_group_check=True)
                            last.then_inc(filled[j].sem, 1)

                def weigh(t):
                    for s in range(2):
                        pe.wait_ge(p_sb[s].sem, p_sb[s].at(t, 4))
                        pe.wait_ge(v_sb[s].sem, v_sb[s].at(t, 1))
                        if s == 0:
                            pe.wait_ge(r_sb[1].sem, r_sb[1].at(t, 0))
                        else:
                            pe.wait_ge(o_sb[0].sem, o_sb[0].at(t, 1))
                        for h in range(H16):
                            last = nc.tensor.matmul(O[:, h * (D8 + 1):(h + 1) * (D8 + 1)], pT[:, s, h, :],
                                                    v1[:, s, h, :], start=True, stop=True)
                        last.then_inc(o_ps[s].sem, 1)

                def project_out(t, after):
                    for s in range(2):
                        pe.wait_ge(o_sb[s].sem, o_sb[s].at(t, 1))
                        if s == 0 and after is not None:
                            pe.wait_ge(xT_sb[1].sem, xT_sb[1].at(after, 1))
                        elif s == 0:
                            pe.wait_ge(nmT_sb[1].sem, nmT_sb[1].at(t, 1))
                        nc.tensor.transpose(turned_o[s], o[:, s, :], ident).then_inc(oT_ps[s].sem, 1)
                    for s in range(2):
                        pe.wait_ge(oT_sb[s].sem, oT_sb[s].at(t, 1))
                        if s == 0 and after is not None:
                            pe.wait_ge(v_sb[1].sem, v_sb[1].at(after, 1))
                        if not mlp:
                            nc.tensor.matmul(y_bank[s][:, 2 * P:3 * P], oT[:, s, :], k.w(name + "Wo"), start=True,
                                             stop=True).then_inc(y_ps[s].sem, 1)
                            continue
                        if s == 1:
                            pe.wait_ge(hid_sb[0].sem, hid_sb[0].at(t, 1))
                        elif after is not None:
                            pe.wait_ge(k_sb[1].sem, k_sb[1].at(after, 1))
                        for c in range(2):
                            last = nc.tensor.matmul(B[:, P * c:P * c + P], k.w(name + "W1")[:, P * c:P * c + P],
                                                    oT[:, s, :], start=True, stop=True)
                        last.then_inc(hid_ps[s].sem, 1)
                        pe.wait_ge(hid_sb[s].sem, hid_sb[s].at(t, 1))
                        for c in range(2):
                            last = nc.tensor.matmul(y_bank[s][:, 2 * P:3 * P], hid[:, s, c, :],
                                                    k.w(name + "W2")[:, P * c:P * c + P], start=c == 0, stop=c == 1)
                        last.then_inc(y_ps[s].sem, 1)

                pe.wait_ge(k.loaded[stage], 16)
                if bias:
                    pe.wait_ge(bias16_sb.sem, bias16_sb.base + 1)
                if cross:
                    pe.wait_ge(k.ctx_loaded, 16)
                project(0, None)
                score_roughly(0, range(2))
                with pe.Fori(0, STEPS - 1) as t:
                    score(t)
                    project(t + 1, t)
                    weigh(t)
                    score_roughly(t + 1, [0])
                    project_out(t, t + 1)
                    score_roughly(t + 1, [1])
                score(STEPS - 1)
                weigh(STEPS - 1)
                project_out(STEPS - 1, None)


def attention64(k, stage, name, heads, cross=False, rope=False, scale=D64 ** -0.5):
    k.sig.new_stage(name)
    nc, sig = k.nc, k.sig
    C2 = heads // 2
    UN = heads // 4
    VN = heads * D64 // 512
    W1 = D64 + 1
    QK = 2 * C2 if rope else C2
    ANY = QK + 2 * VN + 2
    with ExitStack() as ctx:
        def sb(what, shape, dt=F32):
            return ctx.enter_context(nc.sbuf_tensor(f"{name}_{what}", shape, dt))

        xs = sb("xs", [P, 2, DM])
        cs = sb("cs", [DC, 2, P])
        xT = sb("xT", [P, 2, P])
        qk = sb("qk", [P, 2, C2, 2, P])
        qk16 = sb("qk16", [P, 2, C2, 2, P], BF16) if rope else qk
        turned = sb("turned", [P, 2, 2, 2 * P]) if rope else None
        v1 = sb("v1", [P, 2, heads, W1])
        nm = sb("nm", [P, 2, P], BF16)
        nmT = sb("nmT", [P, 2, P], BF16)
        pT = sb("pT", [P, heads, P])
        rs = sb("rs", [P, 2, UN, 4])
        o = sb("o", [P, heads, D64])
        oT = sb("oT", [P, C2, P])
        xb = sb("xb", [P, 2, DM])
        tail = Tail(k, ctx, name)

        A, proj = k.bank[0], k.bank[1:3]
        ring = k.bank[4:8]
        ident = k.w("ident")
        src = cs if cross else xT

        staged = sig.pair("staged")
        xT_ps = sig.pair("xT_ps")
        xT_sb = sig.pair("xT_sb")
        proj_ps = sig.ring("proj_ps", 2, ANY // 2)
        proj_read = sig.ring("proj_read", 2, (ANY - 2 - (QK if rope else 0)) // 2)
        turned_sb = sig.one("turned_units", QK, STEPS)
        qk_sb = sig.one("qk_units", QK, STEPS)
        qk16_sb = sig.one("qk16_sb", 2, STEPS)
        filled = sig.ring("scores_in_bank", UN, 4)
        max_read = sig.ring("max_read", UN, 2)
        nm_sb = sig.pair("nm_both")
        nmT_ps = sig.pair("nmT_ps")
        nmT_sb = sig.pair("nmT_sb")
        p_sb = sig.pair("p_sb", UN)
        o_ps = sig.pair("o_units_ps", UN)
        rs_sb = sig.pair("rs_units", UN)
        o_sb = sig.pair("o_units", UN)
        oT_ps = sig.pair("oT_banks_ps", C2 // 4)
        oT_sb = sig.pair("oT_banks", C2 // 4)
        xb_sb = sig.pair("xb_sb")
        const = sig.one("stage_const", 1, 1)

        def unit_heads(j):
            return [8 * (j // 2) + 2 * i + j % 2 for i in range(4)]

        with nc.Block() as block:

            @block.sync
            def _(sp):
                k.load_weights(sp, k.next_stage(stage))

            @block.gpsimd
            def _(pool):
                nc.gpsimd.memset(nm[:], 0.0)
                nc.gpsimd.memset(v1[:], 1.0).then_inc(const.sem, 1)
                pool.wait_ge(k.loaded[stage], 16)
                pool.wait_ge(k.ctx_loaded, 16)
                def stage_in(t):
                    for s in range(2):
                        pool.wait_ge(xT_ps[s].sem, xT_ps[s].at(t, 0))
                        if cross:
                            pool.wait_ge(nmT_ps[s].sem, nmT_ps[s].at(t, 0))
                            pool.wait_ge(xb_sb[s].sem, xb_sb[s].at(t, 0))
                            nc.gpsimd.tensor_copy(cs[:, s, :], k.ctxT[:, 2 * t + s, :])
                        nc.gpsimd.tensor_copy(xs[:, s, :], k.X[:, 2 * t + s, :]).then_inc(staged[s].sem, 1)

                def add_turned(t):
                    for u in range(QK if rope else 0):
                        if u == 0:
                            pool.wait_ge(p_sb[1].sem, p_sb[1].at(t, 0))
                        pool.wait_ge(turned_sb.sem, turned_sb.at(t, u + 1))
                        nc.gpsimd.tensor_tensor(qk[:, u // C2, u % C2].rearrange("p s q -> p (s q)"),
                                                turned[:, u % 2, 0, :], turned[:, u % 2, 1, :],
                                                ALU.add).then_inc(qk_sb.sem, 1)
                    for s in range(2):
                        if not rope:
                            pool.wait_ge(tail.summed[s].sem, tail.summed[s].at(t, 0))
                            pool.wait_ge(staged[s].sem, staged[s].at(t, 1))
                            nc.gpsimd.tensor_tensor(xb[:, s, :], xs[:, s, :], k.w(name + "bo"),
                                                    ALU.add).then_inc(xb_sb[s].sem, 1)

                stage_in(0)
                with pool.Fori(0, STEPS - 1) as t:
                    add_turned(t)
                    stage_in(t + 1)
                    for s in range(2):
                        tail.rstd(pool, t, s)
                add_turned(STEPS - 1)
                for s in range(2):
                    tail.rstd(pool, STEPS - 1, s)

            @block.scalar
            def _(act):
                act.wait_ge(k.loaded[stage], 16)
                act.wait_ge(const.sem, const.base + 1)
                with act.Fori(0, STEPS) as t:
                    for s in range(2):
                        act.wait_ge(xT_ps[s].sem, xT_ps[s].at(t, 1))
                        nc.scalar.activation(xT[:, s, :], A[:, 0:P], ACT.Copy).then_inc(xT_sb[s].sem, 1)
                    for u in range(0 if rope else QK):
                        act.wait_ge(proj_ps[u % 2].sem, proj_ps[u % 2].at(t, u // 2 + 1))
                        nc.scalar.activation(qk[:, u // (C2 // 2), 2 * (u % (C2 // 2)):2 * (u % (C2 // 2)) + 2]
                                             .rearrange("p c s q -> p (c s q)"), proj[u % 2][:],
                                             ACT.Copy).then_inc(proj_read[u % 2].sem, 1)
                    for s in range(2):
                        act.wait_ge(o_ps[s].sem, o_ps[s].at(t, 0))
                        for i in range(VN):
                            u = QK + VN * s + i
                            act.wait_ge(proj_ps[u % 2].sem, proj_ps[u % 2].at(t, u // 2 + 1))
                            nc.scalar.activation(v1[:, s, 8 * i:8 * i + 8, 0:D64],
                                                 proj[u % 2][:].rearrange("p (h d) -> p h d", d=D64),
                                                 ACT.Copy).then_inc(proj_read[u % 2].sem, 1)
                    for s in range(2):
                        act.wait_ge(nmT_ps[s].sem, nmT_ps[s].at(t, 1))
                        nc.scalar.activation(nmT[:, s, :], A[:, 0:P // 2].bitcast(BF16),
                                             ACT.Copy).then_inc(nmT_sb[s].sem, 1)
                        for j in range(UN):
                            if j == 0 and s == 0:
                                act.wait_ge(o_ps[1].sem, o_ps[1].at(t, 0))
                            elif j == 0:
                                act.wait_ge(o_ps[0].sem, o_ps[0].at(t, UN))
                            act.wait_ge(filled[j].sem, filled[j].at(t, 3 + s))
                            nc.scalar.activation(pT[:, 4 * j:4 * j + 4, :].rearrange("p h q -> p (h q)"), ring[j][:],
                                                 ACT.Exp, scale=scale).then_inc(p_sb[s].sem, 1)
                        for i in range(C2 // 4):
                            act.wait_ge(oT_ps[s].sem, oT_ps[s].at(t, i + 1))
                            nc.scalar.activation(oT[:, 4 * i:4 * i + 4, :].rearrange("p c q -> p (c q)"), A[:],
                                                 ACT.Copy).then_inc(oT_sb[s].sem, 1)

            @block.vector
            def _(dve):
                dve.wait_ge(k.loaded[stage], 16)
                dve.wait_ge(const.sem, const.base + 1)
                with dve.Fori(0, STEPS) as t:
                    for u in range(QK if rope else 0):
                        dve.wait_ge(proj_ps[u % 2].sem, proj_ps[u % 2].at(t, u // 2 + 1))
                        if u >= 2:
                            dve.wait_ge(qk_sb.sem, qk_sb.at(t, u - 1))
                        else:
                            dve.wait_ge(qk_sb.sem, qk_sb.at(t, 0))
                        nc.vector.tensor_tensor(turned[:, u % 2].rearrange("p a q -> p (a q)"), proj[u % 2][:],
                                                k.w("rope64"), ALU.mult).then_inc(turned_sb.sem, 1)
                    for i in range(2 if rope else 0):
                        dve.wait_ge(qk_sb.sem, qk_sb.at(t, C2 * (i + 1)))
                        nc.vector.tensor_copy(qk16[:, i].rearrange("p c s q -> p (c s q)"),
                                              qk[:, i].rearrange("p c s q -> p (c s q)")).then_inc(qk16_sb.sem, 1)
                    for s in range(2):
                        for j in range(UN):
                            dve.wait_ge(filled[j].sem, filled[j].at(t, 1 + s))
                            if j == 0:
                                dve.wait_ge(nmT_ps[s].sem, nmT_ps[s].at(t, 0))
                            nc.vector.tensor_reduce(
                                nm[:, s, 4 * j:4 * j + 4], ring[j][:].rearrange("p (h q) -> p h q", q=P),
                                AX.X, ALU.max, negate=True).then_inc(max_read[j].sem, 1)
                        dve.wait_ge(max_read[UN - 1].sem, max_read[UN - 1].at(t, 1 + s))
                        nc.vector.tensor_copy(nm[:, s, D64:D64 + heads], nm[:, s, 0:heads]).then_inc(nm_sb[s].sem, 1)
                    for s in range(2):
                        for j in range(UN):
                            dve.wait_ge(o_ps[s].sem, o_ps[s].at(t, j + 1))
                            ov = ring[j][:, 0:4 * W1].rearrange("p (h d) -> p h d", d=W1)
                            nc.vector.reciprocal(rs[:, s, j, :], ov[:, :, D64]).then_inc(rs_sb[s].sem, 1)
                            dve.wait_ge(rs_sb[s].sem, rs_sb[s].at(t, j + 1))
                            if j == 0 and s == 0:
                                dve.wait_ge(oT_ps[1].sem, oT_ps[1].at(t, 0))
                            elif j == 0:
                                dve.wait_ge(oT_ps[0].sem, oT_ps[0].at(t, C2 // 4))
                            h0 = unit_heads(j)[0]
                            nc.vector.tensor_tensor(
                                o[:, h0:h0 + 7:2, :], ov[:, :, 0:D64],
                                rs[:, s, j, :].unsqueeze(2).to_broadcast([P, 4, D64]), ALU.mult).then_inc(o_sb[s].sem, 1)
                        u = QK + 2 * VN + s
                        dve.wait_ge(proj_ps[u % 2].sem, proj_ps[u % 2].at(t, u // 2 + 1))
                        dve.wait_ge(tail.written[s].sem, tail.written[s].at(t, 0))
                        if not rope:
                            dve.wait_ge(xb_sb[s].sem, xb_sb[s].at(t, 1))
                        nc.vector.tensor_tensor(tail.r[:, s, :], proj[u % 2][:, 0:P],
                                                k.X[:, 2 * t + s, :] if rope else xb[:, s, :], ALU.add).then_inc(tail.summed[s].sem, 1)
                        tail.stats(dve, t, s)
                    for s in range(2):
                        tail.apply(dve, t, s)

            @block.tensor
            def _(pe):
                pe.wait_ge(k.loaded[stage], 16)
                if cross:
                    pe.wait_ge(k.ctx_loaded, 16)
                with pe.Fori(0, STEPS) as t:

                    def bank_free(u):
                        b = u % 2
                        n = u // 2
                        if n == 0:
                            pe.wait_ge(tail.summed[b].sem, tail.summed[b].at(t, 0))
                        elif rope and u - 2 < QK:
                            pe.wait_ge(turned_sb.sem, turned_sb.at(t, u - 1))
                        else:
                            pe.wait_ge(proj_read[b].sem, proj_read[b].at(t, reads_before(u)))

                    def reads_before(u):
                        return len([v for v in range(u % 2, u, 2) if not (rope and v < QK)])

                    for s in range(2):
                        pe.wait_ge(staged[s].sem, staged[s].at(t, 1))
                        if s == 0:
                            pe.wait_ge(oT_sb[1].sem, oT_sb[1].at(t, 0))
                        else:
                            pe.wait_ge(xT_sb[0].sem, xT_sb[0].at(t, 1))
                        nc.tensor.transpose(A[:, 0:P], xs[:, s, :], ident).then_inc(xT_ps[s].sem, 1)
                    for s in range(2):
                        pe.wait_ge(xT_sb[s].sem, xT_sb[s].at(t, 1))
                    both_x = xT[:].rearrange("p s q -> p (s q)")
                    both_src = src[:].rearrange("p s q -> p (s q)")
                    for u in range(QK):
                        bank_free(u)
                        if rope:
                            w = "Wq" if u < C2 else "Wk"
                            parts = [(name + w, u % C2), (name + w + "_swapped", u % C2)]
                            mov = both_x
                        else:
                            w = "Wq" if u < C2 // 2 else "Wk"
                            parts = [(name + w, 2 * (u % (C2 // 2)) + i) for i in range(2)]
                            mov = both_x if w == "Wq" else both_src
                        for i, (w, c) in enumerate(parts):
                            last = nc.tensor.matmul(proj[u % 2][:, 256 * i:256 * i + 256], k.w(w)[:, P * c:P * c + P],
                                                    mov, start=True, stop=True)
                        last.then_inc(proj_ps[u % 2].sem, 1)
                    for s in range(2):
                        for i in range(VN):
                            u = QK + VN * s + i
                            bank_free(u)
                            nc.tensor.matmul(proj[u % 2][:], src[:, s, :], k.w(name + "Wv")[:, 512 * i:512 * i + 512],
                                             start=True, stop=True).then_inc(proj_ps[u % 2].sem, 1)
                    if rope:
                        pe.wait_ge(qk16_sb.sem, qk16_sb.at(t, 2))
                    else:
                        for b in range(2):
                            pe.wait_ge(proj_read[b].sem, proj_read[b].at(t, QK // 2))
                    for s in range(2):
                        for j in range(UN):
                            if s == 0:
                                pe.wait_ge(o_sb[1].sem, o_sb[1].at(t, 0))
                            else:
                                pe.wait_ge(max_read[j].sem, max_read[j].at(t, 1))
                            if rope:
                                nc.tensor.matmul(ring[j][:], k.ident_bf[:], k.causal[:, 0].rearrange("p h q -> p (h q)"),
                                                 start=True, stop=False, skip_group_check=True)
                            for i, h in enumerate(unit_heads(j)):
                                b0 = D64 * (h % 2)
                                last = nc.tensor.matmul(ring[j][:, P * i:P * i + P], qk16[b0:b0 + D64, 0, h // 2, s, :],
                                                        qk16[b0:b0 + D64, 1, h // 2, s, :], start=not rope, stop=True,
                                                        skip_group_check=True)
                            last.then_inc(filled[j].sem, 1)
                    for s in range(2):
                        pe.wait_ge(nm_sb[s].sem, nm_sb[s].at(t, 1))
                        if s == 0:
                            pe.wait_ge(xT_sb[1].sem, xT_sb[1].at(t, 1))
                        else:
                            pe.wait_ge(oT_sb[0].sem, oT_sb[0].at(t, C2 // 4))
                        nc.tensor.transpose(A[:, 0:P // 2].bitcast(BF16), nm[:, s, :],
                                            k.ident_bf[:]).then_inc(nmT_ps[s].sem, 1)
                        pe.wait_ge(nmT_sb[s].sem, nmT_sb[s].at(t, 1))
                        for j in range(UN):
                            if s == 0:
                                pe.wait_ge(max_read[j].sem, max_read[j].at(t, 2))
                            else:
                                pe.wait_ge(o_sb[0].sem, o_sb[0].at(t, j + 1))
                            if rope:
                                nc.tensor.matmul(ring[j][:], k.ident_bf[:], k.causal[:, 1].rearrange("p h q -> p (h q)"),
                                                 start=True, stop=False, skip_group_check=True)
                            for i, h in enumerate(unit_heads(j)):
                                b0 = D64 * (h % 2)
                                dst = ring[j][:, P * i:P * i + P]
                                nc.tensor.matmul(dst, qk[b0:b0 + D64, 1, h // 2, s, :], qk[b0:b0 + D64, 0, h // 2, s, :],
                                                 start=not rope, stop=False, skip_group_check=True)
                                last = nc.tensor.matmul(dst, k.head_row[b0:b0 + D64, 4 * j + i, :],
                                                        nmT[b0:b0 + D64, s, :], start=False, stop=True,
                                                        skip_group_check=True)
                            last.then_inc(filled[j].sem, 1)
                        if s == 0:
                            for b in range(2):
                                pe.wait_ge(proj_read[b].sem, proj_read[b].at(t, reads_before(ANY - 2 + b)))
                        for j in range(UN):
                            pe.wait_ge(p_sb[s].sem, p_sb[s].at(t, j + 1))
                            for i, h in enumerate(unit_heads(j)):
                                last = nc.tensor.matmul(ring[j][:, i * W1:(i + 1) * W1], pT[:, 4 * j + i, :], v1[:, s, h, :],
                                                        start=True, stop=True)
                            last.then_inc(o_ps[s].sem, 1)
                        pe.wait_ge(o_sb[s].sem, o_sb[s].at(t, UN))
                        for i in range(C2 // 4):
                            if i >= 1:
                                pe.wait_ge(oT_sb[s].sem, oT_sb[s].at(t, i))
                            for c in range(4):
                                last = nc.tensor.transpose(A[:, P * c:P * c + P],
                                                           o[:, 8 * i + 2 * c:8 * i + 2 * c + 2, :]
                                                           .rearrange("p h d -> p (h d)"), ident)
                            last.then_inc(oT_ps[s].sem, 1)
                        pe.wait_ge(oT_sb[s].sem, oT_sb[s].at(t, C2 // 4))
                        u = QK + 2 * VN + s
                        for c in range(C2):
                            last = nc.tensor.matmul(proj[u % 2][:, 0:P], oT[:, c, :],
                                                    k.w(name + "Wo")[:, P * c:P * c + P], start=c == 0,
                                                    stop=c == C2 - 1)
                        last.then_inc(proj_ps[u % 2].sem, 1)


def attention_relu(k, stage, name):
    k.sig.new_stage(name)
    nc, sig = k.nc, k.sig
    with ExitStack() as ctx:
        def sb(what, shape, dt=F32):
            return ctx.enter_context(nc.sbuf_tensor(f"{name}_{what}", shape, dt))

        xs = sb("xs", [P, 2, DM])
        xb = sb("xb", [P, 2, DM])
        xT = sb("xT", [P, 2, P])
        qT = sb("qT", [P, 2, P])
        kv = sb("kv", [P, 2, 2 * DM])
        kr = sb("kr", [P, 2, DM])
        kvm = sb("kvm", [P, 2, DM])
        aT = sb("aT", [P, 2, P])
        tail = Tail(k, ctx, name)
        bank = lambda s, i: k.bank[4 * s + i]
        staged = sig.pair("staged")
        xT_ps, xT_sb = sig.pair("xT_ps"), sig.pair("xT_sb")
        q_ps, q_sb = sig.pair("q_ps"), sig.pair("q_sb")
        kv_ps, kv_sb, kr_sb = sig.pair("kv_ps"), sig.pair("kv_sb"), sig.pair("kr_sb")
        kvm_ps, kvm_sb = sig.pair("kvm_ps"), sig.pair("kvm_sb")
        aT_ps, aT_sb = sig.pair("aT_ps"), sig.pair("aT_sb")
        y_ps, xb_sb = sig.pair("y_ps"), sig.pair("xb_sb")

        with nc.Block() as block:

            @block.sync
            def _(sp):
                k.load_weights(sp, k.next_stage(stage))

            @block.gpsimd
            def _(pool):
                pool.wait_ge(k.loaded[stage], 16)
                with pool.Fori(0, STEPS) as t:
                    for s in range(2):
                        pool.wait_ge(xT_ps[s].sem, xT_ps[s].at(t, 0))
                        nc.gpsimd.tensor_copy(xs[:, s, :], k.X[:, 2 * t + s, :]).then_inc(staged[s].sem, 1)
                    for s in range(2):
                        pool.wait_ge(tail.summed[s].sem, tail.summed[s].at(t, 0))
                        pool.wait_ge(staged[s].sem, staged[s].at(t, 1))
                        nc.gpsimd.tensor_tensor(xb[:, s, :], xs[:, s, :], k.w(name + "bo"),
                                                ALU.add).then_inc(xb_sb[s].sem, 1)
                    for s in range(2):
                        tail.rstd(pool, t, s)

            @block.scalar
            def _(act):
                act.wait_ge(k.loaded[stage], 16)
                with act.Fori(0, STEPS) as t:
                    for s in range(2):
                        act.wait_ge(xT_ps[s].sem, xT_ps[s].at(t, 1))
                        nc.scalar.activation(xT[:, s, :], bank(s, 0)[:, 0:P], ACT.Copy).then_inc(xT_sb[s].sem, 1)
                    for s in range(2):
                        act.wait_ge(q_ps[s].sem, q_ps[s].at(t, 1))
                        nc.scalar.activation(qT[:, s, :], bank(s, 1)[:, 0:P], ACT.Relu,
                                             bias=k.w(name + "bq")).then_inc(q_sb[s].sem, 1)
                    for s in range(2):
                        act.wait_ge(aT_ps[s].sem, aT_ps[s].at(t, 1))
                        nc.scalar.activation(aT[:, s, :], bank(s, 0)[:, 0:P], ACT.Copy).then_inc(aT_sb[s].sem, 1)

            @block.vector
            def _(dve):
                dve.wait_ge(k.loaded[stage], 16)
                with dve.Fori(0, STEPS) as t:
                    for s in range(2):
                        dve.wait_ge(kv_ps[s].sem, kv_ps[s].at(t, 1))
                        nc.vector.tensor_tensor(kv[:, s, :], bank(s, 2)[:, 0:2 * DM], k.w(name + "bkv"),
                                                ALU.add).then_inc(kv_sb[s].sem, 1)
                    for s in range(2):
                        dve.wait_ge(kv_sb[s].sem, kv_sb[s].at(t, 1))
                        nc.vector.tensor_scalar(kr[:, s, :], kv[:, s, 0:DM], 0.0, None,
                                                ALU.max).then_inc(kr_sb[s].sem, 1)
                    for s in range(2):
                        dve.wait_ge(kvm_ps[s].sem, kvm_ps[s].at(t, 1))
                        nc.vector.tensor_tensor(kvm[:, s, :], bank(s, 3)[:, 0:DM], k.w(name + "blocks"),
                                                ALU.mult).then_inc(kvm_sb[s].sem, 1)
                    for s in range(2):
                        dve.wait_ge(y_ps[s].sem, y_ps[s].at(t, 1))
                        dve.wait_ge(xb_sb[s].sem, xb_sb[s].at(t, 1))
                        nc.vector.tensor_tensor(tail.r[:, s, :], bank(s, 3)[:, 0:DM], xb[:, s, :],
                                                ALU.add).then_inc(tail.summed[s].sem, 1)
                        tail.stats(dve, t, s)
                    for s in range(2):
                        tail.apply(dve, t, s)

            @block.tensor
            def _(pe):
                pe.wait_ge(k.loaded[stage], 16)
                with pe.Fori(0, STEPS) as t:
                    for s in range(2):
                        pe.wait_ge(staged[s].sem, staged[s].at(t, 1))
                        pe.wait_ge(aT_sb[s].sem, aT_sb[s].at(t, 0))
                        nc.tensor.transpose(bank(s, 0)[:, 0:P], xs[:, s, :], k.w("ident")).then_inc(xT_ps[s].sem, 1)
                    for s in range(2):
                        pe.wait_ge(xT_sb[s].sem, xT_sb[s].at(t, 1))
                        pe.wait_ge(kr_sb[s].sem, kr_sb[s].at(t, 0))
                        nc.tensor.matmul(bank(s, 2)[:, 0:2 * DM], xT[:, s, :], k.w(name + "Wkv"), start=True,
                                         stop=True).then_inc(kv_ps[s].sem, 1)
                        nc.tensor.matmul(bank(s, 1)[:, 0:P], k.w(name + "Wq"), xT[:, s, :], start=True,
                                         stop=True).then_inc(q_ps[s].sem, 1)
                    for s in range(2):
                        pe.wait_ge(kr_sb[s].sem, kr_sb[s].at(t, 1))
                        pe.wait_ge(tail.summed[s].sem, tail.summed[s].at(t, 0))
                        nc.tensor.matmul(bank(s, 3)[:, 0:DM], kr[:, s, :], kv[:, s, DM:2 * DM], start=True,
                                         stop=True).then_inc(kvm_ps[s].sem, 1)
                    for s in range(2):
                        pe.wait_ge(kvm_sb[s].sem, kvm_sb[s].at(t, 1))
                        pe.wait_ge(q_sb[s].sem, q_sb[s].at(t, 1))
                        nc.tensor.matmul(bank(s, 0)[:, 0:P], kvm[:, s, :], qT[:, s, :], start=True,
                                         stop=True).then_inc(aT_ps[s].sem, 1)
                    for s in range(2):
                        pe.wait_ge(aT_sb[s].sem, aT_sb[s].at(t, 1))
                        nc.tensor.matmul(bank(s, 3)[:, 0:DM], aT[:, s, :], k.w(name + "Wo"), start=True,
                                         stop=True).then_inc(y_ps[s].sem, 1)


def attention_linear(k, stage, name):
    k.sig.new_stage(name)
    nc, sig = k.nc, k.sig
    with ExitStack() as ctx:
        def sb(what, shape, dt=F32):
            return ctx.enter_context(nc.sbuf_tensor(f"{name}_{what}", shape, dt))

        HT = sb("HT", [P, NB, P])
        xs = sb("xs", [P, 2, DM])
        staged = sig.pair("staged")
        xT_ps, xT_sb = sig.pair("xT_ps"), sig.pair("xT_sb")

        with nc.Block() as block:

            @block.gpsimd
            def _(pool):
                with pool.Fori(0, STEPS) as t:
                    for s in range(2):
                        pool.wait_ge(xT_ps[s].sem, xT_ps[s].at(t, 0))
                        nc.gpsimd.tensor_copy(xs[:, s, :], k.X[:, 2 * t + s, :]).then_inc(staged[s].sem, 1)

            @block.scalar
            def _(act):
                act.wait_ge(k.loaded[stage], 16)
                with act.Fori(0, STEPS) as t:
                    for s in range(2):
                        act.wait_ge(xT_ps[s].sem, xT_ps[s].at(t, 1))
                        nc.scalar.activation(HT[:, 2 * t + s, :], k.bank[s][:, 0:P], ACT.Identity,
                                             bias=k.w("positions")[:, bass.ds(2 * t + s, 1)]).then_inc(xT_sb[s].sem, 1)

            @block.tensor
            def _(pe):
                with pe.Fori(0, STEPS) as t:
                    for s in range(2):
                        pe.wait_ge(staged[s].sem, staged[s].at(t, 1))
                        pe.wait_ge(xT_sb[s].sem, xT_sb[s].at(t, 0))
                        nc.tensor.transpose(k.bank[s][:, 0:P], xs[:, s, :], k.w("ident")).then_inc(xT_ps[s].sem, 1)

        hs = sb("hs", [P, 2, 4, NB])
        pre = sb("pre", [P, 2, 2, P])
        low = sb("low", [P, 2, 2, P])
        ex = sb("ex", [P, 2, 2, P])
        phi = sb("phi", [P, 2, 2, P])
        v1 = sb("v1", [P, 2, 2, DM])
        kvz = sb("kvz", [P, 4, 2, DM])
        den, rden, att = sb("den", [P, 2, P]), sb("rden", [P, 2, P]), sb("att", [P, 2, P])
        group = sig.pair("group_staged")
        kv_ps, q_ps = sig.pair("kv_ps"), sig.pair("q_ps")
        k_sb, v_sb, q_sb = sig.pair("k_sb"), sig.pair("v_sb"), sig.pair("q_sb")
        low_sb, ex_sb, phi_sb = sig.pair("low_sb"), sig.pair("elu_exp"), sig.pair("phi_sb")
        kvz_ps, kvz_sb = sig.ring("kvz_ps", 4, 2), sig.ring("kvz_sb", 4, 2)
        att_ps = sig.pair("att_ps")
        den_sb, rden_sb, att_sb = sig.pair("den_sb"), sig.pair("rden_sb"), sig.pair("att_sb")
        y_ps, y_sb = sig.pair("y_ps"), sig.pair("y_sb")
        ones_set = sig.one("ones_set", 1, 1)

        with nc.Block() as block:

            @block.gpsimd
            def _(pool):
                nc.gpsimd.memset(v1[:], 1.0).then_inc(ones_set.sem, 1)
                with pool.Fori(0, STEPS) as t:
                    for s in range(2):
                        pool.wait_ge(q_ps[s].sem, q_ps[s].at(t, 0))
                        nc.gpsimd.tensor_copy(hs[:, s].rearrange("p q b -> p b q"),
                                              HT[:, :, bass.ds(4 * (2 * t + s), 4)]).then_inc(group[s].sem, 1)

            @block.scalar
            def _(act):
                with act.Fori(0, STEPS) as t:
                    for s in range(2):
                        act.wait_ge(q_ps[s].sem, q_ps[s].at(t, 1))
                        act.wait_ge(phi_sb[s].sem, phi_sb[s].at(t, 0))
                        nc.scalar.activation(pre[:, s, 1, :], k.bank[2 * s + 1][:, 0:P], ACT.Identity,
                                             bias=k.w(name + "bq")).then_inc(q_sb[s].sem, 1)
                        act.wait_ge(low_sb[s].sem, low_sb[s].at(t, 1))
                        nc.scalar.activation(ex[:, s], low[:, s], ACT.Exp).then_inc(ex_sb[s].sem, 1)
                    for s in range(2):
                        act.wait_ge(y_ps[s].sem, y_ps[s].at(t, 1))
                        nc.scalar.activation(HT[:, :, bass.ds(4 * (2 * t + s), 4)],
                                             k.bank[2 * s][:, 0:P].rearrange("p (q b) -> p b q", b=NB), ACT.Identity,
                                             bias=k.w(name + "bo")).then_inc(y_sb[s].sem, 1)

            @block.vector
            def _(dve):
                dve.wait_ge(ones_set.sem, ones_set.base + 1)
                dve.wait_ge(k.loaded[stage], 16)
                with dve.Fori(0, STEPS) as t:
                    for s in range(2):
                        dve.wait_ge(kv_ps[s].sem, kv_ps[s].at(t, 1))
                        dve.wait_ge(phi_sb[s].sem, phi_sb[s].at(t, 0))
                        nc.vector.tensor_tensor(pre[:, s, 0, :], k.bank[2 * s][:, 0:DM], k.w(name + "bkv")[:, 0:DM],
                                                ALU.add).then_inc(k_sb[s].sem, 1)
                        nc.vector.tensor_tensor(v1[:, s, 0, :], k.bank[2 * s][:, DM:2 * DM],
                                                k.w(name + "bkv")[:, DM:2 * DM], ALU.add).then_inc(v_sb[s].sem, 1)
                        dve.wait_ge(k_sb[s].sem, k_sb[s].at(t, 1))
                        dve.wait_ge(q_sb[s].sem, q_sb[s].at(t, 1))
                        nc.vector.tensor_scalar(low[:, s], pre[:, s], 0.0, None, ALU.min).then_inc(low_sb[s].sem, 1)
                    for s in range(2):
                        dve.wait_ge(ex_sb[s].sem, ex_sb[s].at(t, 1))
                        dve.wait_ge(att_ps[s].sem, att_ps[s].at(t, 0))
                        nc.vector.scalar_tensor_tensor(out=phi[:, s], in0=pre[:, s], scalar=0.0, in1=ex[:, s],
                                                       op0=ALU.max, op1=ALU.add).then_inc(phi_sb[s].sem, 1)
                    for s in range(2):
                        for i in range(4):
                            dve.wait_ge(kvz_ps[i].sem, kvz_ps[i].at(t, s + 1))
                            if i == 0 and s == 0:
                                dve.wait_ge(att_ps[1].sem, att_ps[1].at(t, 0))
                            elif i == 0:
                                dve.wait_ge(att_ps[0].sem, att_ps[0].at(t, 1))
                            nc.vector.tensor_tensor(kvz[:, i].rearrange("p a d -> p (a d)"), k.bank[4 + i][:, 0:2 * DM],
                                                    k.w(name + "blocks"), ALU.mult).then_inc(kvz_sb[i].sem, 1)
                        dve.wait_ge(att_ps[s].sem, att_ps[s].at(t, 1))
                        nc.vector.tensor_scalar(den[:, s, :], k.bank[2 * s + 1][:, 2 * P:3 * P], 1e-6, None,
                                                ALU.add).then_inc(den_sb[s].sem, 1)
                        dve.wait_ge(den_sb[s].sem, den_sb[s].at(t, 1))
                        nc.vector.reciprocal(rden[:, s, :], den[:, s, :]).then_inc(rden_sb[s].sem, 1)
                        dve.wait_ge(rden_sb[s].sem, rden_sb[s].at(t, 1))
                        dve.wait_ge(y_ps[s].sem, y_ps[s].at(t, 0))
                        nc.vector.tensor_tensor(att[:, s, :], k.bank[2 * s + 1][:, P:2 * P], rden[:, s, :],
                                                ALU.mult).then_inc(att_sb[s].sem, 1)

            @block.tensor
            def _(pe):
                with pe.Fori(0, STEPS) as t:
                    for s in range(2):
                        pe.wait_ge(group[s].sem, group[s].at(t, 1))
                        pe.wait_ge(y_sb[s].sem, y_sb[s].at(t, 0))
                        pe.wait_ge(att_sb[s].sem, att_sb[s].at(t, 0))
                        flat = hs[:, s].rearrange("p q b -> p (q b)")
                        nc.tensor.matmul(k.bank[2 * s][:, 0:2 * DM], flat, k.w(name + "Wkv"), start=True,
                                         stop=True).then_inc(kv_ps[s].sem, 1)
                        nc.tensor.matmul(k.bank[2 * s + 1][:, 0:P], k.w(name + "Wq"), flat, start=True,
                                         stop=True).then_inc(q_ps[s].sem, 1)
                    for s in range(2):
                        pe.wait_ge(phi_sb[s].sem, phi_sb[s].at(t, 1))
                        pe.wait_ge(v_sb[s].sem, v_sb[s].at(t, 1))
                        for i in range(4):
                            pe.wait_ge(kvz_sb[i].sem, kvz_sb[i].at(t, s))
                            nc.tensor.matmul(k.bank[4 + i][:, 0:2 * DM], phi[NB * i:NB * i + NB, s, 0, :],
                                             v1[NB * i:NB * i + NB, s].rearrange("p a d -> p (a d)"), start=True,
                                             stop=True).then_inc(kvz_ps[i].sem, 1)
                        for i in range(4):
                            pe.wait_ge(kvz_sb[i].sem, kvz_sb[i].at(t, s + 1))
                            for a in range(2):
                                o = P * (1 + a) + NB * i
                                last = nc.tensor.matmul(k.bank[2 * s + 1][:, o:o + NB], kvz[:, i, a, :],
                                                        phi[:, s, 1, NB * i:NB * i + NB], start=True, stop=True)
                        last.then_inc(att_ps[s].sem, 1)
                    for s in range(2):
                        pe.wait_ge(att_sb[s].sem, att_sb[s].at(t, 1))
                        nc.tensor.matmul(k.bank[2 * s][:, 0:P], k.w(name + "Wo"), att[:, s, :], start=True,
                                         stop=True).then_inc(y_ps[s].sem, 1)

        tail = Tail(k, ctx, name)
        staged = sig.pair("staged")
        y_back = sig.pair("y_ps")

        with nc.Block() as block:

            @block.sync
            def _(sp):
                k.load_weights(sp, k.next_stage(stage))

            @block.gpsimd
            def _(pool):
                with pool.Fori(0, STEPS) as t:
                    for s in range(2):
                        pool.wait_ge(y_back[s].sem, y_back[s].at(t, 0))
                        nc.gpsimd.tensor_copy(xs[:, s, :], HT[:, 2 * t + s, :]).then_inc(staged[s].sem, 1)
                    for s in range(2):
                        tail.rstd(pool, t, s)

            @block.vector
            def _(dve):
                with dve.Fori(0, STEPS) as t:
                    for s in range(2):
                        dve.wait_ge(y_back[s].sem, y_back[s].at(t, 1))
                        dve.wait_ge(tail.written[s].sem, tail.written[s].at(t, 0))
                        nc.vector.tensor_tensor(tail.r[:, s, :], k.bank[s][:, 0:P], k.X[:, 2 * t + s, :],
                                                ALU.add).then_inc(tail.summed[s].sem, 1)
                        tail.stats(dve, t, s)
                    for s in range(2):
                        tail.apply(dve, t, s)

            @block.tensor
            def _(pe):
                with pe.Fori(0, STEPS) as t:
                    for s in range(2):
                        pe.wait_ge(staged[s].sem, staged[s].at(t, 1))
                        pe.wait_ge(tail.summed[s].sem, tail.summed[s].at(t, 0))
                        nc.tensor.transpose(k.bank[s][:, 0:P], xs[:, s, :], k.w("ident")).then_inc(y_back[s].sem, 1)


def film_conv(k, stage, name):
    nc, sig = k.nc, k.sig
    k.sig.new_stage(name)
    heads, dh = 4, 32
    rounds = 32 // 8
    NN = 64
    FINE = 16
    COARSE = P // FINE
    scale = float(dh ** -0.5)
    with ExitStack() as outer:
        def keep(what, shape, dt=F32):
            return outer.enter_context(nc.sbuf_tensor(f"{name}_{what}", shape, dt))

        UY = keep("UY", [P, NB, DM])
        FO = keep("FO", [P, NB, 2 * DM])
        kernel_dram = nc.dram_tensor("s4d_kernel", (P, 2 * P), F32)
        kernel_stored = sig.one("kernel_stored", 16, 1)

        with ExitStack() as mid:
            def hold(what, shape, dt=F32):
                return mid.enter_context(nc.sbuf_tensor(f"{name}_{what}", shape, dt))

            key_bias = hold("key_bias", [P, NB, P], BF16)
            text_gate = hold("text_gate", [P, NB])
            film_bias = hold("film_bias", [P, 4 * DM])
            with ExitStack() as ctx:
                def sb(what, shape, dt=F32):
                    return ctx.enter_context(nc.sbuf_tensor(f"{name}_{what}", shape, dt))

                mask_keys = sb("mask_keys", [P, NB, P], U8)
                mask_text = sb("mask_text", [P, NB], U8)
                text = sb("text", [P, NB])
                kz = sb("kz", [P, 2 * P])
                dt = sb("dt", [P, 1])
                a_re, a_im = sb("a_re", [P, NN]), sb("a_im", [P, NN])
                turn, whole, ang1, ang, nang, aang, cang = (
                    sb(n, [P, NN]) for n in ("turn", "whole", "ang1", "ang", "nang", "aang", "cang"))
                mag, sn, cs = sb("mag", [P, NN]), sb("sin", [P, NN]), sb("cos", [P, NN])
                sq, sq2, inv = sb("sq", [P, NN]), sb("sq2", [P, NN]), sb("inv", [P, NN])
                z1, nim = sb("z1", [P, NN]), sb("nim", [P, NN])
                g_re, g_im = sb("g_re", [P, NN]), sb("g_im", [P, NN])
                h_re, h_im = sb("h_re", [P, NN]), sb("h_im", [P, NN])
                pw = [sb("pw_re", [P, FINE + 1, NN]), sb("pw_im", [P, FINE + 1, NN])]
                ws = [sb("w_re", [P, COARSE, NN]), sb("w_im", [P, COARSE, NN])]
                q2 = [sb("q2_re", [P, 1, NN]), sb("q2_im", [P, 1, NN])]
                q4 = [sb("q4_re", [P, 1, NN]), sb("q4_im", [P, 1, NN])]
                t4 = [sb(f"prod{i}", [P, FINE * NN]) for i in range(4)]
                step = sig.one("kernel_step", 1, 1)
                masks_in = sig.one("masks_loaded", 32, 1)
                dt_sb, angles, sines, kz_sb = (sig.one(n, 1, 1) for n in ("dt_sb", "angles", "sines", "kernel_sb"))
                magic = 12582912.0
                two_pi_hi = 6.28125
                two_pi_lo = float(2 * np.pi - two_pi_hi)
                w = lambda n: k.w(name + n)

                with nc.Block() as block:

                    @block.sync
                    def _(sp):
                        sp.dma_start(mask_keys[:], k.masks[1]).then_inc(masks_in.sem, 16)
                        sp.dma_start(mask_text[:], k.masks[0]).then_inc(masks_in.sem, 16)
                        sp.wait_ge(kz_sb.sem, kz_sb.base + 1)
                        sp.dma_start(kernel_dram.ap(), kz[:]).then_inc(kernel_stored.sem, 16)
                        sp.wait_ge(kernel_stored.sem, 16)

                    @block.scalar
                    def _(act):
                        act.wait_ge(k.loaded[stage], 16)
                        nc.scalar.activation(dt[:], w("log_dt"), ACT.Exp).then_inc(dt_sb.sem, 1)
                        act.wait_ge(angles.sem, angles.base + 1)
                        nc.scalar.activation(mag[:], a_re[:], ACT.Exp)
                        nc.scalar.activation(sn[:], ang[:], ACT.Sin)
                        nc.scalar.activation(cs[:], cang[:], ACT.Sin).then_inc(sines.sem, 1)

                    @block.vector
                    def _(dve):
                        n = [0]

                        def link(ins):
                            n[0] += 1
                            ins.then_inc(step.sem, 1)
                            dve.wait_ge(step.sem, n[0])

                        tt, ts = nc.vector.tensor_tensor, nc.vector.tensor_scalar
                        stt = nc.vector.scalar_tensor_tensor

                        def times(out, a, b, shape):
                            m = shape[1]
                            p = [t[:, 0:m * NN].rearrange("p (m n) -> p m n", n=NN) for t in t4]
                            tt(p[0], a[0], b[0], ALU.mult)
                            tt(p[1], a[1], b[1], ALU.mult)
                            tt(p[2], a[0], b[1], ALU.mult)
                            link(tt(p[3], a[1], b[0], ALU.mult))
                            tt(out[0], p[0], p[1], ALU.subtract)
                            link(tt(out[1], p[2], p[3], ALU.add))

                        dve.wait_ge(k.loaded[stage], 16)
                        nc.vector.memset(kz[:], 0.0)
                        for i in range(2):
                            nc.vector.memset(pw[i][:, 0, :], 1.0 - i)
                        ts(film_bias[:], w("b_film"), w("gate"), None, ALU.mult)
                        tt(sq[:], w("A_re"), w("A_re"), ALU.mult)
                        link(tt(sq2[:], w("A_im"), w("A_im"), ALU.mult))
                        for c in (0, 2):
                            ts(film_bias[:, DM * c:DM * c + DM], film_bias[:, DM * c:DM * c + DM], 1.0, None, ALU.add)
                        link(tt(nim[:], sq[:], sq2[:], ALU.add))
                        link(nc.vector.reciprocal(inv[:], nim[:]))
                        dve.wait_ge(masks_in.sem, 32)
                        ts(key_bias[:], mask_keys[:], -NEG, NEG, ALU.mult, ALU.add)
                        link(nc.vector.tensor_copy(text[:], mask_text[:]))
                        ts(text_gate[:], text[:], w("gate"), 1.0 / heads, ALU.mult, ALU.mult)
                        dve.wait_ge(dt_sb.sem, dt_sb.base + 1)
                        ts(a_re[:], w("A_re"), dt[:], None, ALU.mult)
                        link(ts(a_im[:], w("A_im"), dt[:], None, ALU.mult))
                        link(ts(turn[:], a_im[:], float(1 / (2 * np.pi)), None, ALU.mult))
                        link(ts(ang1[:], turn[:], magic, None, ALU.add))
                        link(ts(whole[:], ang1[:], magic, None, ALU.subtract))
                        link(stt(out=nang[:], in0=whole[:], scalar=-two_pi_hi, in1=a_im[:], op0=ALU.mult, op1=ALU.add))
                        link(stt(out=aang[:], in0=whole[:], scalar=-two_pi_lo, in1=nang[:], op0=ALU.mult, op1=ALU.add))
                        link(ts(ang[:], aang[:], 3.1415925, -3.1415925, ALU.min, ALU.max))
                        link(ts(nang[:], ang[:], -1.0, None, ALU.mult))
                        link(tt(aang[:], ang[:], nang[:], ALU.max))
                        ts(cang[:], aang[:], -1.0, float(np.pi / 2), ALU.mult, ALU.add).then_inc(angles.sem, 1)
                        dve.wait_ge(sines.sem, sines.base + 1)
                        tt(pw[0][:, 1, :], mag[:], cs[:], ALU.mult)
                        link(tt(pw[1][:, 1, :], mag[:], sn[:], ALU.mult))
                        ts(z1[:], pw[0][:, 1, :], 1.0, None, ALU.subtract)
                        link(ts(nim[:], w("A_im"), -1.0, None, ALU.mult))
                        one = lambda a: a.unsqueeze(1)
                        times((one(g_re[:]), one(g_im[:])), (one(z1[:]), pw[1][:, 1:2, :]),
                              (one(w("A_re")), one(nim[:])), [P, 1, NN])
                        stt(out=h_re[:], in0=g_re[:], scalar=2.0, in1=inv[:], op0=ALU.mult, op1=ALU.mult)
                        link(stt(out=h_im[:], in0=g_im[:], scalar=2.0, in1=inv[:], op0=ALU.mult, op1=ALU.mult))
                        times([a[:, 0:1, :] for a in ws], (one(h_re[:]), one(h_im[:])),
                              (one(w("C_re")), one(w("C_im"))), [P, 1, NN])
                        m = 1
                        while m < FINE:
                            times([a[:, m + 1:2 * m + 1, :] for a in pw], [a[:, 1:m + 1, :] for a in pw],
                                  [a[:, m:m + 1, :].to_broadcast([P, m, NN]) for a in pw], [P, m, NN])
                            m *= 2
                        q = [a[:, FINE:FINE + 1, :] for a in pw]
                        times([a[:] for a in q2], q, q, [P, 1, NN])
                        times([a[:] for a in q4], [a[:] for a in q2], [a[:] for a in q2], [P, 1, NN])
                        for m, f in ((1, q), (2, [a[:] for a in q2]), (4, [a[:] for a in q4])):
                            times([a[:, m:2 * m, :] for a in ws], [a[:, 0:m, :] for a in ws],
                                  [a.to_broadcast([P, m, NN]) for a in f], [P, m, NN])
                        p = [t[:].rearrange("p (m n) -> p m n", n=NN) for t in t4]
                        for a in range(COARSE):
                            for i in range(2):
                                last = tt(p[i], pw[i][:, 0:FINE, :], ws[i][:, a:a + 1, :].to_broadcast([P, FINE, NN]),
                                          ALU.mult)
                            link(last)
                            link(tt(p[2], p[0], p[1], ALU.subtract))
                            o = P - 1 + FINE * a
                            link(nc.vector.tensor_reduce(kz[:, o:o + FINE], p[2], AX.X, ALU.add))
                        tt(kz[:, P - 1:P], kz[:, P - 1:P], w("D_skip"), ALU.add).then_inc(kz_sb.sem, 1)

            with ExitStack() as ctx:
                def sb(what, shape, dt=F32):
                    return ctx.enter_context(nc.sbuf_tensor(f"{name}_{what}", shape, dt))

                bank = lambda s, i: k.bank[4 * s + i]
                xs = sb("xs", [P, 2, DM])
                cx = sb("cx", [DC, 2, P])
                xb = sb("xb", [P, 2, DM])
                gate = sb("gate_now", [P, 2, 1])
                xT, qT = sb("xT", [P, 2, P]), sb("qT", [P, 2, P])
                kT = sb("kT", [P, 2, heads, P])
                v = sb("v", [P, 2, DM])
                sc = sb("sc", [P, 2, heads, P])
                left = [sb(f"left{i}", [P, 2, heads, P]) for i in range(2)]
                top = sb("top", [P, 2, heads, 8 * rounds])
                nmax = sb("nmax", [P, 2, heads])
                den, rden = sb("den", [P, 2, heads]), sb("rden", [P, 2, heads])
                etop = sb("etop", [P, 2, heads, 8 * rounds])
                ex, pn = sb("ex", [P, 2, heads, P]), sb("pn", [P, 2, heads, P])
                amT, cT = sb("amT", [P, 2, P]), sb("cT", [P, 2, P])
                film = sb("film", [P, 2, 4 * DM])
                st, mv, rs = sb("st", [P, 2, 6]), sb("mv", [P, 2, 2]), sb("rs", [P, 2, 2])
                lg, ln, u1 = sb("lg", [P, 2, DM]), sb("ln", [P, 2, DM]), sb("u1", [P, 2, DM])
                zeroed = sig.one("keys_zeroed", 1, 1)
                xs_sb, xT_ps, xT_sb, qk_ps, q_sb, k_sb = (
                    sig.pair(n) for n in ("xs_sb", "xT_ps", "xT_sb", "qk_ps", "q_sb", "k_sb"))
                sc_ps, sc_sb = sig.pair("scores_ps"), sig.pair("scores_sb")
                top_sb, left_sb = sig.pair("top_sb", rounds), sig.pair("left_sb", rounds)
                nmax_sb, ex_sb, den_sb, rden_sb, pn_sb = (
                    sig.pair(n) for n in ("nmax_sb", "ex_sb", "den_sb", "rden_sb", "pn_sb"))
                sel_sb = sig.pair("selected_sb")
                cx_sb, xb_sb, v_ps, v_sb = (sig.pair(n) for n in ("cx_sb", "xb_sb", "v_ps", "v_sb"))
                amT_ps, amT_sb, cT_ps, cT_sb, film_ps, film_sb = (
                    sig.pair(n) for n in ("amT_ps", "amT_sb", "cT_ps", "cT_sb", "film_ps", "film_sb"))
                halves, moments, var_eps, rstd = (sig.pair(n) for n in ("halves", "moments", "var_eps", "rstd"))
                lg_sb, ln_sb, u1_sb, u_sb = (sig.pair(n) for n in ("lg_sb", "ln_sb", "u1_sb", "u_sb"))

                with nc.Block() as block:

                    @block.gpsimd
                    def _(pool):
                        with pool.Fori(0, STEPS) as t:
                            for s in range(2):
                                pool.wait_ge(v_ps[s].sem, v_ps[s].at(t, 0))
                                nc.gpsimd.tensor_copy(cx[:, s, :], k.ctxT[:, 2 * t + s, :]).then_inc(cx_sb[s].sem, 1)
                                pool.wait_ge(film_sb[s].sem, film_sb[s].at(t, 0))
                                nc.gpsimd.tensor_copy(gate[:, s, :], text_gate[:, bass.ds(2 * t + s, 1)])
                                pool.wait_ge(lg_sb[s].sem, lg_sb[s].at(t, 0))
                                nc.gpsimd.tensor_copy(xb[:, s, :], k.X[:, 2 * t + s, :]).then_inc(xb_sb[s].sem, 1)
                            for s in range(2):
                                pool.wait_ge(moments[s].sem, moments[s].at(t, 1))
                                nc.gpsimd.tensor_tensor(rs[:, s, 0:1], mv[:, s, 1:2], k.eps[:, 0:1],
                                                        ALU.add).then_inc(var_eps[s].sem, 1)
                                pool.wait_ge(var_eps[s].sem, var_eps[s].at(t, 1))
                                nc.gpsimd.tensor_tensor(rs[:, s, 1:2], rs[:, s, 0:1], k.neg_half[:, 0:1],
                                                        ALU.pow).then_inc(rstd[s].sem, 1)
                            for s in range(2):
                                pool.wait_ge(ln_sb[s].sem, ln_sb[s].at(t, 1))
                                pool.wait_ge(film_sb[s].sem, film_sb[s].at(t, 1))
                                nc.gpsimd.tensor_tensor(u1[:, s, :], ln[:, s, :], film[:, s, 0:DM],
                                                        ALU.mult).then_inc(u1_sb[s].sem, 1)
                                nc.gpsimd.tensor_copy(FO[:, 2 * t + s, :], film[:, s, 2 * DM:4 * DM])
                                pool.wait_ge(u1_sb[s].sem, u1_sb[s].at(t, 1))
                                nc.gpsimd.tensor_tensor(UY[:, 2 * t + s, :], u1[:, s, :], film[:, s, DM:2 * DM],
                                                        ALU.add).then_inc(u_sb[s].sem, 1)

                    @block.scalar
                    def _(act):
                        def front(t):
                            for s in range(2):
                                act.wait_ge(xT_ps[s].sem, xT_ps[s].at(t, 1))
                                nc.scalar.activation(xT[:, s, :], bank(s, 0)[:, 0:P], ACT.Copy).then_inc(xT_sb[s].sem, 1)
                            for s in range(2):
                                act.wait_ge(qk_ps[s].sem, qk_ps[s].at(t, 1))
                                act.wait_ge(sc_ps[s].sem, sc_ps[s].at(t, 0))
                                nc.scalar.activation(qT[:, s, :], bank(s, 0)[:, P:2 * P], ACT.Copy).then_inc(q_sb[s].sem, 1)
                                for h in range(heads):
                                    last = nc.scalar.activation(kT[dh * h:dh * h + dh, s, h, :],
                                                                bank(s, 0)[dh * h:dh * h + dh, 2 * P:3 * P], ACT.Copy)
                                last.then_inc(k_sb[s].sem, 1)

                        def weights(t):
                            for s in range(2):
                                act.wait_ge(nmax_sb[s].sem, nmax_sb[s].at(t, 1))
                                act.wait_ge(pn_sb[s].sem, pn_sb[s].at(t, 0))
                                for h in range(heads):
                                    last = nc.scalar.activation(ex[:, s, h, :], sc[:, s, h, :], ACT.Exp,
                                                                bias=nmax[:, s, h:h + 1], scale=scale)
                                last.then_inc(ex_sb[s].sem, 1)
                            for s in range(2):
                                act.wait_ge(top_sb[s].sem, top_sb[s].at(t, rounds))
                                for h in range(heads):
                                    last = nc.scalar.activation(etop[:, s, h, :], top[:, s, h, :], ACT.Exp,
                                                                bias=nmax[:, s, h:h + 1], scale=scale,
                                                                accum_out=den[:, s, h:h + 1])
                                last.then_inc(den_sb[s].sem, 1)

                        def back(t):
                            for s in range(2):
                                act.wait_ge(v_ps[s].sem, v_ps[s].at(t, 1))
                                act.wait_ge(cT_ps[s].sem, cT_ps[s].at(t, 0))
                                nc.scalar.activation(v[:, s, :], bank(s, 3)[:, 2 * P:3 * P], ACT.Copy).then_inc(v_sb[s].sem, 1)
                            for s in range(2):
                                act.wait_ge(amT_ps[s].sem, amT_ps[s].at(t, 1))
                                nc.scalar.activation(amT[:, s, :], bank(s, 3)[:, 0:P], ACT.Copy).then_inc(amT_sb[s].sem, 1)
                            for s in range(2):
                                act.wait_ge(cT_ps[s].sem, cT_ps[s].at(t, 1))
                                act.wait_ge(film_ps[s].sem, film_ps[s].at(t, 0))
                                nc.scalar.activation(cT[:, s, :], bank(s, 3)[:, P:2 * P], ACT.Copy).then_inc(cT_sb[s].sem, 1)

                        act.wait_ge(zeroed.sem, zeroed.base + 1)
                        front(0)
                        weights(0)
                        with act.Fori(0, STEPS - 1) as t:
                            front(t + 1)
                            back(t)
                            weights(t + 1)
                        back(STEPS - 1)

                    @block.vector
                    def _(dve):
                        def carry(s):
                            nc.vector.tensor_copy(k.carry[:, 2 + s:3 + s], k.carry[:, 0:1])

                        def stage_x(t):
                            for s in range(2):
                                if not isinstance(t, int) or t:
                                    dve.wait_ge(xT_ps[s].sem, xT_ps[s].at(t, 0))
                                nc.vector.tensor_copy(xs[:, s, :], k.X[:, 2 * t + s, :]).then_inc(xs_sb[s].sem, 1)

                        def best(t, stage_next=True):
                            first = isinstance(t, int) and t == 0
                            for s in range(2):
                                dve.wait_ge(sc_ps[s].sem, sc_ps[s].at(t, 1))
                                if not first:
                                    dve.wait_ge(ex_sb[s].sem, ex_sb[s].at(t, 0))
                                    dve.wait_ge(sel_sb[s].sem, sel_sb[s].at(t, 0))
                                nc.vector.tensor_tensor(
                                    sc[:, s], bank(s, 2)[:].rearrange("p (h g) -> p h g", h=heads),
                                    key_bias[:, bass.ds(2 * t + s, 1), :].to_broadcast([P, heads, P]),
                                    ALU.add).then_inc(sc_sb[s].sem, 1)
                            if stage_next:
                                stage_x(t + 1)
                            source = sc
                            for r in range(rounds):
                                into = left[r % 2]
                                for s in range(2):
                                    if r == 0:
                                        dve.wait_ge(sc_sb[s].sem, sc_sb[s].at(t, 1))
                                        if not first:
                                            dve.wait_ge(den_sb[s].sem, den_sb[s].at(t, 0))
                                    else:
                                        dve.wait_ge(left_sb[s].sem, left_sb[s].at(t, r))
                                    carry(s)
                                    for h in range(heads):
                                        last = nc.vector.max(top[:, s, h, 8 * r:8 * r + 8], source[:, s, h, :])
                                    last.then_inc(top_sb[s].sem, 1)
                                for s in range(2):
                                    dve.wait_ge(top_sb[s].sem, top_sb[s].at(t, r + 1))
                                    if r == 0:
                                        nc.vector.tensor_scalar(nmax[:, s, :], top[:, s, :, 0], -scale, None,
                                                                ALU.mult).then_inc(nmax_sb[s].sem, 1)
                                    else:
                                        carry(s)
                                    for h in range(heads):
                                        last = nc.vector.match_replace(into[:, s, h, :], top[:, s, h, 8 * r:8 * r + 8],
                                                                       source[:, s, h, :], 2 * NEG)
                                    last.then_inc(left_sb[s].sem, 1)
                                source = into
                            for s in range(2):
                                dve.wait_ge(left_sb[s].sem, left_sb[s].at(t, rounds))
                                nc.vector.tensor_tensor(left[0][:, s], source[:, s], sc[:, s],
                                                        ALU.not_equal).then_inc(sel_sb[s].sem, 1)
                            for s in range(2):
                                dve.wait_ge(den_sb[s].sem, den_sb[s].at(t, 1))
                                nc.vector.reciprocal(rden[:, s, :], den[:, s, :]).then_inc(rden_sb[s].sem, 1)
                            for s in range(2):
                                dve.wait_ge(rden_sb[s].sem, rden_sb[s].at(t, 1))
                                dve.wait_ge(sel_sb[s].sem, sel_sb[s].at(t, 1))
                                dve.wait_ge(ex_sb[s].sem, ex_sb[s].at(t, 1))
                                if not first:
                                    dve.wait_ge(amT_ps[s].sem, amT_ps[s].at(t, 0))
                                for h in range(heads):
                                    last = nc.vector.scalar_tensor_tensor(
                                        out=pn[:, s, h, :], in0=ex[:, s, h, :], scalar=rden[:, s, h:h + 1],
                                        in1=left[0][:, s, h, :], op0=ALU.mult, op1=ALU.mult)
                                last.then_inc(pn_sb[s].sem, 1)

                        def normed(t):
                            for s in range(2):
                                dve.wait_ge(xb_sb[s].sem, xb_sb[s].at(t, 1))
                                nc.vector.bn_stats(st[:, s, :], xb[:, s, :]).then_inc(halves[s].sem, 1)
                            for s in range(2):
                                dve.wait_ge(halves[s].sem, halves[s].at(t, 1))
                                carry(s)
                                nc.vector.bn_aggr(mv[:, s, :], st[:, s, :]).then_inc(moments[s].sem, 1)
                            for s in range(2):
                                dve.wait_ge(moments[s].sem, moments[s].at(t, 1))
                                nc.vector.scalar_tensor_tensor(out=lg[:, s, :], in0=xb[:, s, :], scalar=mv[:, s, 0:1],
                                                               in1=k.w(name + "g_in"), op0=ALU.subtract,
                                                               op1=ALU.mult).then_inc(lg_sb[s].sem, 1)
                            for s in range(2):
                                dve.wait_ge(rstd[s].sem, rstd[s].at(t, 1))
                                dve.wait_ge(lg_sb[s].sem, lg_sb[s].at(t, 1))
                                dve.wait_ge(u_sb[s].sem, u_sb[s].at(t, 0))
                                nc.vector.scalar_tensor_tensor(out=ln[:, s, :], in0=lg[:, s, :], scalar=rs[:, s, 1:2],
                                                               in1=k.w(name + "b_in"), op0=ALU.mult,
                                                               op1=ALU.add).then_inc(ln_sb[s].sem, 1)
                            for s in range(2):
                                dve.wait_ge(film_ps[s].sem, film_ps[s].at(t, 1))
                                nc.vector.scalar_tensor_tensor(out=film[:, s, :], in0=bank(s, 1)[:],
                                                               scalar=gate[:, s, :], in1=film_bias[:], op0=ALU.mult,
                                                               op1=ALU.add).then_inc(film_sb[s].sem, 1)

                        nc.vector.memset(kT[:], 0.0).then_inc(zeroed.sem, 1)
                        stage_x(0)
                        best(0)
                        with dve.Fori(0, STEPS - 2) as t:
                            best(t + 1)
                            normed(t)
                        best(STEPS - 1, stage_next=False)
                        normed(STEPS - 2)
                        normed(STEPS - 1)

                    @block.tensor
                    def _(pe):
                        def front(t):
                            first = isinstance(t, int) and t == 0
                            for s in range(2):
                                pe.wait_ge(xs_sb[s].sem, xs_sb[s].at(t, 1))
                                if not first:
                                    pe.wait_ge(k_sb[s].sem, k_sb[s].at(t, 0))
                                nc.tensor.transpose(bank(s, 0)[:, 0:P], xs[:, s, :], k.w("ident")).then_inc(xT_ps[s].sem, 1)
                            for s in range(2):
                                pe.wait_ge(xT_sb[s].sem, xT_sb[s].at(t, 1))
                                nc.tensor.matmul(bank(s, 0)[:, P:2 * P], k.w(name + "Wq"), xT[:, s, :], start=True, stop=True)
                                nc.tensor.matmul(bank(s, 0)[:, 2 * P:3 * P], k.w(name + "Wk"), k.ctxT[:, 2 * t + s, :],
                                                 start=True, stop=True).then_inc(qk_ps[s].sem, 1)
                            for s in range(2):
                                pe.wait_ge(q_sb[s].sem, q_sb[s].at(t, 1))
                                pe.wait_ge(k_sb[s].sem, k_sb[s].at(t, 1))
                                if not first:
                                    pe.wait_ge(sc_sb[s].sem, sc_sb[s].at(t, 0))
                                nc.tensor.matmul(bank(s, 2)[:], qT[:, s, :], kT[:, s].rearrange("p h g -> p (h g)"),
                                                 start=True, stop=True).then_inc(sc_ps[s].sem, 1)

                        def back(t):
                            for s in range(2):
                                pe.wait_ge(cx_sb[s].sem, cx_sb[s].at(t, 1))
                                pe.wait_ge(cT_sb[s].sem, cT_sb[s].at(t, 0))
                                nc.tensor.matmul(bank(s, 3)[:, 2 * P:3 * P], cx[:, s, :], k.w(name + "Wv"),
                                                 start=True, stop=True).then_inc(v_ps[s].sem, 1)
                            for s in range(2):
                                pe.wait_ge(v_sb[s].sem, v_sb[s].at(t, 1))
                                pe.wait_ge(pn_sb[s].sem, pn_sb[s].at(t, 1))
                                for h in range(heads):
                                    last = nc.tensor.matmul(bank(s, 3)[:, 0:P], pn[:, s, h, :], k.w("ident"),
                                                            start=h == 0, stop=h == heads - 1)
                                last.then_inc(amT_ps[s].sem, 1)
                            for s in range(2):
                                pe.wait_ge(amT_sb[s].sem, amT_sb[s].at(t, 1))
                                nc.tensor.matmul(bank(s, 3)[:, P:2 * P], v[:, s, :], amT[:, s, :], start=True,
                                                 stop=True).then_inc(cT_ps[s].sem, 1)
                            for s in range(2):
                                pe.wait_ge(cT_sb[s].sem, cT_sb[s].at(t, 1))
                                pe.wait_ge(film_sb[s].sem, film_sb[s].at(t, 0))
                                nc.tensor.matmul(bank(s, 1)[:], cT[:, s, :], k.w(name + "W_film"), start=True,
                                                 stop=True).then_inc(film_ps[s].sem, 1)

                        front(0)
                        with pe.Fori(0, STEPS - 1) as t:
                            front(t + 1)
                            back(t)
                        back(STEPS - 1)

        with ExitStack() as ctx:
            CH = 16
            toeplitz = ctx.enter_context(nc.sbuf_tensor(f"{name}_toeplitz", [P, 2, CH, P], F32))
            toe_in = sig.pair("toeplitz_loaded", 16)
            flip_ps, flip_sb = sig.pair("flip_ps"), sig.pair("flip_sb")
            conv_ps, conv_sb = sig.pair("conv_ps"), sig.pair("conv_sb")
            tiles = bass.AP(tensor=kernel_dram, offset=0, ap=[[1, P], [2 * P, P], [1, P]])
            QUAD = 4

            with nc.Block() as block:

                @block.sync
                def _(sp):
                    for c in range(P // CH):
                        s, turn_of = c % 2, c // 2
                        if turn_of:
                            sp.wait_ge(conv_ps[s].sem, turn_of)
                        sp.dma_start(toeplitz[:, s], tiles[:, CH * c:CH * c + CH, :]).then_inc(toe_in[s].sem, 16)

                @block.scalar
                def _(act):
                    with act.Fori(0, NB // (2 * QUAD)) as t:
                        act.wait_ge(flip_ps[1].sem, flip_ps[1].at(t, 1))
                        nc.scalar.activation(UY[:, bass.ds(2 * QUAD * t + QUAD, QUAD), :],
                                             k.bank[4][:].rearrange("p (b d) -> p b d", b=QUAD),
                                             ACT.Copy).then_inc(flip_sb[1].sem, 1)
                    with act.Fori(0, P // (2 * CH)) as t:
                        act.wait_ge(conv_ps[1].sem, conv_ps[1].at(t, 1))
                        nc.scalar.activation(UY[:, :, bass.ds(2 * CH * t + CH, CH)],
                                             k.bank[5][:].rearrange("p (d b) -> p b d", b=NB),
                                             ACT.Copy).then_inc(conv_sb[1].sem, 1)

                @block.vector
                def _(dve):
                    with dve.Fori(0, NB // (2 * QUAD)) as t:
                        dve.wait_ge(flip_ps[0].sem, flip_ps[0].at(t, 1))
                        nc.vector.tensor_copy(UY[:, bass.ds(2 * QUAD * t, QUAD), :],
                                              k.bank[0][:].rearrange("p (b d) -> p b d", b=QUAD)
                                              ).then_inc(flip_sb[0].sem, 1)
                    with dve.Fori(0, P // (2 * CH)) as t:
                        dve.wait_ge(conv_ps[0].sem, conv_ps[0].at(t, 1))
                        nc.vector.tensor_copy(UY[:, :, bass.ds(2 * CH * t, CH)],
                                              k.bank[1][:].rearrange("p (d b) -> p b d", b=NB)
                                              ).then_inc(conv_sb[0].sem, 1)

                @block.tensor
                def _(pe):
                    with pe.Fori(0, NB // (2 * QUAD)) as t:
                        for s in range(2):
                            pe.wait_ge(flip_sb[s].sem, flip_sb[s].at(t, 0))
                            nc.tensor.matmul(k.bank[4 * s][:], k.w(name + "flip"),
                                             UY[:, bass.ds(2 * QUAD * t + QUAD * s, QUAD), :], start=True,
                                             stop=True).then_inc(flip_ps[s].sem, 1)
                    for s in range(2):
                        pe.wait_ge(flip_sb[s].sem, NB // (2 * QUAD))
                    with pe.Fori(0, P // (2 * CH)) as t:
                        for s in range(2):
                            pe.wait_ge(toe_in[s].sem, toe_in[s].at(t, 16))
                            pe.wait_ge(conv_sb[s].sem, conv_sb[s].at(t, 0))
                            for j in range(CH):
                                last = nc.tensor.matmul(k.bank[4 * s + 1][:, NB * j:NB * j + NB], toeplitz[:, s, j, :],
                                                        UY[:, :, bass.ds(2 * CH * t + (CH * s + j), 1)], start=True,
                                                        stop=True)
                            last.then_inc(conv_ps[s].sem, 1)

        with ExitStack() as ctx:
            def sb(what, shape, dt=F32):
                return ctx.enter_context(nc.sbuf_tensor(f"{name}_{what}", shape, dt))

            HC = 4
            hid_bank = [k.bank[i] for i in (1, 2, 5, 6)]
            y1, y2, xt = sb("y1", [P, 2, DM]), sb("y2", [P, 2, DM]), sb("xt", [P, 2, DM])
            xtb, res, hn = sb("xtb", [P, 2, DM]), sb("res", [P, 2, DM]), sb("hn", [P, 2, DM])
            hT = sb("hT", [P, 2, P])
            gh = sb("gh", [P, HC, 2, P])
            rg, lno = sb("rg", [P, 2, DM]), sb("lno", [P, 2, DM])
            st, mv, rs = sb("st_b", [P, 2, 2, 6]), sb("mv_b", [P, 2, 2, 2]), sb("rs_b", [P, 2, 2, 2])
            tail = Tail(k, ctx, name)
            y1_sb, y2_sb, xt_sb, xtb_sb = (sig.pair(n) for n in ("y1_sb", "y2_sb", "xt_sb", "xtb_sb"))
            h_halves, h_moments, h_var, h_rstd = (sig.pair(n, 2) for n in ("h_halves", "h_moments", "h_var", "h_rstd"))
            hn_sb, hT_ps, hT_sb = sig.pair("hn_sb"), sig.pair("hT_ps"), sig.pair("hT_sb")
            hid_ps, hid_sb = sig.ring("hid_ps", HC, 1), sig.ring("hid_sb", HC, 1)
            mlp_ps, res_sb, rg_sb, lno_sb = (sig.pair(n) for n in ("mlp_ps", "res_sb", "rg_sb", "lno_sb"))

            with nc.Block() as block:

                @block.sync
                def _(sp):
                    k.load_weights(sp, k.next_stage(stage))

                @block.gpsimd
                def _(pool):
                    def root(t, s, i):
                        pool.wait_ge(h_moments[s].sem, h_moments[s].at(t, i + 1))
                        nc.gpsimd.tensor_tensor(rs[:, s, i, 0:1], mv[:, s, i, 1:2], k.eps[:, 0:1],
                                                ALU.add).then_inc(h_var[s].sem, 1)
                        pool.wait_ge(h_var[s].sem, h_var[s].at(t, i + 1))
                        nc.gpsimd.tensor_tensor(rs[:, s, i, 1:2], rs[:, s, i, 0:1], k.neg_half[:, 0:1],
                                                ALU.pow).then_inc(h_rstd[s].sem, 1)

                    def modulate(t):
                        for s in range(2):
                            nc.gpsimd.tensor_tensor(y1[:, s, :], UY[:, 2 * t + s, :], FO[:, 2 * t + s, 0:DM],
                                                    ALU.mult).then_inc(y1_sb[s].sem, 1)
                        for s in range(2):
                            pool.wait_ge(y1_sb[s].sem, y1_sb[s].at(t, 1))
                            nc.gpsimd.tensor_tensor(y2[:, s, :], y1[:, s, :], FO[:, 2 * t + s, DM:2 * DM],
                                                    ALU.add).then_inc(y2_sb[s].sem, 1)
                        for s in range(2):
                            pool.wait_ge(y2_sb[s].sem, y2_sb[s].at(t, 1))
                            pool.wait_ge(hn_sb[s].sem, hn_sb[s].at(t, 0))
                            nc.gpsimd.tensor_tensor(xt[:, s, :], y2[:, s, :], k.X[:, 2 * t + s, :],
                                                    ALU.add).then_inc(xt_sb[s].sem, 1)
                    with pool.Fori(0, STEPS) as t:
                        modulate(t)
                        for s in range(2):
                            root(t, s, 0)
                        for s in range(2):
                            pool.wait_ge(xt_sb[s].sem, xt_sb[s].at(t, 1))
                            pool.wait_ge(res_sb[s].sem, res_sb[s].at(t, 0))
                            nc.gpsimd.tensor_tensor(xtb[:, s, :], xt[:, s, :], k.w(name + "b2"),
                                                    ALU.add).then_inc(xtb_sb[s].sem, 1)
                        for s in range(2):
                            root(t, s, 1)
                        for s in range(2):
                            tail.rstd(pool, t, s)

                @block.scalar
                def _(act):
                    with act.Fori(0, STEPS) as t:
                        for s in range(2):
                            act.wait_ge(hT_ps[s].sem, hT_ps[s].at(t, 1))
                            act.wait_ge(hid_ps[HC - 1].sem, hid_ps[HC - 1].at(t, 0))
                            nc.scalar.activation(hT[:, s, :], k.bank[4 * s][:, 0:P], ACT.Identity,
                                                 bias=k.w(name + "b_ffn"), scale=k.w(name + "g_ffn")
                                                 ).then_inc(hT_sb[s].sem, 1)
                        for c in range(HC):
                            act.wait_ge(hid_ps[c].sem, hid_ps[c].at(t, 1))
                            act.wait_ge(mlp_ps[1].sem, mlp_ps[1].at(t, 0))
                            nc.scalar.activation(gh[:, c].rearrange("p s t -> p (s t)"), hid_bank[c][:, 0:2 * P],
                                                 ACT.Gelu, bias=k.w(name + "b1")[:, c:c + 1]).then_inc(hid_sb[c].sem, 1)

                @block.vector
                def _(dve):
                    def moments_of(t, i, source, ready):
                        for s in range(2):
                            dve.wait_ge(ready[s].sem, ready[s].at(t, 1))
                            nc.vector.bn_stats(st[:, s, i, :], source[:, s, :]).then_inc(h_halves[s].sem, 1)
                        for s in range(2):
                            dve.wait_ge(h_halves[s].sem, h_halves[s].at(t, i + 1))
                            nc.vector.tensor_copy(k.carry[:, 2 + s:3 + s], k.carry[:, 0:1])
                            nc.vector.bn_aggr(mv[:, s, i, :], st[:, s, i, :]).then_inc(h_moments[s].sem, 1)

                    with dve.Fori(0, STEPS) as t:
                        moments_of(t, 0, xt, xt_sb)
                        for s in range(2):
                            dve.wait_ge(h_rstd[s].sem, h_rstd[s].at(t, 1))
                            dve.wait_ge(hT_ps[s].sem, hT_ps[s].at(t, 0))
                            nc.vector.tensor_scalar(hn[:, s, :], xt[:, s, :], mv[:, s, 0, 0:1], rs[:, s, 0, 1:2],
                                                    ALU.subtract, ALU.mult).then_inc(hn_sb[s].sem, 1)
                        for s in range(2):
                            dve.wait_ge(mlp_ps[s].sem, mlp_ps[s].at(t, 1))
                            dve.wait_ge(xtb_sb[s].sem, xtb_sb[s].at(t, 1))
                            nc.vector.tensor_tensor(res[:, s, :], k.bank[4 * s][:, P:2 * P], xtb[:, s, :],
                                                    ALU.add).then_inc(res_sb[s].sem, 1)
                        moments_of(t, 1, res, res_sb)
                        for s in range(2):
                            dve.wait_ge(h_moments[s].sem, h_moments[s].at(t, 2))
                            nc.vector.scalar_tensor_tensor(out=rg[:, s, :], in0=res[:, s, :], scalar=mv[:, s, 1, 0:1],
                                                           in1=k.w(name + "g_out"), op0=ALU.subtract,
                                                           op1=ALU.mult).then_inc(rg_sb[s].sem, 1)
                        for s in range(2):
                            dve.wait_ge(h_rstd[s].sem, h_rstd[s].at(t, 2))
                            dve.wait_ge(rg_sb[s].sem, rg_sb[s].at(t, 1))
                            nc.vector.scalar_tensor_tensor(out=lno[:, s, :], in0=rg[:, s, :], scalar=rs[:, s, 1, 1:2],
                                                           in1=k.w(name + "b_out"), op0=ALU.mult,
                                                           op1=ALU.add).then_inc(lno_sb[s].sem, 1)
                        for s in range(2):
                            dve.wait_ge(lno_sb[s].sem, lno_sb[s].at(t, 1))
                            dve.wait_ge(tail.written[s].sem, tail.written[s].at(t, 0))
                            nc.vector.tensor_tensor(tail.r[:, s, :], lno[:, s, :], k.X[:, 2 * t + s, :],
                                                    ALU.add).then_inc(tail.summed[s].sem, 1)
                        for s in range(2):
                            tail.stats(dve, t, s)
                        for s in range(2):
                            tail.apply(dve, t, s)

                @block.tensor
                def _(pe):
                    with pe.Fori(0, STEPS) as t:
                        for s in range(2):
                            pe.wait_ge(hn_sb[s].sem, hn_sb[s].at(t, 1))
                            pe.wait_ge(res_sb[s].sem, res_sb[s].at(t, 0))
                            nc.tensor.transpose(k.bank[4 * s][:, 0:P], hn[:, s, :], k.w("ident")).then_inc(hT_ps[s].sem, 1)
                        for s in range(2):
                            pe.wait_ge(hT_sb[s].sem, hT_sb[s].at(t, 1))
                        for c in range(HC):
                            pe.wait_ge(hid_sb[c].sem, hid_sb[c].at(t, 0))
                            nc.tensor.matmul(hid_bank[c][:, 0:2 * P], k.w(name + "W1")[:, P * c:P * c + P],
                                             hT[:].rearrange("p s t -> p (s t)"), start=True,
                                             stop=True).then_inc(hid_ps[c].sem, 1)
                        for s in range(2):
                            for c in range(HC):
                                pe.wait_ge(hid_sb[c].sem, hid_sb[c].at(t, 1))
                                last = nc.tensor.matmul(k.bank[4 * s][:, P:2 * P], gh[:, c, s, :],
                                                        k.w(name + "W2")[:, P * c:P * c + P], start=c == 0,
                                                        stop=c == HC - 1)
                            last.then_inc(mlp_ps[s].sem, 1)


def slots(k, stage, name):
    k.sig.new_stage(name)
    nc, sig = k.nc, k.sig
    with ExitStack() as ctx:
        def sb(what, shape, dt=F32):
            return ctx.enter_context(nc.sbuf_tensor(f"{name}_{what}", shape, dt))

        LG = sb("LG", [P, NB, NS])
        slot = sb("slot", [NS, DM])
        hsT = sb("hsT", [P, NS])
        mean = sb("mean", [P, 2])
        c1 = sb("c1", [NS, 1])
        gh = sb("gh", [P, 3, NS])
        tau = sb("tau", [P, 4])
        b2 = sb("b2", [P, NS])
        bsum = sb("bsum", [P, 3])
        step = sig.one("slots_step", 8, 1)
        slot_sb, hsT_ps, hsT_sb = (sig.one(n, 1, 1) for n in ("slot_sb", "slotT_ps", "slotT_sb"))
        mean_sb, setup_ps = sig.one("slot_mean", 1, 1), sig.one("slot_setup_ps", 1, 1)
        A, B = k.bank[0], k.bank[1]

        with nc.Block() as block:

            @block.vector
            def _(dve):
                n = [0]

                def link(ins):
                    n[0] += 1
                    ins.then_inc(step.sem, 1)
                    dve.wait_ge(step.sem, step.base + n[0])

                dve.wait_ge(k.loaded[stage], 16)
                nc.vector.tensor_scalar(slot[:], k.w(name + "slot_init"), k.w(name + "slot_scale"), None,
                                        ALU.mult).then_inc(slot_sb.sem, 1)
                link(nc.vector.tensor_scalar(tau[:, 2:3], k.w(name + "tau"), -1.0, None, ALU.mult))
                link(nc.vector.tensor_tensor(tau[:, 3:4], k.w(name + "tau"), tau[:, 2:3], ALU.max))
                link(nc.vector.tensor_scalar(tau[:, 0:1], tau[:, 3:4], 0.1, None, ALU.add))
                link(nc.vector.reciprocal(tau[:, 1:2], tau[:, 0:1]))
                nc.vector.tensor_scalar(b2[:], k.w(name + "b2"), tau[:, 1:2], None, ALU.mult)
                link(nc.vector.tensor_tensor(bsum[:], k.w(name + "bih"), k.w(name + "bhh"), ALU.add))
                dve.wait_ge(hsT_ps.sem, hsT_ps.base + 1)
                nc.vector.tensor_copy(hsT[:], A[:, 0:NS]).then_inc(hsT_sb.sem, 1)
                dve.wait_ge(hsT_sb.sem, hsT_sb.base + 1)
                link(nc.vector.tensor_reduce(mean[:, 0:1], hsT[:], AX.X, ALU.add))
                nc.vector.tensor_scalar(mean[:, 1:2], mean[:, 0:1], 1.0 / NS, None, ALU.mult).then_inc(mean_sb.sem, 1)
                dve.wait_ge(setup_ps.sem, setup_ps.base + 1)
                nc.vector.tensor_tensor(c1[:], B[0:NS, 3 * NS:3 * NS + 1], k.w(name + "b1"), ALU.add)
                for c in range(2):
                    nc.vector.tensor_scalar(gh[:, c, :], B[:, NS * c:NS * c + NS], bsum[:, c:c + 1], None, ALU.add)
                link(nc.vector.tensor_scalar(gh[:, 2, :], B[:, 2 * NS:3 * NS], k.w(name + "bhh")[:, 2:3], None, ALU.add))
                link(nc.vector.tensor_copy(k.carry[:, 1:2], k.carry[:, 0:1]))

            @block.tensor
            def _(pe):
                pe.wait_ge(slot_sb.sem, slot_sb.base + 1)
                nc.tensor.transpose(A[:, 0:NS], slot[:], k.w("ident")[0:NS, 0:NS]).then_inc(hsT_ps.sem, 1)
                pe.wait_ge(hsT_sb.sem, hsT_sb.base + 1)
                for c in range(3):
                    nc.tensor.matmul(B[:, NS * c:NS * c + NS], k.w(name + "whh")[:, P * c:P * c + P], hsT[:],
                                     start=True, stop=True)
                pe.wait_ge(mean_sb.sem, mean_sb.base + 1)
                nc.tensor.matmul(B[0:NS, 3 * NS:3 * NS + 1], k.w(name + "w1")[:, NS:2 * NS], mean[:, 1:2], start=True,
                                 stop=True).then_inc(setup_ps.sem, 1)

        xs = sb("xs", [P, 2, DM])
        xT = sb("xT", [P, 2, P])
        hT = sb("hT", [NS, 2, P])
        bank = lambda s, i: k.bank[4 * s + i]
        staged = sig.pair("staged")
        xT_ps, xT_sb = sig.pair("xT_ps"), sig.pair("xT_sb")
        hid_ps, hid_sb = sig.pair("hid_ps"), sig.pair("hid_sb")
        logits_ps, logits_sb = sig.pair("logits_ps"), sig.pair("logits_sb")

        with nc.Block() as block:

            @block.gpsimd
            def _(pool):
                with pool.Fori(0, STEPS) as t:
                    for s in range(2):
                        pool.wait_ge(xT_ps[s].sem, xT_ps[s].at(t, 0))
                        nc.gpsimd.tensor_copy(xs[:, s, :], k.X[:, 2 * t + s, :]).then_inc(staged[s].sem, 1)

            @block.scalar
            def _(act):
                with act.Fori(0, STEPS) as t:
                    for s in range(2):
                        act.wait_ge(xT_ps[s].sem, xT_ps[s].at(t, 1))
                        act.wait_ge(hid_ps[s].sem, hid_ps[s].at(t, 0))
                        nc.scalar.activation(xT[:, s, :], bank(s, 0)[:, 0:P], ACT.Copy).then_inc(xT_sb[s].sem, 1)
                    for s in range(2):
                        act.wait_ge(hid_ps[s].sem, hid_ps[s].at(t, 1))
                        nc.scalar.activation(hT[:, s, :], bank(s, 1)[0:NS, 0:P], ACT.Gelu,
                                             bias=c1[:]).then_inc(hid_sb[s].sem, 1)

            @block.vector
            def _(dve):
                with dve.Fori(0, STEPS) as t:
                    for s in range(2):
                        dve.wait_ge(logits_ps[s].sem, logits_ps[s].at(t, 1))
                        nc.vector.scalar_tensor_tensor(out=LG[:, 2 * t + s, :], in0=bank(s, 2)[:, 0:NS],
                                                       scalar=tau[:, 1:2], in1=b2[:], op0=ALU.mult,
                                                       op1=ALU.add).then_inc(logits_sb[s].sem, 1)

            @block.tensor
            def _(pe):
                with pe.Fori(0, STEPS) as t:
                    for s in range(2):
                        pe.wait_ge(staged[s].sem, staged[s].at(t, 1))
                        nc.tensor.transpose(bank(s, 0)[:, 0:P], xs[:, s, :], k.w("ident")).then_inc(xT_ps[s].sem, 1)
                    for s in range(2):
                        pe.wait_ge(xT_sb[s].sem, xT_sb[s].at(t, 1))
                        nc.tensor.matmul(bank(s, 1)[0:NS, 0:P], k.w(name + "w1")[:, 0:NS], xT[:, s, :], start=True,
                                         stop=True).then_inc(hid_ps[s].sem, 1)
                    for s in range(2):
                        pe.wait_ge(hid_sb[s].sem, hid_sb[s].at(t, 1))
                        pe.wait_ge(logits_sb[s].sem, logits_sb[s].at(t, 0))
                        nc.tensor.matmul(bank(s, 2)[:, 0:NS], hT[:, s, :], k.w(name + "w2"), start=True,
                                         stop=True).then_inc(logits_ps[s].sem, 1)

        x1 = sb("x1", [P, 2, DM + 1])
        lg = sb("lg", [P, 2, NS])
        top = sb("top", [P, 2, 8])
        left = sb("left", [P, 2, NS])
        sel = sb("sel", [P, 2, NS])
        stat = sb("stat", [P, 2, 4])
        etop = sb("etop", [P, 2, 8])
        ex = sb("ex", [P, 2, NS])
        alpha = sb("alpha", [P, 2, NS])
        wsum = sb("wsum", [NS, 2, 2])
        gi = sb("gi", [NS, 2, DM])
        giT = sb("giT", [P, 2, NS])
        alT = sb("alT", [NS, 2, P])
        rz = sb("rz", [P, 2, 2, NS])
        th = sb("th", [P, 2, 2, NS])
        sg = sb("sg", [P, 2, 2, NS])
        rh = sb("rh", [P, 2, NS])
        npre, nt = sb("npre", [P, 2, NS]), sb("nt", [P, 2, NS])
        dif, zd, hnew = sb("dif", [P, 2, NS]), sb("zd", [P, 2, NS]), sb("hnew", [P, 2, NS])
        sv = sb("sv", [NS, 2, DM])
        oT = sb("oT", [P, 2, P])
        xb = sb("xb", [P, 2, DM])
        tail = Tail(k, ctx, name)
        staged, xb_sb = sig.pair("staged"), sig.pair("xb_sb")
        top_sb, left_sb, sel_sb = sig.pair("top_sb"), sig.pair("left_sb"), sig.pair("sel_sb")
        nmax_sb, ex_sb, etop_sb, rsum_sb = (sig.pair(n) for n in ("nmax_sb", "ex_sb", "etop_sb", "rsum_sb"))
        alpha_sb = sig.pair("alpha_sb")
        in_ps, wsum_sb, rw_sb, gi_sb = (sig.pair(n) for n in ("slot_in_ps", "wsum_sb", "rwsum_sb", "gi_sb"))
        giT_ps, giT_sb, alT_ps, alT_sb = (sig.pair(n) for n in ("giT_ps", "giT_sb", "alphaT_ps", "alphaT_sb"))
        gx_ps, rz_sb, th_sb, sg_sb = (sig.pair(n) for n in ("gx_ps", "rz_sb", "tanh_sb", "sigmoid_sb"))
        rh_sb, npre_sb, nt_sb = (sig.pair(n) for n in ("rh_sb", "npre_sb", "n_sb"))
        dif_sb, zd_sb, hnew_sb = (sig.pair(n) for n in ("dif_sb", "zd_sb", "hnew_sb"))
        sv_ps, sv_sb, oT_ps, oT_sb, y_ps = (sig.pair(n) for n in ("sv_ps", "sv_sb", "oT_ps", "oT_sb", "y_ps"))
        ones_set = sig.one("ones_set", 1, 1)

        with nc.Block() as block:

            @block.sync
            def _(sp):
                k.load_weights(sp, k.next_stage(stage))

            @block.gpsimd
            def _(pool):
                nc.gpsimd.memset(x1[:], 1.0).then_inc(ones_set.sem, 1)
                pool.wait_ge(ones_set.sem, ones_set.base + 1)
                with pool.Fori(0, STEPS) as t:
                    for s in range(2):
                        pool.wait_ge(in_ps[s].sem, in_ps[s].at(t, 0))
                        pool.wait_ge(alpha_sb[s].sem, alpha_sb[s].at(t, 0))
                        nc.gpsimd.tensor_copy(lg[:, s, :], LG[:, 2 * t + s, :])
                        nc.gpsimd.tensor_copy(x1[:, s, 0:DM], k.X[:, 2 * t + s, :]).then_inc(staged[s].sem, 1)
                    for s in range(2):
                        pool.wait_ge(tail.summed[s].sem, tail.summed[s].at(t, 0))
                        pool.wait_ge(staged[s].sem, staged[s].at(t, 1))
                        nc.gpsimd.tensor_tensor(xb[:, s, :], x1[:, s, 0:DM], k.w(name + "bo"),
                                                ALU.add).then_inc(xb_sb[s].sem, 1)
                    for s in range(2):
                        pool.wait_ge(nt_sb[s].sem, nt_sb[s].at(t, 1))
                        nc.gpsimd.tensor_tensor(dif[:, s, :], hsT[:], nt[:, s, :], ALU.subtract).then_inc(dif_sb[s].sem, 1)
                        pool.wait_ge(dif_sb[s].sem, dif_sb[s].at(t, 1))
                        nc.gpsimd.tensor_tensor(zd[:, s, :], sg[:, s, 1, :], dif[:, s, :], ALU.mult).then_inc(zd_sb[s].sem, 1)
                        pool.wait_ge(zd_sb[s].sem, zd_sb[s].at(t, 1))
                        nc.gpsimd.tensor_tensor(hnew[:, s, :], nt[:, s, :], zd[:, s, :], ALU.add).then_inc(hnew_sb[s].sem, 1)
                    for s in range(2):
                        tail.rstd(pool, t, s)

            @block.scalar
            def _(act):
                with act.Fori(0, STEPS) as t:
                    for s in range(2):
                        act.wait_ge(nmax_sb[s].sem, nmax_sb[s].at(t, 1))
                        nc.scalar.activation(ex[:, s, :], lg[:, s, :], ACT.Exp, bias=stat[:, s, 0:1]).then_inc(ex_sb[s].sem, 1)
                        nc.scalar.activation(etop[:, s, :], top[:, s, :], ACT.Exp, bias=stat[:, s, 0:1],
                                             accum_out=stat[:, s, 1:2]).then_inc(etop_sb[s].sem, 1)
                    for s in range(2):
                        act.wait_ge(alT_ps[s].sem, alT_ps[s].at(t, 1))
                        nc.scalar.activation(alT[:, s, :], bank(s, 0)[0:NS, 0:P], ACT.Copy).then_inc(alT_sb[s].sem, 1)
                        act.wait_ge(giT_ps[s].sem, giT_ps[s].at(t, 1))
                        nc.scalar.activation(giT[:, s, :], bank(s, 1)[:, P:P + NS], ACT.Copy).then_inc(giT_sb[s].sem, 1)
                    for s in range(2):
                        act.wait_ge(rz_sb[s].sem, rz_sb[s].at(t, 1))
                        nc.scalar.activation(th[:, s], rz[:, s], ACT.Tanh, scale=0.5).then_inc(th_sb[s].sem, 1)
                    for s in range(2):
                        act.wait_ge(npre_sb[s].sem, npre_sb[s].at(t, 1))
                        nc.scalar.activation(nt[:, s, :], npre[:, s, :], ACT.Tanh).then_inc(nt_sb[s].sem, 1)
                    for s in range(2):
                        act.wait_ge(oT_ps[s].sem, oT_ps[s].at(t, 1))
                        nc.scalar.activation(oT[:, s, :], bank(s, 0)[:, P:2 * P], ACT.Copy).then_inc(oT_sb[s].sem, 1)

            @block.vector
            def _(dve):
                with dve.Fori(0, STEPS) as t:
                    for s in range(2):
                        dve.wait_ge(staged[s].sem, staged[s].at(t, 1))
                        nc.vector.tensor_copy(k.carry[:, 2 + s:3 + s], k.carry[:, 0:1])
                        nc.vector.max(top[:, s, :], lg[:, s, :]).then_inc(top_sb[s].sem, 1)
                    for s in range(2):
                        dve.wait_ge(top_sb[s].sem, top_sb[s].at(t, 1))
                        nc.vector.tensor_scalar(stat[:, s, 0:1], top[:, s, 0:1], -1.0, None,
                                                ALU.mult).then_inc(nmax_sb[s].sem, 1)
                        nc.vector.match_replace(left[:, s, :], top[:, s, :], lg[:, s, :], NEG).then_inc(left_sb[s].sem, 1)
                    for s in range(2):
                        dve.wait_ge(left_sb[s].sem, left_sb[s].at(t, 1))
                        nc.vector.tensor_tensor(sel[:, s, :], left[:, s, :], lg[:, s, :],
                                                ALU.not_equal).then_inc(sel_sb[s].sem, 1)
                        dve.wait_ge(etop_sb[s].sem, etop_sb[s].at(t, 1))
                        nc.vector.reciprocal(stat[:, s, 2:3], stat[:, s, 1:2]).then_inc(rsum_sb[s].sem, 1)
                    for s in range(2):
                        dve.wait_ge(rsum_sb[s].sem, rsum_sb[s].at(t, 1))
                        dve.wait_ge(sel_sb[s].sem, sel_sb[s].at(t, 1))
                        nc.vector.scalar_tensor_tensor(out=alpha[:, s, :], in0=ex[:, s, :], scalar=stat[:, s, 2:3],
                                                       in1=sel[:, s, :], op0=ALU.mult,
                                                       op1=ALU.mult).then_inc(alpha_sb[s].sem, 1)
                    for s in range(2):
                        dve.wait_ge(in_ps[s].sem, in_ps[s].at(t, 1))
                        nc.vector.tensor_scalar(wsum[:, s, 0:1], bank(s, 1)[0:NS, DM:DM + 1], 1e-8, None,
                                                ALU.add).then_inc(wsum_sb[s].sem, 1)
                        dve.wait_ge(wsum_sb[s].sem, wsum_sb[s].at(t, 1))
                        nc.vector.reciprocal(wsum[:, s, 1:2], wsum[:, s, 0:1]).then_inc(rw_sb[s].sem, 1)
                        dve.wait_ge(rw_sb[s].sem, rw_sb[s].at(t, 1))
                        nc.vector.tensor_scalar(gi[:, s, :], bank(s, 1)[0:NS, 0:DM], wsum[:, s, 1:2], None,
                                                ALU.mult).then_inc(gi_sb[s].sem, 1)
                    for s in range(2):
                        dve.wait_ge(gx_ps[s].sem, gx_ps[s].at(t, 1))
                        nc.vector.tensor_tensor(rz[:, s].rearrange("p a n -> p (a n)"), bank(s, 2)[:, 0:2 * NS],
                                                gh[:, 0:2].rearrange("p a n -> p (a n)"), ALU.add).then_inc(rz_sb[s].sem, 1)
                    for s in range(2):
                        dve.wait_ge(th_sb[s].sem, th_sb[s].at(t, 1))
                        nc.vector.tensor_scalar(sg[:, s], th[:, s], 0.5, 0.5, ALU.mult, ALU.add).then_inc(sg_sb[s].sem, 1)
                        dve.wait_ge(sg_sb[s].sem, sg_sb[s].at(t, 1))
                        nc.vector.tensor_tensor(rh[:, s, :], sg[:, s, 0, :], gh[:, 2, :], ALU.mult).then_inc(rh_sb[s].sem, 1)
                        dve.wait_ge(rh_sb[s].sem, rh_sb[s].at(t, 1))
                        nc.vector.scalar_tensor_tensor(out=npre[:, s, :], in0=bank(s, 2)[:, 2 * NS:3 * NS],
                                                       scalar=k.w(name + "bih")[:, 2:3], in1=rh[:, s, :], op0=ALU.add,
                                                       op1=ALU.add).then_inc(npre_sb[s].sem, 1)
                    for s in range(2):
                        dve.wait_ge(sv_ps[s].sem, sv_ps[s].at(t, 1))
                        nc.vector.tensor_tensor(sv[:, s, :], bank(s, 3)[0:NS, 0:DM], k.w(name + "bv"),
                                                ALU.add).then_inc(sv_sb[s].sem, 1)
                    for s in range(2):
                        dve.wait_ge(y_ps[s].sem, y_ps[s].at(t, 1))
                        dve.wait_ge(xb_sb[s].sem, xb_sb[s].at(t, 1))
                        dve.wait_ge(tail.written[s].sem, tail.written[s].at(t, 0))
                        nc.vector.tensor_tensor(tail.r[:, s, :], bank(s, 3)[:, P:2 * P], xb[:, s, :],
                                                ALU.add).then_inc(tail.summed[s].sem, 1)
                        tail.stats(dve, t, s)
                    for s in range(2):
                        tail.apply(dve, t, s)

            @block.tensor
            def _(pe):
                pe.wait_ge(ones_set.sem, ones_set.base + 1)
                with pe.Fori(0, STEPS) as t:
                    for s in range(2):
                        pe.wait_ge(alpha_sb[s].sem, alpha_sb[s].at(t, 1))
                        pe.wait_ge(giT_sb[s].sem, giT_sb[s].at(t, 0))
                        pe.wait_ge(oT_sb[s].sem, oT_sb[s].at(t, 0))
                        nc.tensor.matmul(bank(s, 1)[0:NS, 0:DM + 1], alpha[:, s, :], x1[:, s, :], start=True,
                                         stop=True).then_inc(in_ps[s].sem, 1)
                        nc.tensor.transpose(bank(s, 0)[0:NS, 0:P], alpha[:, s, :], k.w("ident")).then_inc(alT_ps[s].sem, 1)
                    for s in range(2):
                        pe.wait_ge(gi_sb[s].sem, gi_sb[s].at(t, 1))
                        nc.tensor.matmul(bank(s, 1)[:, P:P + NS], gi[:, s, :], k.w("ident")[0:NS, 0:NS], start=True,
                                         stop=True).then_inc(giT_ps[s].sem, 1)
                    for s in range(2):
                        pe.wait_ge(giT_sb[s].sem, giT_sb[s].at(t, 1))
                        pe.wait_ge(npre_sb[s].sem, npre_sb[s].at(t, 0))
                        for c in range(3):
                            last = nc.tensor.matmul(bank(s, 2)[:, NS * c:NS * c + NS], k.w(name + "wih")[:, P * c:P * c + P],
                                                    giT[:, s, :], start=True, stop=True)
                        last.then_inc(gx_ps[s].sem, 1)
                    for s in range(2):
                        pe.wait_ge(hnew_sb[s].sem, hnew_sb[s].at(t, 1))
                        pe.wait_ge(tail.summed[s].sem, tail.summed[s].at(t, 0))
                        nc.tensor.matmul(bank(s, 3)[0:NS, 0:DM], hnew[:, s, :], k.w(name + "wv"), start=True,
                                         stop=True).then_inc(sv_ps[s].sem, 1)
                    for s in range(2):
                        pe.wait_ge(sv_sb[s].sem, sv_sb[s].at(t, 1))
                        pe.wait_ge(alT_sb[s].sem, alT_sb[s].at(t, 1))
                        nc.tensor.matmul(bank(s, 0)[:, P:2 * P], sv[:, s, :], alT[:, s, :], start=True,
                                         stop=True).then_inc(oT_ps[s].sem, 1)
                    for s in range(2):
                        pe.wait_ge(oT_sb[s].sem, oT_sb[s].at(t, 1))
                        nc.tensor.matmul(bank(s, 3)[:, P:2 * P], oT[:, s, :], k.w(name + "wo"), start=True,
                                         stop=True).then_inc(y_ps[s].sem, 1)


def router(k, stage, name, source, XT, L, rms):
    k.sig.new_stage(name)
    nc, sig = k.nc, k.sig
    with ExitStack() as ctx:
        def sb(what, shape, dt=F32):
            return ctx.enter_context(nc.sbuf_tensor(f"{name}_r_{what}", shape, dt))

        xs = sb("xs", [P, 2, DM])
        xn = sb("xn", [P, 2, DM])
        sq = sb("sq", [P, 2, DM])
        ms = sb("ms", [P, 2, 4])
        xT = sb("xT", [P, 2, P])
        staged = sig.pair("staged")
        rms_in, rms_eps, rms_rs = sig.pair("rms_in"), sig.pair("rms_eps"), sig.pair("rms_rs")
        xn_sb = sig.pair("xn_sb")
        xT_ps, xT_sb = sig.pair("xT_ps"), sig.pair("xT_sb", 2)
        logits_ps, logits_sb = sig.pair("logits_ps"), sig.pair("logits_sb")
        if not rms:
            xn, xn_sb = xs, staged
        bank = lambda s, i: k.bank[4 * s + i]

        with nc.Block() as block:

            @block.gpsimd
            def _(pool):
                pool.wait_ge(k.loaded[stage], 16)
                with pool.Fori(0, STEPS) as t:
                    for s in range(2):
                        pool.wait_ge(xT_ps[s].sem, xT_ps[s].at(t, 0))
                        nc.gpsimd.tensor_copy(xs[:, s, :], source[:, 2 * t + s, :]).then_inc(staged[s].sem, 1)
                    for s in range(2):
                        if rms:
                            rms_root(k, pool, ms, s, t, rms_in, rms_eps, rms_rs)

            @block.scalar
            def _(act):
                with act.Fori(0, STEPS) as t:
                    for s in range(2):
                        if rms:
                            act.wait_ge(staged[s].sem, staged[s].at(t, 1))
                            nc.scalar.activation(sq[:, s, :], xs[:, s, :], ACT.Square, scale=DM ** -0.5,
                                                 accum_out=ms[:, s, 0:1]).then_inc(rms_in[s].sem, 1)
                    for s in range(2):
                        act.wait_ge(xT_ps[s].sem, xT_ps[s].at(t, 1))
                        act.wait_ge(logits_ps[s].sem, logits_ps[s].at(t, 0))
                        nc.scalar.activation(xT[:, s, :], bank(s, 0)[:, 0:P], ACT.Copy).then_inc(xT_sb[s].sem, 1)
                        nc.scalar.activation(XT[:, 2 * t + s, :], bank(s, 0)[:, 0:P], ACT.Copy).then_inc(xT_sb[s].sem, 1)

            @block.vector
            def _(dve):
                dve.wait_ge(k.loaded[stage], 16)
                with dve.Fori(0, STEPS) as t:
                    for s in range(2):
                        if rms:
                            dve.wait_ge(rms_rs[s].sem, rms_rs[s].at(t, 1))
                            nc.vector.scalar_tensor_tensor(
                                out=xn[:, s, :], in0=xs[:, s, :], scalar=ms[:, s, 2:3], in1=k.w(name + "ln2_w"),
                                op0=ALU.mult, op1=ALU.mult).then_inc(xn_sb[s].sem, 1)
                    for s in range(2):
                        dve.wait_ge(logits_ps[s].sem, logits_ps[s].at(t, 1))
                        if rms:
                            nc.vector.tensor_copy(L[:, 2 * t + s, :], bank(s, 1)[:, 0:NE]).then_inc(logits_sb[s].sem, 1)
                        else:
                            nc.vector.tensor_tensor(L[:, 2 * t + s, :], bank(s, 1)[:, 0:NE], k.w(name + "bg"),
                                                    ALU.add).then_inc(logits_sb[s].sem, 1)

            @block.tensor
            def _(pe):
                pe.wait_ge(k.loaded[stage], 16)
                with pe.Fori(0, STEPS) as t:
                    for s in range(2):
                        pe.wait_ge(xn_sb[s].sem, xn_sb[s].at(t, 1))
                        pe.wait_ge(xT_sb[s].sem, xT_sb[s].at(t, 0))
                        nc.tensor.transpose(bank(s, 0)[:, 0:P], xn[:, s, :], k.w("ident")).then_inc(xT_ps[s].sem, 1)
                    for s in range(2):
                        pe.wait_ge(xT_sb[s].sem, xT_sb[s].at(t, 1))
                        pe.wait_ge(logits_sb[s].sem, logits_sb[s].at(t, 0))
                        nc.tensor.matmul(bank(s, 1)[:, 0:NE], xT[:, s, :], k.w(name + ("Wr" if rms else "Wg")),
                                         start=True, stop=True).then_inc(logits_ps[s].sem, 1)


def top2(k, name, L, W):
    k.sig.new_stage(name)
    nc, sig = k.nc, k.sig
    with ExitStack() as ctx:
        def sb(what, shape, dt=F32):
            return ctx.enter_context(nc.sbuf_tensor(f"{name}_t_{what}", shape, dt))

        top = sb("top", [P, NB, 8])
        index = sb("index", [P, NB, 8], U32)
        place = sb("place", [P, NB, 2])
        second = sb("second", [P, NB, NE])
        e = sb("e", [P, 4, NB])
        found = sig.one("top_found", NB, 1)
        step = sig.one("top2_step", 8, 1)
        exp_in, exp_out = sig.one("top2_exp_in", 1, 1), sig.one("top2_exp_out", 1, 1)
        wide = lambda a: a.unsqueeze(2).to_broadcast([P, NB, NE])

        with nc.Block() as block:

            @block.scalar
            def _(act):
                act.wait_ge(exp_in.sem, exp_in.base + 1)
                nc.scalar.activation(e[:, 1, :], e[:, 0, :], ACT.Exp).then_inc(exp_out.sem, 1)

            @block.vector
            def _(dve):
                n = [0]

                def link(ins):
                    n[0] += 1
                    ins.then_inc(step.sem, 1)
                    dve.wait_ge(step.sem, step.base + n[0])

                for b in range(NB):
                    nc.vector.max(top[:, b, :], L[:, b, :]).then_inc(found.sem, 1)
                for b in range(NB):
                    dve.wait_ge(found.sem, found.base + b + 1)
                    last = nc.vector.max_index(index[:, b, :], top[:, b, :], L[:, b, :])
                nc.vector.tensor_tensor(e[:, 0, :], top[:, :, 1], top[:, :, 0], ALU.subtract).then_inc(exp_in.sem, 1)
                link(last)
                link(nc.vector.tensor_copy(place[:], index[:, :, 0:2]))
                iota = k.w("iota8").rearrange("p (b e) -> p b e", e=NE)
                link(nc.vector.tensor_tensor(W[:], iota, wide(place[:, :, 0]), ALU.is_equal))
                link(nc.vector.tensor_tensor(second[:], iota, wide(place[:, :, 1]), ALU.is_equal))
                dve.wait_ge(exp_out.sem, exp_out.base + 1)
                nc.vector.tensor_tensor(second[:], second[:], wide(e[:, 1, :]), ALU.mult)
                link(nc.vector.tensor_scalar(e[:, 2, :], e[:, 1, :], 1.0, None, ALU.add))
                link(nc.vector.tensor_tensor(W[:], W[:], second[:], ALU.add))
                link(nc.vector.reciprocal(e[:, 3, :], e[:, 2, :]))
                link(nc.vector.tensor_tensor(W[:], W[:], wide(e[:, 3, :]), ALU.mult))


def weighted_sum_pool(k, pool, t, s, prod, half, quarter, moe, prod_sb, steps, moe_sb):
    nc = k.nc
    pool.wait_ge(prod_sb[s].sem, prod_sb[s].at(t, 2))
    nc.gpsimd.tensor_tensor(half[:, s], prod[:, s, 0:4, :], prod[:, s, 4:8, :], ALU.add).then_inc(steps[s].sem, 1)
    pool.wait_ge(steps[s].sem, steps[s].at(t, 1))
    nc.gpsimd.tensor_tensor(quarter[:, s], half[:, s, 0:2, :], half[:, s, 2:4, :], ALU.add).then_inc(steps[s].sem, 1)
    pool.wait_ge(steps[s].sem, steps[s].at(t, 2))
    nc.gpsimd.tensor_tensor(moe[:, s, :], quarter[:, s, 0, :], quarter[:, s, 1, :],
                            ALU.add).then_inc(moe_sb[s].sem, 1)


def experts_gated(k, stage, name, M, HT, W):
    k.sig.new_stage(name)
    nc, sig = k.nc, k.sig
    with ExitStack() as ctx:
        def sb(what, shape, dt=F32):
            return ctx.enter_context(nc.sbuf_tensor(f"{name}_e_{what}", shape, dt))

        sg = sb("sg", [P, 2, 512])
        a = sb("a", [P, 2, 2, 2, P])
        prod = sb("prod", [P, 2, NE, DM])
        half, quarter = sb("half", [P, 2, 4, DM]), sb("quarter", [P, 2, 2, DM])
        moe = sb("moe", [P, 2, DM])
        m = sb("m", [P, 2, 2, DM])
        tail = Tail(k, ctx, name + "e_")
        gate, up = k.bank[0:2], k.bank[2:4]
        Y = [k.bank[4:6], k.bank[6:8]]

        gu_ps = sig.ring("gate_up_ps", 2, NE // 2)
        sg_sb = sig.ring("silu_sb", 2, NE // 2)
        a_sb = sig.ring("act_sb", 2, NE // 2)
        y_ps = sig.one("experts_ps", NE, STEPS)
        prod_sb = sig.pair("prod_sb", 2)
        pool_sum = sig.pair("pool_sum", 2)
        moe_sb = sig.pair("moe_sb")
        mid_sum, clipped = sig.pair("mid_sum"), sig.pair("mid_clipped")

        with nc.Block() as block:

            @block.sync
            def _(sp):
                k.load_weights(sp, k.next_stage(stage))

            @block.gpsimd
            def _(pool):
                with pool.Fori(0, STEPS) as t:
                    for s in range(2):
                        weighted_sum_pool(k, pool, t, s, prod, half, quarter, moe, prod_sb, pool_sum, moe_sb)
                    for s in range(2):
                        tail.rstd(pool, t, s)

            @block.scalar
            def _(act):
                with act.Fori(0, STEPS) as t:
                    for e in range(NE):
                        b, n = e % 2, e // 2
                        act.wait_ge(gu_ps[b].sem, gu_ps[b].at(t, n + 1))
                        act.wait_ge(a_sb[b].sem, a_sb[b].at(t, n))
                        nc.scalar.activation(sg[:, b, :], gate[b][:], ACT.Silu).then_inc(sg_sb[b].sem, 1)

            @block.vector
            def _(dve):
                with dve.Fori(0, STEPS) as t:
                    for e in range(NE):
                        b, n = e % 2, e // 2
                        dve.wait_ge(sg_sb[b].sem, sg_sb[b].at(t, n + 1))
                        dve.wait_ge(y_ps.sem, y_ps.at(t, e - 1 if e >= 2 else 0))
                        nc.vector.tensor_tensor(a[:, b].rearrange("p c s q -> p (c s q)"), sg[:, b, :], up[b][:],
                                                ALU.mult).then_inc(a_sb[b].sem, 1)
                    for s in range(2):
                        dve.wait_ge(moe_sb[s].sem, moe_sb[s].at(t, 0))
                        dve.wait_ge(y_ps.sem, y_ps.at(t, NE))
                        for i in range(2):
                            nc.vector.tensor_tensor(
                                prod[:, s, 4 * i:4 * i + 4, :], Y[s][i][:].rearrange("p (e d) -> p e d", d=DM),
                                W[:, 2 * t + s, 4 * i:4 * i + 4].unsqueeze(2).to_broadcast([P, 4, DM]),
                                ALU.mult).then_inc(prod_sb[s].sem, 1)
                    for s in range(2):
                        dve.wait_ge(moe_sb[s].sem, moe_sb[s].at(t, 1))
                        nc.vector.tensor_tensor(m[:, s, 0, :], moe[:, s, :], M[:, 2 * t + s, :],
                                                ALU.add).then_inc(mid_sum[s].sem, 1)
                        dve.wait_ge(mid_sum[s].sem, mid_sum[s].at(t, 1))
                        nc.vector.tensor_scalar(m[:, s, 1, :], m[:, s, 0, :], -100.0, 100.0, ALU.max,
                                                ALU.min).then_inc(clipped[s].sem, 1)
                        dve.wait_ge(clipped[s].sem, clipped[s].at(t, 1))
                        nc.vector.tensor_tensor(tail.r[:, s, :], m[:, s, 1, :], k.X[:, 2 * t + s, :],
                                                ALU.add).then_inc(tail.summed[s].sem, 1)
                        tail.stats(dve, t, s)
                    for s in range(2):
                        tail.apply(dve, t, s)

            @block.tensor
            def _(pe):
                with pe.Fori(0, STEPS) as t:

                    def down(e):
                        b, n = e % 2, e // 2
                        pe.wait_ge(a_sb[b].sem, a_sb[b].at(t, n + 1))
                        if e % 4 == 0:
                            for s in range(2):
                                pe.wait_ge(prod_sb[s].sem, prod_sb[s].at(t, 0))
                        for s in range(2):
                            for c in range(2):
                                last = nc.tensor.matmul(
                                    Y[s][e // 4][:, P * (e % 4):P * (e % 4) + P], a[:, b, c, s, :],
                                    k.w(name + "Wd")[:, P * (2 * e + c):P * (2 * e + c) + P],
                                    start=c == 0, stop=c == 1, skip_group_check=True)
                        last.then_inc(y_ps.sem, 1)

                    for e in range(NE):
                        b, n = e % 2, e // 2
                        pe.wait_ge(a_sb[b].sem, a_sb[b].at(t, n))
                        hT = HT[:, bass.ts(t, 2), :].rearrange("p s q -> p (s q)")
                        for bank, w in ((gate, "Wg"), (up, "Wu")):
                            for c in range(2):
                                o = 2 * P * e + P * c
                                last = nc.tensor.matmul(bank[b][:, 256 * c:256 * c + 256], k.w(name + w)[:, o:o + P],
                                                        hT, start=True, stop=True)
                        last.then_inc(gu_ps[b].sem, 1)
                        if e >= 1:
                            down(e - 1)
                    down(NE - 1)


def experts_linear(k, stage, name, XT, W):
    k.sig.new_stage(name)
    nc, sig = k.nc, k.sig
    with ExitStack() as ctx:
        def sb(what, shape, dt=F32):
            return ctx.enter_context(nc.sbuf_tensor(f"{name}_e_{what}", shape, dt))

        xT = sb("xT", [P, 2, P])
        ws = sb("ws", [P, 2, NE])
        wT = sb("wT", [NE, 2, P])
        prod = sb("prod", [P, 2, NE, DM])
        half, quarter = sb("half", [P, 2, 4, DM]), sb("quarter", [P, 2, 2, DM])
        moe = sb("moe", [P, 2, DM])
        xb = sb("xb", [P, 2, DM])
        tail = Tail(k, ctx, name)
        bank = lambda s, i: k.bank[4 * s + i]
        staged = sig.pair("staged")
        wT_ps, wT_sb = sig.pair("wT_ps"), sig.pair("wT_sb")
        bias_ps, xb_sb = sig.pair("bias_ps"), sig.pair("xb_sb")
        y_ps = sig.pair("y_ps")
        prod_sb = sig.pair("prod_sb", 2)
        pool_sum = sig.pair("pool_sum", 2)
        moe_sb = sig.pair("moe_sb")

        with nc.Block() as block:

            @block.sync
            def _(sp):
                k.load_weights(sp, k.next_stage(stage))

            @block.gpsimd
            def _(pool):
                with pool.Fori(0, STEPS) as t:
                    for s in range(2):
                        pool.wait_ge(y_ps[s].sem, y_ps[s].at(t, 0))
                        nc.gpsimd.tensor_copy(ws[:, s, :], W[:, 2 * t + s, :])
                        nc.gpsimd.tensor_copy(xT[:, s, :], XT[:, 2 * t + s, :]).then_inc(staged[s].sem, 1)
                    for s in range(2):
                        weighted_sum_pool(k, pool, t, s, prod, half, quarter, moe, prod_sb, pool_sum, moe_sb)
                    for s in range(2):
                        tail.rstd(pool, t, s)

            @block.scalar
            def _(act):
                with act.Fori(0, STEPS) as t:
                    for s in range(2):
                        act.wait_ge(wT_ps[s].sem, wT_ps[s].at(t, 1))
                        nc.scalar.activation(wT[:, s, :], bank(s, 0)[0:NE, 0:P], ACT.Copy).then_inc(wT_sb[s].sem, 1)

            @block.vector
            def _(dve):
                with dve.Fori(0, STEPS) as t:
                    for s in range(2):
                        dve.wait_ge(bias_ps[s].sem, bias_ps[s].at(t, 1))
                        nc.vector.tensor_tensor(xb[:, s, :], bank(s, 1)[:, 0:DM], k.X[:, 2 * t + s, :],
                                                ALU.add).then_inc(xb_sb[s].sem, 1)
                        dve.wait_ge(y_ps[s].sem, y_ps[s].at(t, 1))
                        dve.wait_ge(moe_sb[s].sem, moe_sb[s].at(t, 0))
                        for i in range(2):
                            nc.vector.tensor_tensor(
                                prod[:, s, 4 * i:4 * i + 4, :], bank(s, 2 + i)[:].rearrange("p (e d) -> p e d", d=DM),
                                W[:, 2 * t + s, 4 * i:4 * i + 4].unsqueeze(2).to_broadcast([P, 4, DM]),
                                ALU.mult).then_inc(prod_sb[s].sem, 1)
                    for s in range(2):
                        dve.wait_ge(moe_sb[s].sem, moe_sb[s].at(t, 1))
                        nc.vector.tensor_tensor(tail.r[:, s, :], moe[:, s, :], xb[:, s, :],
                                                ALU.add).then_inc(tail.summed[s].sem, 1)
                        tail.stats(dve, t, s)
                    for s in range(2):
                        tail.apply(dve, t, s)

            @block.tensor
            def _(pe):
                with pe.Fori(0, STEPS) as t:
                    for s in range(2):
                        pe.wait_ge(staged[s].sem, staged[s].at(t, 1))
                        pe.wait_ge(wT_sb[s].sem, wT_sb[s].at(t, 0))
                        nc.tensor.transpose(bank(s, 0)[0:NE, 0:P], ws[:, s, :], k.w("ident")).then_inc(wT_ps[s].sem, 1)
                    for s in range(2):
                        pe.wait_ge(prod_sb[s].sem, prod_sb[s].at(t, 0))
                        for i in range(2):
                            last = nc.tensor.matmul(bank(s, 2 + i)[:], xT[:, s, :],
                                                    k.w(name + "We")[:, 512 * i:512 * i + 512], start=True, stop=True)
                        last.then_inc(y_ps[s].sem, 1)
                        pe.wait_ge(wT_sb[s].sem, wT_sb[s].at(t, 1))
                        pe.wait_ge(xb_sb[s].sem, xb_sb[s].at(t, 0))
                        nc.tensor.matmul(bank(s, 1)[:, 0:DM], wT[:, s, :], k.w(name + "be"), start=True,
                                         stop=True).then_inc(bias_ps[s].sem, 1)


def sequence_gates(k, stage, name, XT, G):
    k.sig.new_stage(name)
    nc, sig = k.nc, k.sig
    with ExitStack() as ctx:
        def sb(what, shape, dt=F32):
            return ctx.enter_context(nc.sbuf_tensor(f"{name}_g_{what}", shape, dt))

        xs = sb("xs", [P, 2, DM])
        total = sb("total", [P, NB])
        pooled = sb("pooled", [P, NB])
        lg = sb("lg", [NB, NE])
        top = sb("top", [NB, 8])
        keep = sb("keep", [NB, NE])
        d = sb("d", [NB, NE])
        ex = sb("ex", [NB, NE])
        gate = sb("gate", [NB, NE])
        den = sb("den", [NB, 2])
        diag = sb("diag", [NB, NB, NE])
        staged = sig.pair("staged")
        xT_ps, xT_sb = sig.pair("xT_ps"), sig.pair("xT_sb")
        step = sig.one("gates_step", 9, 1)
        pooled_sb, lg_ps = sig.one("pooled_sb", 1, 1), sig.one("gate_logits_ps", 1, 1)
        exp_in, exp_out = sig.one("gates_exp_in", 1, 1), sig.one("gates_exp_out", 1, 1)
        diag_sb, spread_ps = sig.one("gates_diag", 1, 1), sig.one("gates_spread", 1, 1)

        with nc.Block() as block:

            @block.gpsimd
            def _(pool):
                with pool.Fori(0, STEPS) as t:
                    for s in range(2):
                        pool.wait_ge(xT_ps[s].sem, xT_ps[s].at(t, 0))
                        nc.gpsimd.tensor_copy(xs[:, s, :], k.X[:, 2 * t + s, :]).then_inc(staged[s].sem, 1)

            @block.scalar
            def _(act):
                with act.Fori(0, STEPS) as t:
                    for s in range(2):
                        act.wait_ge(xT_ps[s].sem, xT_ps[s].at(t, 1))
                        nc.scalar.activation(XT[:, 2 * t + s, :], k.bank[s][:, 0:P], ACT.Copy).then_inc(xT_sb[s].sem, 1)
                act.wait_ge(exp_in.sem, exp_in.base + 1)
                nc.scalar.activation(ex[:], d[:], ACT.Exp).then_inc(exp_out.sem, 1)

            @block.vector
            def _(dve):
                n = [0]

                def link(ins):
                    n[0] += 1
                    ins.then_inc(step.sem, 1)
                    dve.wait_ge(step.sem, step.base + n[0])

                dve.wait_ge(k.loaded[stage], 16)
                for s in range(2):
                    dve.wait_ge(xT_sb[s].sem, xT_sb[s].base + STEPS)
                link(nc.vector.tensor_reduce(total[:], XT[:], AX.X, ALU.add))
                nc.vector.tensor_scalar(pooled[:], total[:], 1.0 / P, None, ALU.mult).then_inc(pooled_sb.sem, 1)
                dve.wait_ge(lg_ps.sem, lg_ps.base + 1)
                link(nc.vector.tensor_tensor(lg[:], k.bank[2][0:NB, 0:NE], k.w(name + "gate_b")[0:NB, :], ALU.add))
                link(nc.vector.max(top[:], lg[:]))
                link(nc.vector.tensor_scalar(keep[:], lg[:], top[:, 1:2], None, ALU.is_ge))
                nc.vector.tensor_scalar(d[:], lg[:], top[:, 0:1], None, ALU.subtract).then_inc(exp_in.sem, 1)
                dve.wait_ge(exp_out.sem, exp_out.base + 1)
                link(nc.vector.tensor_tensor(lg[:], ex[:], keep[:], ALU.mult))
                link(nc.vector.tensor_reduce(den[:, 0:1], lg[:], AX.X, ALU.add))
                link(nc.vector.reciprocal(den[:, 1:2], den[:, 0:1]))
                link(nc.vector.tensor_scalar(gate[:], lg[:], den[:, 1:2], None, ALU.mult))
                nc.vector.tensor_tensor(diag[:], gate[:].unsqueeze(1).to_broadcast([NB, NB, NE]),
                                        k.w("ident")[0:NB, 0:NB].unsqueeze(2).to_broadcast([NB, NB, NE]),
                                        ALU.mult).then_inc(diag_sb.sem, 1)
                dve.wait_ge(spread_ps.sem, spread_ps.base + 1)
                link(nc.vector.tensor_copy(G[:].rearrange("p b e -> p (b e)"), k.bank[3][:, 0:NB * NE]))

            @block.tensor
            def _(pe):
                with pe.Fori(0, STEPS) as t:
                    for s in range(2):
                        pe.wait_ge(staged[s].sem, staged[s].at(t, 1))
                        pe.wait_ge(xT_sb[s].sem, xT_sb[s].at(t, 0))
                        nc.tensor.transpose(k.bank[s][:, 0:P], xs[:, s, :], k.w("ident")).then_inc(xT_ps[s].sem, 1)
                pe.wait_ge(k.loaded[stage], 16)
                pe.wait_ge(pooled_sb.sem, pooled_sb.base + 1)
                nc.tensor.matmul(k.bank[2][0:NB, 0:NE], pooled[:], k.w(name + "gate_w"), start=True,
                                 stop=True).then_inc(lg_ps.sem, 1)
                pe.wait_ge(diag_sb.sem, diag_sb.base + 1)
                nc.tensor.matmul(k.bank[3][:, 0:NB * NE], k.w("ones")[0:NB, :], diag[:].rearrange("p b e -> p (b e)"),
                                 start=True, stop=True).then_inc(spread_ps.sem, 1)


def experts_gelu(k, stage, name, XT, G):
    k.sig.new_stage(name)
    nc, sig = k.nc, k.sig
    with ExitStack() as ctx:
        def sb(what, shape, dt=F32):
            return ctx.enter_context(nc.sbuf_tensor(f"{name}_e_{what}", shape, dt))

        ge = sb("ge", [P, 2, NE, 2, P])
        gI = sb("gI", [P, 2, NE, P])
        tail = Tail(k, ctx, name)
        Z = k.bank[0:4]
        Y = k.bank[4:6]
        z_ps = sig.ring("expert_ps", 4, 1)
        ge_sb = sig.ring("gelu_sb", 4, 2)
        gI_sb = sig.pair("gate_diag_sb")
        y_ps = sig.pair("y_ps")

        with nc.Block() as block:

            @block.sync
            def _(sp):
                k.load_weights(sp, k.next_stage(stage))

            @block.gpsimd
            def _(pool):
                with pool.Fori(0, STEPS) as t:
                    for s in range(2):
                        pool.wait_ge(y_ps[s].sem, y_ps[s].at(t, 0))
                        nc.gpsimd.tensor_tensor(
                            gI[:, s], k.w("ident").unsqueeze(1).to_broadcast([P, NE, P]),
                            G[:, 2 * t + s, :].unsqueeze(2).to_broadcast([P, NE, P]), ALU.mult).then_inc(gI_sb[s].sem, 1)
                    for s in range(2):
                        tail.rstd(pool, t, s)

            @block.scalar
            def _(act):
                with act.Fori(0, STEPS) as t:
                    act.wait_ge(y_ps[1].sem, y_ps[1].at(t, 0))
                    for e in range(NE):
                        act.wait_ge(z_ps[e // 2].sem, z_ps[e // 2].at(t, 1))
                        nc.scalar.activation(ge[:, 0, e].rearrange("p s q -> p (s q)"),
                                             Z[e // 2][:, 256 * (e % 2):256 * (e % 2) + 256], ACT.Gelu,
                                             bias=k.w(name + "expert_b")[:, e:e + 1]).then_inc(ge_sb[e // 2].sem, 1)

            @block.vector
            def _(dve):
                with dve.Fori(0, STEPS) as t:
                    for s in range(2):
                        dve.wait_ge(y_ps[s].sem, y_ps[s].at(t, 1))
                        dve.wait_ge(tail.written[s].sem, tail.written[s].at(t, 0))
                        nc.vector.tensor_tensor(tail.r[:, s, :], Y[s][:, 0:DM], k.X[:, 2 * t + s, :],
                                                ALU.add).then_inc(tail.summed[s].sem, 1)
                        tail.stats(dve, t, s)
                    for s in range(2):
                        tail.apply(dve, t, s)

            @block.tensor
            def _(pe):
                with pe.Fori(0, STEPS) as t:
                    for e in range(NE):
                        if e % 2 == 0:
                            pe.wait_ge(ge_sb[e // 2].sem, ge_sb[e // 2].at(t, 0))
                        last = nc.tensor.matmul(Z[e // 2][:, 256 * (e % 2):256 * (e % 2) + 256],
                                                k.w(name + "expert_w")[:, P * e:P * e + P],
                                                XT[:, bass.ts(t, 2), :].rearrange("p s q -> p (s q)"),
                                                start=True, stop=True)
                        if e % 2 == 1:
                            last.then_inc(z_ps[e // 2].sem, 1)
                    for s in range(2):
                        pe.wait_ge(gI_sb[s].sem, gI_sb[s].at(t, 1))
                        pe.wait_ge(tail.summed[s].sem, tail.summed[s].at(t, 0))
                        for e in range(NE):
                            if s == 0 and e % 2 == 0:
                                pe.wait_ge(ge_sb[e // 2].sem, ge_sb[e // 2].at(t, 2))
                            last = nc.tensor.matmul(Y[s][:, 0:DM], ge[:, 0, e, s, :], gI[:, s, e, :], start=e == 0,
                                                    stop=e == NE - 1)
                        last.then_inc(y_ps[s].sem, 1)


def build(nc, table, pack, x, ctxT, masks, out):
    with ExitStack() as ctx:
        k = Kernel(nc, ctx, table, pack, x, ctxT, masks, out)
        load_stage(k)
        if 0 in STAGES:
            attention8(k, 0, "L0_attn_", bias=True)
        if 1 in STAGES:
            film_conv(k, 1, "L0_xattn_")
        if 2 in STAGES:
            slots(k, 2, "L0_ffn_")
        if 3 in STAGES:
            attention_linear(k, 3, "L1_attn_")
        if 4 in STAGES:
            attention64(k, 4, "L1_xattn_", heads=8, cross=True)
        if 5 in STAGES:
            with ExitStack() as mid:
                M = mid.enter_context(nc.sbuf_tensor("L1_ffn_mid", [P, NB, DM], F32))
                attention8(k, 5, "L1_ffn_", grouped=M)
                HT = mid.enter_context(nc.sbuf_tensor("L1_ffn_hT", [P, NB, P], F32))
                L = mid.enter_context(nc.sbuf_tensor("L1_ffn_L", [P, NB, NE], F32))
                W = mid.enter_context(nc.sbuf_tensor("L1_ffn_W", [P, NB, NE], F32))
                router(k, 5.5, "L1_ffn_", M, HT, L, rms=True)
                top2(k, "L1_ffn_", L, W)
                experts_gated(k, 5.5, "L1_ffn_", M, HT, W)
        if 6 in STAGES:
            attention_relu(k, 6, "L2_attn_")
        if 7 in STAGES:
            attention8(k, 7, "L2_xattn_", cross=True, mlp=True)
        if 8 in STAGES:
            with ExitStack() as mid:
                XT = mid.enter_context(nc.sbuf_tensor("L2_ffn_xT", [P, NB, P], F32))
                L = mid.enter_context(nc.sbuf_tensor("L2_ffn_L", [P, NB, NE], F32))
                W = mid.enter_context(nc.sbuf_tensor("L2_ffn_W", [P, NB, NE], F32))
                router(k, 8, "L2_ffn_", k.X, XT, L, rms=False)
                top2(k, "L2_ffn_", L, W)
                experts_linear(k, 8, "L2_ffn_", XT, W)
        if 9 in STAGES:
            attention64(k, 9, "L3_attn_", heads=16, rope=True)
        if 10 in STAGES:
            attention8(k, 10, "L3_xattn_", cross=True)
        if 11 in STAGES:
            with ExitStack() as mid:
                XT = mid.enter_context(nc.sbuf_tensor("L3_ffn_xT", [P, NB, P], F32))
                G = mid.enter_context(nc.sbuf_tensor("L3_ffn_G", [P, NB, NE], F32))
                sequence_gates(k, 11, "L3_ffn_", XT, G)
                experts_gelu(k, 11, "L3_ffn_", XT, G)
        store_stage(k)


def kernel(**inputs):
    import concourse.bacc as bacc
    from concourse.bass_utils import run_bass_kernel_spmd

    parts = host_pack(inputs)
    table = [(s, n, a.shape[0], a.shape[1]) for s, n, a in parts]
    cols = [np.concatenate([a, np.zeros((P - a.shape[0], a.shape[1]), a.dtype)], 0) if a.shape[0] < P else a
            for _, _, a in parts]
    arrays = {
        "pack": np.ascontiguousarray(np.concatenate(cols, 1)),
        "x_in": np.ascontiguousarray(inputs["x"]),
        "ctxT_in": np.ascontiguousarray(np.asarray(inputs["ctx_768"]).transpose(2, 0, 1)),
        "mask_text": np.ascontiguousarray(np.asarray(inputs["mask_BxS_bf1"]).view(np.uint8).T),
        "mask_keys": np.ascontiguousarray(np.broadcast_to(
            np.asarray(inputs["mask_BxS2_bf1"]).view(np.uint8).reshape(1, NB, P), (P, NB, P))),
    }
    nc = bacc.Bacc("TRN2", target_bir_lowering=False, num_devices=1)
    d = {n: nc.dram_tensor(n, a.shape, mybir.dt.from_np(a.dtype), kind="ExternalInput").ap()
         for n, a in arrays.items()}
    out = nc.dram_tensor("out_0_dram", (NB, P, DM), F32, kind="ExternalOutput").ap()
    build(nc, table, d["pack"], d["x_in"], d["ctxT_in"], (d["mask_text"], d["mask_keys"]), out)
    r = run_bass_kernel_spmd(nc, [arrays], core_ids=[0])
    return r.results[0]["out_0_dram"]
```
